# Optimizing a Trainium2 kernel written in Bass

```python
import numpy as np
import jax
import jax.numpy as jnp

def _softmax(x, axis=-1):
    return jax.nn.softmax(x, axis=axis)

def _gelu(x):
    return jax.nn.gelu(x, approximate=True)

def _silu(x):
    return jax.nn.silu(x)

def _sigmoid(x):
    return jax.nn.sigmoid(x)

def _layernorm(x, axis=-1, eps=1e-05):
    m = jnp.mean(x, axis=axis, keepdims=True)
    v = jnp.var(x, axis=axis, keepdims=True)
    return (x - m) / jnp.sqrt(v + eps)

def _scatter_add(tgt, idx, src, axis=0):
    return tgt.at[idx].add(src)

def _segment_sum(src, seg, n):
    return jax.ops.segment_sum(src, seg, n)
kernel_name = 'mk_macaron_d1_jaxref_r4_b91ba2'

def setup_inputs(seed: int=0):
    np.random.seed(seed)
    _w = jnp.asarray

    def _L0_attn_setup():
        import jax, jax.numpy as jnp
        import numpy as np
        D_MODEL = 256
        EXPAND = 2
        D_INNER = EXPAND * D_MODEL
        D_STATE = 64
        D_CONV = 4
        HEADDIM = 64
        NHEADS = D_INNER // HEADDIM
        NGROUPS = 1
        D_CONV_CH = D_INNER + 2 * NGROUPS * D_STATE
        D_IN_PROJ = 2 * D_INNER + 2 * NGROUPS * D_STATE + NHEADS
        EPS = 1e-05

        def _mamba2_fwd(x, W_in, conv_w, conv_b, dt_bias, A_log, D, norm_weight, W_out):
            Bsz, L, _ = x.shape
            zxbcdt = x @ W_in
            z = zxbcdt[..., :D_INNER]
            xBC = zxbcdt[..., D_INNER:D_INNER + D_CONV_CH]
            dt = zxbcdt[..., D_INNER + D_CONV_CH:]
            dt = jax.nn.softplus(dt + dt_bias)
            lhs = jnp.transpose(xBC, (0, 2, 1))
            rhs = conv_w[:, None, :]
            conv = jax.lax.conv_general_dilated(lhs, rhs, window_strides=(1,), padding=[(D_CONV - 1, 0)], feature_group_count=D_CONV_CH, dimension_numbers=('NCH', 'OIH', 'NCH'))
            xBC = jax.nn.silu(jnp.transpose(conv, (0, 2, 1)) + conv_b)
            x_ssm = xBC[..., :D_INNER].reshape(Bsz, L, NHEADS, HEADDIM)
            Bmat = xBC[..., D_INNER:D_INNER + D_STATE]
            Cmat = xBC[..., D_INNER + D_STATE:]
            A = -jnp.exp(A_log)
            dA = jnp.exp(dt * A)
            dBx = dt[..., None, None] * x_ssm[..., None] * Bmat[:, :, None, None, :]

            def step(s, inp):
                dA_t, dBx_t, C_t = inp
                s = s * dA_t[..., None, None] + dBx_t
                y = jnp.einsum('bhpn,bn->bhp', s, C_t)
                return (s, y)
            s0 = jnp.zeros((Bsz, NHEADS, HEADDIM, D_STATE), dtype=x.dtype)
            _, ys = jax.lax.scan(step, s0, (jnp.moveaxis(dA, 1, 0), jnp.moveaxis(dBx, 1, 0), jnp.moveaxis(Cmat, 1, 0)))
            y = jnp.moveaxis(ys, 0, 1)
            y = y + D[None, None, :, None] * x_ssm
            y = y.reshape(Bsz, L, D_INNER)
            y = y * jax.nn.silu(z)
            y = y * jax.lax.rsqrt(jnp.mean(y * y, axis=-1, keepdims=True) + EPS) * norm_weight
            return y @ W_out
        key = jax.random.key(seed)
        ks = jax.random.split(key, 8)
        B, L = (2, 1024)
        x = jax.random.normal(ks[0], (B, L, D_MODEL), dtype=jnp.float32)
        W_in = jax.random.normal(ks[1], (D_MODEL, D_IN_PROJ), dtype=jnp.float32) * 0.02
        conv_w = jax.random.normal(ks[2], (D_CONV_CH, D_CONV), dtype=jnp.float32) * 0.2
        conv_b = jnp.zeros((D_CONV_CH,), dtype=jnp.float32)
        dt = jnp.exp(jax.random.uniform(ks[3], (NHEADS,)) * (np.log(0.1) - np.log(0.001)) + np.log(0.001))
        dt_bias = (dt + jnp.log(-jnp.expm1(-dt))).astype(jnp.float32)
        A_log = jnp.log(jax.random.uniform(ks[4], (NHEADS,), minval=1.0, maxval=16.0)).astype(jnp.float32)
        D = jnp.ones((NHEADS,), dtype=jnp.float32)
        norm_weight = jnp.ones((D_INNER,), dtype=jnp.float32)
        W_out = jax.random.normal(ks[5], (D_INNER, D_MODEL), dtype=jnp.float32) * 0.02
        return {'x': x, 'W_in': W_in, 'conv_w': conv_w, 'conv_b': conv_b, 'dt_bias': dt_bias, 'A_log': A_log, 'D': D, 'norm_weight': norm_weight, 'W_out': W_out}
    _L0_attn_in = _L0_attn_setup()

    def _L0_ffn_setup():
        import jax, jax.numpy as jnp
        import numpy as np
        B, T, D, E, H, K = (4, 512, 256, 8, 512, 2)
        key = jax.random.key(seed)
        k0, k1, k2, k3 = jax.random.split(key, 4)
        x = jax.random.normal(k0, (B, T, D), dtype=jnp.float32)
        router_w = jax.random.normal(k1, (E, D), dtype=jnp.float32) * D ** (-0.5)
        w1 = jax.random.normal(k2, (E, D, H), dtype=jnp.float32) * D ** (-0.5)
        w2 = jax.random.normal(k3, (E, H, D), dtype=jnp.float32) * H ** (-0.5)
        return {'x': x, 'router_w': router_w, 'w1': w1, 'w2': w2}
    _L0_ffn_in = _L0_ffn_setup()
    _d = {'L0_attn_x': _L0_attn_in['x'], 'L0_attn_W_in': _L0_attn_in['W_in'], 'L0_attn_conv_w': _L0_attn_in['conv_w'], 'L0_attn_conv_b': _L0_attn_in['conv_b'], 'L0_attn_dt_bias': _L0_attn_in['dt_bias'], 'L0_attn_A_log': _L0_attn_in['A_log'], 'L0_attn_D': _L0_attn_in['D'], 'L0_attn_norm_weight': _L0_attn_in['norm_weight'], 'L0_attn_W_out': _L0_attn_in['W_out'], 'L0_ffn_router_w': _L0_ffn_in['router_w'], 'L0_ffn_w1': _L0_ffn_in['w1'], 'L0_ffn_w2': _L0_ffn_in['w2']}
    _x0 = _d['L0_attn_x']
    _d['L0_attn_x'] = jax.random.normal(jax.random.fold_in(jax.random.key(seed), 1), (2, 2048, 256), dtype=_x0.dtype)
    del _x0
    return _d

def reference(L0_attn_x, L0_attn_W_in, L0_attn_conv_w, L0_attn_conv_b, L0_attn_dt_bias, L0_attn_A_log, L0_attn_D, L0_attn_norm_weight, L0_attn_W_out, L0_ffn_router_w, L0_ffn_w1, L0_ffn_w2):

    def _L0_attn_ref(x, W_in, conv_w, conv_b, dt_bias, A_log, D, norm_weight, W_out):
        import jax, jax.numpy as jnp
        import numpy as np
        D_MODEL = 256
        EXPAND = 2
        D_INNER = EXPAND * D_MODEL
        D_STATE = 64
        D_CONV = 4
        HEADDIM = 64
        NHEADS = D_INNER // HEADDIM
        NGROUPS = 1
        D_CONV_CH = D_INNER + 2 * NGROUPS * D_STATE
        D_IN_PROJ = 2 * D_INNER + 2 * NGROUPS * D_STATE + NHEADS
        EPS = 1e-05

        def _mamba2_fwd(x, W_in, conv_w, conv_b, dt_bias, A_log, D, norm_weight, W_out):
            Bsz, L, _ = x.shape
            zxbcdt = x @ W_in
            z = zxbcdt[..., :D_INNER]
            xBC = zxbcdt[..., D_INNER:D_INNER + D_CONV_CH]
            dt = zxbcdt[..., D_INNER + D_CONV_CH:]
            dt = jax.nn.softplus(dt + dt_bias)
            lhs = jnp.transpose(xBC, (0, 2, 1))
            rhs = conv_w[:, None, :]
            conv = jax.lax.conv_general_dilated(lhs, rhs, window_strides=(1,), padding=[(D_CONV - 1, 0)], feature_group_count=D_CONV_CH, dimension_numbers=('NCH', 'OIH', 'NCH'))
            xBC = jax.nn.silu(jnp.transpose(conv, (0, 2, 1)) + conv_b)
            x_ssm = xBC[..., :D_INNER].reshape(Bsz, L, NHEADS, HEADDIM)
            Bmat = xBC[..., D_INNER:D_INNER + D_STATE]
            Cmat = xBC[..., D_INNER + D_STATE:]
            A = -jnp.exp(A_log)
            dA = jnp.exp(dt * A)
            dBx = dt[..., None, None] * x_ssm[..., None] * Bmat[:, :, None, None, :]

            def step(s, inp):
                dA_t, dBx_t, C_t = inp
                s = s * dA_t[..., None, None] + dBx_t
                y = jnp.einsum('bhpn,bn->bhp', s, C_t)
                return (s, y)
            s0 = jnp.zeros((Bsz, NHEADS, HEADDIM, D_STATE), dtype=x.dtype)
            _, ys = jax.lax.scan(step, s0, (jnp.moveaxis(dA, 1, 0), jnp.moveaxis(dBx, 1, 0), jnp.moveaxis(Cmat, 1, 0)))
            y = jnp.moveaxis(ys, 0, 1)
            y = y + D[None, None, :, None] * x_ssm
            y = y.reshape(Bsz, L, D_INNER)
            y = y * jax.nn.silu(z)
            y = y * jax.lax.rsqrt(jnp.mean(y * y, axis=-1, keepdims=True) + EPS) * norm_weight
            return y @ W_out
        return _mamba2_fwd(x, W_in, conv_w, conv_b, dt_bias, A_log, D, norm_weight, W_out)

    def _L0_ffn_ref(x, router_w, w1, w2):
        import jax, jax.numpy as jnp
        import numpy as np
        B, T, D, E, H, K = (4, 512, 256, 8, 512, 2)
        Bb, Tt, Dd = x.shape
        N = Bb * Tt
        logits = jnp.einsum('btd,ed->bte', x, router_w)
        top_vals, top_idx = jax.lax.top_k(logits, K)
        top_w = jax.nn.softmax(top_vals, axis=-1)
        xf = x.reshape(N, Dd)
        h = jnp.einsum('nd,edh->enh', xf, w1)
        h = jnp.square(jax.nn.relu(h))
        y = jnp.einsum('enh,ehd->end', h, w2)
        idx_f = top_idx.reshape(N, K)
        w_f = top_w.reshape(N, K)
        y_sel = y[idx_f, jnp.arange(N)[:, None]]
        out = jnp.einsum('nk,nkd->nd', w_f, y_sel)
        return out.reshape(Bb, Tt, Dd)
    x = L0_attn_x
    x = x + 0.5 * _L0_ffn_ref(_layernorm(x, axis=-1), L0_ffn_router_w, L0_ffn_w1, L0_ffn_w2)
    x = x + _L0_attn_ref(_layernorm(x, axis=-1), L0_attn_W_in, L0_attn_conv_w, L0_attn_conv_b, L0_attn_dt_bias, L0_attn_A_log, L0_attn_D, L0_attn_norm_weight, L0_attn_W_out)
    x = x + 0.5 * _L0_ffn_ref(_layernorm(x, axis=-1), L0_ffn_router_w, L0_ffn_w1, L0_ffn_w2)
    return x

_drawn_inputs = setup_inputs


def setup_inputs(seed=0):
    import zlib

    import numpy as np

    out = dict(_drawn_inputs(seed))
    spreads = {'L0_attn_conv_b': (0.0, 0.1), 'L0_attn_D': (1.0, 0.2), 'L0_attn_norm_weight': (1.0, 0.2)}
    factors = {}
    for name, (base, spread) in spreads.items():
        noise = np.random.default_rng([zlib.crc32(name.encode()), seed]).standard_normal(out[name].shape)
        drawn = base * np.exp(spread * noise) if base else spread * noise
        out[name] = jnp.asarray(drawn.astype(out[name].dtype))
    for name, factor in factors.items():
        out[name] = (out[name] * factor).astype(out[name].dtype)
    return out
```

```python
from contextlib import ExitStack

import concourse.bass as bass
from concourse import mybir

F32 = mybir.dt.float32
F32R = mybir.dt.float32r
BF16 = mybir.dt.bfloat16
I32 = mybir.dt.int32
U32 = mybir.dt.uint32
ALU = mybir.AluOpType
ACT = mybir.ActivationFunctionType
AX = mybir.AxisListType

P = 128
D = 256
KD = D // P
E = 8
HID = 512
KH = HID // P
TOP = 2
EPS = 1e-5
BIG = 3.0e38
WCOLS = KD * HID

CREDIT = 2


class Step:

    def __init__(self, sem, unit=1, credit=CREDIT):
        self.sem, self.unit, self.credit = sem, unit, credit

    def open(self, eng):
        eng.sem_inc(self.sem, self.credit * self.unit)

    def done(self, item):
        return (item + (1 + self.credit)) * self.unit


class Gathers:

    def __init__(self, nc, ctx):
        self.sems = [ctx.enter_context(nc.semaphore(f"gather{u}")) for u in range(2)]
        self.before = 0

    def take(self, n):
        steps = [Step(s, 16, self.before) for s in self.sems]
        self.before += n
        return steps


class Chain:

    def __init__(self, eng, sem):
        self.eng, self.sem, self.n = eng, sem, 0

    def link(self, ins):
        self.n += 1
        ins.then_inc(self.sem, 1)
        self.eng.wait_ge(self.sem, self.n)


class Sems:

    def __init__(self, nc, ctx):
        self.nc, self.ctx, self.all = nc, ctx, []

    def __call__(self, name):
        self.all.append(self.ctx.enter_context(self.nc.semaphore(name)))
        return self.all[-1]

    def clear(self):
        with self.nc.Block() as block:
            @block.sync
            def _(sp):
                for s in self.all:
                    sp.sem_clear(s)


def make_constants(nc, ctx):
    def sb(name, shape, dt):
        return ctx.enter_context(nc.sbuf_tensor(name, shape, dt))
    return {
        "ident": sb("ident", [P, P], F32),
        "incl_tri": sb("incl_tri", [P, P], F32),
        "strict_tri": sb("strict_tri", [P, P], BF16),
        "ones_bf": sb("ones_bf", [P, P], BF16),
        "ones_f": sb("ones_f", [P, P], F32),
        "part": sb("part", [P, 1], F32),
        "neghalf": sb("neghalf", [P, 8], F32),
    }


def build_constants(nc, c):
    with ExitStack() as ctx:
        sems = Sems(nc, ctx)
        s_set = sems("s_const")
        ctx.callback(sems.clear)
        block = ctx.enter_context(nc.Block())

        @block.gpsimd
        def _(pool):
            chain = Chain(pool, s_set)
            pool.memset(c["ident"][:, :], 0.0)
            pool.memset(c["incl_tri"][:, :], 1.0)
            pool.memset(c["strict_tri"][:, :], 1.0)
            pool.memset(c["ones_bf"][:, :], 1.0)
            pool.memset(c["ones_f"][:, :], 1.0)
            pool.memset(c["neghalf"][:, :], -0.5)
            chain.link(pool.iota(c["part"][:, :], pattern=[[0, 1]], base=0, channel_multiplier=1,
                                 allow_small_or_imprecise_dtypes=True))
            for name, op, fill, sign in (("ident", ALU.not_equal, 1.0, -1), ("incl_tri", ALU.is_ge, 0.0, 1),
                                         ("strict_tri", ALU.is_gt, 0.0, 1)):
                chain.link(pool.affine_select(out=c[name][:, :], in_=c[name][:, :], compare_op=op, fill=fill,
                                              base=0, pattern=[[sign, P]], channel_multiplier=-sign))


def ffn_block(nc, c, keep, x, router_w, w1, w2, xn_d, ys_d, lo_d, out, first):
    TOK = x.shape[0]
    T = TOK // P
    NT = (TOP * TOK + E * (P - 1)) // P
    NT += NT % 2
    C = TOP * T
    with ExitStack() as ctx:
        def sb(name, shape, dt):
            return ctx.enter_context(nc.sbuf_tensor(name, shape, dt))

        def psum(name, dt=F32, n=512):
            return ctx.enter_context(nc.psum_tensor(name, [P, n], dt))

        sem = Sems(nc, ctx)

        def step(name, unit=1):
            return Step(sem(name), unit)


        tag = "1" if first else "2"
        ident = c["ident"]
        w1h, w2h, slots, gates = keep["w1h"], keep["w2h"], keep["slots"], keep["gates"]
        w1l = sb("w1l" + tag, [P, E * WCOLS], F32R)
        w2l = sb("w2l" + tag, [P, E * WCOLS], F32R)
        wst = sb("wst" + tag, [P, 2, WCOLS], F32)
        xa = sb("xa" + tag, [P, 2, D], F32)
        xn = sb("xn" + tag, [P, 2, D], F32)
        st = sb("st" + tag, [P, 2, 6], F32)
        mv = sb("mv" + tag, [P, 2, 2], F32)
        ve = sb("ve" + tag, [P, 2], F32)
        rstd = sb("rstd" + tag, [P, 2], F32)
        xT = sb("xT" + tag, [P, 2, KD, P], F32)
        rw = sb("rw" + tag, [E, D], F32)
        rwT = sb("rwT" + tag, [P, KD, E], F32)
        logits = sb("logits" + tag, [P, T, E], F32)
        iota_e = sb("iota_e" + tag, [P, T, E], F32)
        iota_col = sb("iota_col" + tag, [P, P], F32)
        iota_bf = sb("iota_bf" + tag, [P, P], BF16)
        iota_j = sb("iota_j" + tag, [P, NT, E], F32)
        tnum = sb("tnum" + tag, [P, C], F32)
        work = [sb(f"work{n}_{tag}", [P, T, E], F32) for n in range(6)]
        oh = [sb(f"oh{n}_{tag}", [P, T, E], F32) for n in range(TOP)]
        top = sb("top" + tag, [P, 6, T], F32)
        both = sb("both" + tag, [P, T * E], BF16)
        small = sb("small" + tag, [P, 8, E], F32)
        smalli = sb("smalli" + tag, [P, 2, E], I32)
        slotf = sb("slotf" + tag, [P, C], F32)
        parts_i = sb("parts_i" + tag, [P, 2, C], U32)
        parts_f = sb("parts_f" + tag, [P, 2, C], F32)
        expert_f = sb("expert_f" + tag, [P, NT], F32)
        expert_i = sb("expert_i" + tag, [P, NT], I32)
        ohhi = sb("ohhi" + tag, [P, 2, NT], BF16)
        ohlo = sb("ohlo" + tag, [P, 2, 2, P], BF16)
        inv = sb("inv" + tag, [P, P], F32)
        inv2 = sb("inv2" + tag, [P, P], F32)
        token_of = sb("token_of" + tag, [P, NT], U32)
        idx = sb("idx" + tag, [P, 2, TOP], U32)
        xg = sb("xg" + tag, [P, 2, D], F32)
        xh = sb("xh" + tag, [P, 2, KD, P], F32R)
        xl = sb("xl" + tag, [P, 2, KD, P], F32R)
        r = sb("r" + tag, [P, 2, HID], F32)
        h2 = sb("h2" + tag, [P, 2, KH, P], F32)
        h2h = sb("h2h" + tag, [P, 2, KH, P], F32R)
        h2l = sb("h2l" + tag, [P, 2, KH, P], F32R)
        y = sb("y" + tag, [P, 2, D], F32)
        yg = sb("yg" + tag, [P, 2, TOP, D], F32) if out is not None else None

        pT = [psum(f"pT{u}{tag}") for u in range(2)]
        pH = [psum(f"pH{u}{tag}") for u in range(2)]
        pR = [psum(f"pR{u}{tag}") for u in range(2)]
        pY = [psum(f"pY{u}{tag}") for u in range(2)]

        w_loaded = [sem(f"w_loaded{u}") for u in range(2)]
        w_hi, w_lo = step("w_hi"), step("w_lo")
        w_spilt, rw_loaded = sem("w_spilt"), sem("rw_loaded")
        xa_loaded = [step(f"xa_loaded{u}", 16) for u in range(2)]
        var_done, pow_done, norm_done = step("var_done"), step("pow_done"), step("norm_done")
        st_chain, aggr_go = step("st_chain"), sem("aggr_go")
        xn_stored = [step(f"xn_stored{u}", 16) for u in range(2)]
        xT_ready, xT_copied, logit_ready, logit_copied = (step(n) for n in ("xT_ready", "xT_copied", "logit_ready", "logit_copied"))
        iotas, b_chain, exp_in, exp_out, counts_in, counts_out = (sem(n) for n in ("iotas", "b_chain", "exp_in", "exp_out", "counts_in", "counts_out"))
        rwT_ready = sem("rwT_ready")
        oh_built, oh_used = step("oh_built"), step("oh_used")
        inv_ready, invT_ready, routed = sem("inv_ready"), sem("invT_ready"), sem("routed")
        idx_set, gather_go, gathered = step("idx_set"), sem("gather_go"), keep["gathers"].take(NT // 2)
        g_T, g_hi, g_split, h_ready, relu_done, rT_ready, sq_done, h2_hi, h2_split, y_ready, y_copied = (
            step(n) for n in ("g_T", "g_hi", "g_split", "h_ready", "relu_done", "rT_ready", "sq_done", "h2_hi", "h2_split", "y_ready", "y_copied"))
        y_stored = [step(f"y_stored{u}", 16) for u in range(2)]
        e_loaded, e_stored = ([step(f"e_{n}{u}", 16) for u in range(2)] for n in ("loaded", "stored"))
        e_gath = keep["gathers"].take(TOP * T // 2) if out is not None else None
        e_idx, e_first, e_done = step("e_idx"), step("e_first"), step("e_done")

        def wsrc(n):
            return (w1 if n % 2 == 0 else w2)[n // 2].rearrange("(k p) n -> p k n", p=P)

        def whi(n):
            return (w1h if n % 2 == 0 else w2h)[:, (n // 2) * WCOLS:(n // 2 + 1) * WCOLS]

        def wlo(n):
            return (w1l if n % 2 == 0 else w2l)[:, (n // 2) * WCOLS:(n // 2 + 1) * WCOLS]

        NW = 2 * E
        ctx.callback(sem.clear)
        block = ctx.enter_context(nc.Block())

        @block.sync
        def _(sp):
            sp.dma_start(rw[:, :], router_w).then_inc(rw_loaded, 16)
            if not first:
                sp.dma_start(w1l[:, :].bitcast(F32), lo_d[0]).then_inc(w_loaded[0], 16)
                sp.dma_start(w2l[:, :].bitcast(F32), lo_d[1]).then_inc(w_loaded[1], 16)
            for s in (*xa_loaded, *xn_stored, *y_stored):
                s.open(sp)
            with sp.Fori(0, T // 2) as j:
                for u in range(2):
                    sp.wait_ge(norm_done.sem, norm_done.done(2 * j + (u - 2)))
                    sp.dma_start(xa[:, u, :], x[bass.ds((2 * j + u) * P, P), :]).then_inc(xa_loaded[u].sem, 16)
                for u in range(2):
                    sp.wait_ge(norm_done.sem, norm_done.done(2 * j + u))
                    sp.dma_start(xn_d[bass.ds((2 * j + u) * P, P), :], xn[:, u, :]).then_inc(xn_stored[u].sem, 16)
            if first:
                sp.wait_ge(w_lo.sem, w_lo.done(NW - 1))
                sp.dma_start(lo_d[0], w1l[:, :].bitcast(F32)).then_inc(w_spilt, 16)
                sp.dma_start(lo_d[1], w2l[:, :].bitcast(F32)).then_inc(w_spilt, 16)
            with sp.Fori(0, NT // 2) as j:
                for u in range(2):
                    sp.wait_ge(y_copied.sem, y_copied.done(2 * j + u))
                    sp.dma_start(ys_d[bass.ds((2 * j + u) * P, P), :], y[:, u, :]).then_inc(y_stored[u].sem, 16)
            for u in range(2):
                sp.wait_ge(y_stored[u].sem, y_stored[u].done(NT // 2 - 1))
            if first:
                sp.wait_ge(w_spilt, 32)
            if out is not None:
                for s in (*e_loaded, *e_stored):
                    s.open(sp)
                with sp.Fori(0, T // 2) as j:
                    for u in range(2):
                        sp.wait_ge(e_stored[u].sem, e_stored[u].done(j - 1))
                        sp.dma_start(xa[:, u, :], x[bass.ds((2 * j + u) * P, P), :]).then_inc(e_loaded[u].sem, 16)
                    for u in range(2):
                        sp.wait_ge(e_done.sem, e_done.done(2 * j + u))
                        sp.dma_start(out[bass.ds((2 * j + u) * P, P), :], xa[:, u, :]).then_inc(e_stored[u].sem, 16)
                for u in range(2):
                    sp.wait_ge(e_stored[u].sem, e_stored[u].done(T // 2 - 1))

        @block.gpsimd
        def _(pool):
            pool.iota(iota_e[:, :, :], pattern=[[0, T], [1, E]], base=0, channel_multiplier=0,
                      allow_small_or_imprecise_dtypes=True)
            pool.iota(iota_col[:, :], pattern=[[1, P]], base=0, channel_multiplier=0,
                      allow_small_or_imprecise_dtypes=True).then_inc(iotas, 1)
            pool.iota(iota_j[:, :, :], pattern=[[1, NT], [0, E]], base=0, channel_multiplier=0,
                      allow_small_or_imprecise_dtypes=True)
            pool.iota(tnum[:, :], pattern=[[0, TOP], [1, T]], base=0, channel_multiplier=0,
                      allow_small_or_imprecise_dtypes=True).then_inc(iotas, 1)
            pow_done.open(pool)
            w_lo.open(pool)

            def lo_weights(n):
                pool.wait_ge(w_hi.sem, w_hi.done(n))
                pool.tensor_tensor(wlo(n), wst[:, n % 2, :], whi(n).bitcast(F32), ALU.subtract).then_inc(w_lo.sem, 1)

            def pows(j):
                for u in range(2):
                    pool.wait_ge(var_done.sem, var_done.done(2 * j + u))
                    pool.tensor_tensor(rstd[:, u:u + 1], ve[:, u:u + 1], c["neghalf"][:, 0:1], ALU.pow).then_inc(pow_done.sem, 1)

            if first:
                for n in range(NW):
                    pows(n)
                    lo_weights(n)
                for j in range(NW, T // 2):
                    pows(j)
            else:
                with pool.Fori(0, T // 2) as j:
                    pows(j)
            pool.wait_ge(routed, 1)
            for u in range(2):
                pool.wait_ge(xn_stored[u].sem, xn_stored[u].done(T // 2 - 1))
            idx_set.open(pool)
            with pool.Fori(0, NT // 2) as j:
                for u in range(2):
                    t = 2 * j + u
                    pool.wait_ge(g_T.sem, g_T.done(t - 2))
                    pool.tensor_copy(idx[:, u, 0:1], token_of[:, bass.ds(t, 1)]).then_inc(idx_set.sem, 1)
                    pool.wait_ge(idx_set.sem, idx_set.done(t))
                    pool.sem_inc(gather_go, 1)
                    pool.indirect_dma_start(out=xg[:, u, :], out_offset=None, in_=xn_d,
                                            in_offset=bass.IndirectOffsetOnAxis(ap=idx[:, u, 0:1], axis=0)).then_inc(gathered[u].sem, 16)
            if out is not None:
                for u in range(2):
                    pool.wait_ge(y_stored[u].sem, y_stored[u].done(NT // 2 - 1))
                e_idx.open(pool)
                with pool.Fori(0, T // 2) as j:
                    for u in range(2):
                        i = 2 * j + u
                        pool.wait_ge(e_done.sem, e_done.done(i - 2))
                        pool.tensor_copy(idx[:, u, 0:1], slots[:, bass.ds(i, 1)])
                        pool.tensor_copy(idx[:, u, 1:2], slots[:, bass.ds(T + i, 1)]).then_inc(e_idx.sem, 1)
                        pool.wait_ge(e_idx.sem, e_idx.done(i))
                        pool.sem_inc(gather_go, 1)
                        for k in range(TOP):
                            pool.indirect_dma_start(out=yg[:, u, k, :], out_offset=None, in_=ys_d,
                                                    in_offset=bass.IndirectOffsetOnAxis(ap=idx[:, u, k:k + 1], axis=0)).then_inc(e_gath[u].sem, 16)

        @block.scalar
        def _(act):
            for s in (w_hi, xT_copied, logit_copied, relu_done, sq_done):
                s.open(act)

            def hi_weights(n):
                act.wait_ge(w_loaded[n % 2], 16 * (n // 2 + 1))
                act.activation(whi(n), wst[:, n % 2, :], ACT.Copy).then_inc(w_hi.sem, 1)

            def load_weights(n):
                if n >= 2:
                    act.wait_ge(w_lo.sem, w_lo.done(n - 2))
                act.dma_start(wst[:, n % 2, :].rearrange("p (k n) -> p k n", k=KD if n % 2 == 0 else KH), wsrc(n)).then_inc(w_loaded[n % 2], 16)

            def stage_a(j):
                for u in range(2):
                    i = 2 * j + u
                    act.wait_ge(xT_ready.sem, xT_ready.done(i))
                    act.wait_ge(logit_ready.sem, logit_ready.done(i - 2))
                    act.activation(xT[:, u, :, :], pT[u][:, 0:D].rearrange("p (k q) -> p k q", k=KD), ACT.Copy).then_inc(xT_copied.sem, 1)
                for u in range(2):
                    i = 2 * j + u
                    act.wait_ge(logit_ready.sem, logit_ready.done(i))
                    dst = logits[:, i, :] if isinstance(i, int) else logits[:, bass.ds(i, 1), :].rearrange("p a e -> p (a e)")
                    act.activation(dst, pY[u][:, 0:E], ACT.Copy).then_inc(logit_copied.sem, 1)

            if first:
                load_weights(0)
                for n in range(NW):
                    if n + 1 < NW:
                        load_weights(n + 1)
                    hi_weights(n)
                    stage_a(n)
                for j in range(NW, T // 2):
                    stage_a(j)
            else:
                with act.Fori(0, T // 2) as j:
                    stage_a(j)
            act.wait_ge(exp_in, 1)
            act.activation(top[:, 3, :], top[:, 2, :], ACT.Exp).then_inc(exp_out, 1)

            def relu(t, u):
                act.wait_ge(h_ready.sem, h_ready.done(t))
                act.wait_ge(rT_ready.sem, rT_ready.done(t - 2))
                act.activation(r[:, u, :], pH[u][:, :], ACT.Relu).then_inc(relu_done.sem, 1)

            def square(t, u):
                act.wait_ge(rT_ready.sem, rT_ready.done(t))
                act.wait_ge(h2_split.sem, h2_split.done(t - 2))
                act.activation(h2[:, u, :, :], pR[u][:, :].rearrange("p (k q) -> p k q", k=KH), ACT.Square).then_inc(sq_done.sem, 1)

            relu(0, 0)
            with act.Fori(0, NT // 2 - 1) as j:
                for u in range(2):
                    relu(2 * j + (u + 1), 1 - u)
                    square(2 * j + u, u)
            relu(NT - 1, 1)
            square(NT - 2, 0)
            square(NT - 1, 1)

        @block.tensor
        def _(pe):
            for s in (xT_ready, logit_ready, oh_used, g_T, h_ready, rT_ready, y_ready):
                s.open(pe)
            pe.wait_ge(rw_loaded, 16)
            for k in range(KD):
                last = pe.transpose(pR[0][:, k * E:(k + 1) * E], rw[:, k * P:(k + 1) * P], ident[0:E, 0:E])
            last.then_inc(rwT_ready, 1)
            pe.wait_ge(rwT_ready, 2)
            with pe.Fori(0, T // 2) as j:
                for u in range(2):
                    i = 2 * j + u
                    pe.wait_ge(norm_done.sem, norm_done.done(i))
                    pe.wait_ge(xT_copied.sem, xT_copied.done(i - 2))
                    for k in range(KD):
                        last = pe.transpose(pT[u][:, k * P:(k + 1) * P], xn[:, u, k * P:(k + 1) * P], ident[:, :])
                    last.then_inc(xT_ready.sem, 1)
                for u in range(2):
                    i = 2 * j + u
                    pe.wait_ge(xT_copied.sem, xT_copied.done(i))
                    pe.wait_ge(logit_copied.sem, logit_copied.done(i - 2))
                    for k in range(KD):
                        last = pe.matmul(pY[u][:, 0:E], xT[:, u, k, :], rwT[:, k, :], start=(k == 0), stop=(k == KD - 1))
                    last.then_inc(logit_ready.sem, 1)
            pe.wait_ge(counts_in, 1)
            pe.matmul(pR[0][:, 0:T * E], c["strict_tri"][:, :], both[:, :], start=True, stop=True)
            pe.matmul(pR[1][:, 0:T * E], c["ones_bf"][:, :], both[:, :], start=True, stop=True).then_inc(counts_out, 1)

            def invert(cc, u, start, stop):
                pe.wait_ge(oh_built.sem, oh_built.done(cc))
                pe.matmul(pT[0][0:NT, 0:2 * P], ohhi[:, u, :], ohlo[:, u, :, :].rearrange("p a q -> p (a q)"),
                          start=start, stop=stop).then_inc(oh_used.sem, 1)

            invert(0, 0, True, False)
            invert(1, 1, False, False)
            with pe.Fori(1, C // 2 - 1) as j:
                for u in range(2):
                    invert(2 * j + u, u, False, False)
            invert(C - 2, 0, False, False)
            invert(C - 1, 1, False, True)
            pe.wait_ge(inv_ready, 1)
            pe.transpose(pT[1][:, 0:NT], inv[0:NT, :], ident[0:NT, 0:NT]).then_inc(invT_ready, 1)

            def expert_columns(t):
                return pe.value_load(expert_i[0:1, t:t + 1] if isinstance(t, int) else expert_i[0:1, bass.ds(t, 1)],
                                     min_val=0, max_val=(E - 1) * WCOLS)

            def turn_x(t, u):
                pe.wait_ge(gathered[u].sem, gathered[u].done(half(t, u)))
                pe.wait_ge(g_split.sem, g_split.done(t - 2))
                for k in range(KD):
                    last = pe.transpose(pT[u][:, k * P:(k + 1) * P], xg[:, u, k * P:(k + 1) * P], ident[:, :])
                last.then_inc(g_T.sem, 1)

            def up(t, u):
                at = expert_columns(t)
                pe.wait_ge(g_split.sem, g_split.done(t))
                pe.wait_ge(relu_done.sem, relu_done.done(t - 2))
                n = 0
                for a, w in ((xh, w1h), (xh, w1l), (xl, w1h)):
                    for k in range(KD):
                        last = pe.matmul(pH[u][:, :], a[:, u, k, :], w[:, bass.ds(at + k * HID, HID)],
                                         start=(n == 0), stop=(n == 3 * KD - 1))
                        n += 1
                last.then_inc(h_ready.sem, 1)

            def turn_h(t, u):
                pe.wait_ge(relu_done.sem, relu_done.done(t))
                pe.wait_ge(sq_done.sem, sq_done.done(t - 2))
                for k in range(KH):
                    last = pe.transpose(pR[u][:, k * P:(k + 1) * P], r[:, u, k * P:(k + 1) * P], ident[:, :])
                last.then_inc(rT_ready.sem, 1)

            def down(t, u):
                at = expert_columns(t)
                pe.wait_ge(h2_split.sem, h2_split.done(t))
                pe.wait_ge(y_copied.sem, y_copied.done(t - 2))
                n = 0
                for a, w in ((h2h, w2h), (h2h, w2l), (h2l, w2h)):
                    for k in range(KH):
                        last = pe.matmul(pY[u][:, 0:D], a[:, u, k, :], w[:, bass.ds(at + k * D, D)],
                                         start=(n == 0), stop=(n == 3 * KH - 1))
                        n += 1
                last.then_inc(y_ready.sem, 1)

            def half(t, u):
                return (t - u) // 2 if isinstance(t, int) else t

            if not first:
                for s in w_loaded:
                    pe.wait_ge(s, 16)
            turn_x(0, 0)
            turn_x(1, 1)
            up(0, 0)
            turn_x(2, 0)
            up(1, 1)
            turn_h(0, 0)
            with pe.Fori(0, NT // 2 - 2) as j:
                for u in range(2):
                    v = 1 - u
                    pe.wait_ge(gathered[v].sem, gathered[v].done(j + 1 + u))
                    pe.wait_ge(g_split.sem, g_split.done(2 * j + (1 + u)))
                    for k in range(KD):
                        last = pe.transpose(pT[v][:, k * P:(k + 1) * P], xg[:, v, k * P:(k + 1) * P], ident[:, :])
                    last.then_inc(g_T.sem, 1)
                    up(2 * j + (2 + u), u)
                    turn_h(2 * j + (1 + u), v)
                    down(2 * j + u, u)
            t = NT - 3
            turn_x(t + 2, 1)
            up(t + 1, 0)
            turn_h(t, 1)
            down(t - 1, 0)
            up(t + 2, 1)
            turn_h(t + 1, 0)
            down(t, 1)
            turn_h(t + 2, 1)
            down(t + 1, 0)
            down(t + 2, 1)

        @block.vector
        def _(dve):
            for s in (st_chain, var_done, norm_done, oh_built, g_hi, g_split, h2_hi, h2_split, y_copied):
                s.open(dve)
            dve.wait_ge(rwT_ready, 1)
            dve.tensor_copy(rwT[:, :, :], pR[0][:, 0:KD * E].rearrange("p (k e) -> p k e", k=KD)).then_inc(rwT_ready, 1)

            with dve.Fori(0, T // 2) as j:
                for u in range(2):
                    i = 2 * j + u
                    dve.wait_ge(xa_loaded[u].sem, xa_loaded[u].done(j))
                    dve.bn_stats(st[:, u, :], xa[:, u, :]).then_inc(st_chain.sem, 1)
                    dve.wait_ge(st_chain.sem, st_chain.done(4 * j + 2 * u))
                    dve.sem_inc(aggr_go, 1)
                    dve.bn_aggr(mv[:, u, :], st[:, u, :]).then_inc(st_chain.sem, 1)
                    dve.wait_ge(st_chain.sem, st_chain.done(4 * j + (2 * u + 1)))
                    dve.wait_ge(pow_done.sem, pow_done.done(i - 2))
                    dve.tensor_scalar(ve[:, u:u + 1], mv[:, u, 1:2], EPS, None, ALU.add).then_inc(var_done.sem, 1)
                for u in range(2):
                    i = 2 * j + u
                    dve.wait_ge(pow_done.sem, pow_done.done(i))
                    dve.wait_ge(xT_ready.sem, xT_ready.done(i - 2))
                    dve.wait_ge(xn_stored[u].sem, xn_stored[u].done(j - 1))
                    dve.tensor_scalar(xn[:, u, :], xa[:, u, :], mv[:, u, 0:1], rstd[:, u:u + 1],
                                      ALU.subtract, ALU.mult).then_inc(norm_done.sem, 1)

            chain = Chain(dve, b_chain)
            link = chain.link
            dve.wait_ge(iotas, 2)
            dve.wait_ge(logit_copied.sem, logit_copied.done(T - 1))

            def wide(ap):
                return ap.rearrange("p (t a) -> p t a", a=1).to_broadcast([P, T, E])

            def first_largest(scores, best, num, onehot):
                link(dve.tensor_reduce(best, scores, AX.X, ALU.max))
                link(dve.tensor_tensor(work[0][:, :, :], scores, wide(best), ALU.not_equal))
                link(dve.scalar_tensor_tensor(work[1][:, :, :], work[0][:, :, :], float(E), iota_e[:, :, :], ALU.mult, ALU.add))
                link(dve.tensor_reduce(num, work[1][:, :, :], AX.X, ALU.min))
                link(dve.tensor_tensor(onehot, iota_e[:, :, :], wide(num), ALU.is_equal))

            first_largest(logits[:, :, :], top[:, 0, :], top[:, 4, :], oh[0][:, :, :])
            link(dve.tensor_scalar(work[2][:, :, :], oh[0][:, :, :], -2.0, 1.0, ALU.mult, ALU.add))
            link(dve.scalar_tensor_tensor(work[3][:, :, :], work[2][:, :, :], BIG, logits[:, :, :], ALU.mult, ALU.min))
            first_largest(work[3][:, :, :], top[:, 1, :], top[:, 5, :], oh[1][:, :, :])
            link(dve.tensor_tensor(top[:, 2, :], top[:, 1, :], top[:, 0, :], ALU.subtract))
            dve.tensor_tensor(both[:, :].rearrange("p (t e) -> p t e", e=E), oh[0][:, :, :], oh[1][:, :, :], ALU.add).then_inc(counts_in, 1)
            dve.sem_inc(exp_in, 1)
            dve.wait_ge(exp_out, 1)
            link(dve.tensor_scalar(top[:, 4, :], top[:, 3, :], 1.0, None, ALU.add))
            link(dve.reciprocal(top[:, 5, :], top[:, 4, :]))
            link(dve.tensor_scalar(gates[:, 0:T], top[:, 5, :], 0.5, None, ALU.mult))
            link(dve.tensor_tensor(gates[:, T:2 * T], gates[:, 0:T], top[:, 3, :], ALU.mult))
            dve.wait_ge(counts_out, 1)
            per, run, ahead = work[0], work[1], work[2]
            reset = work[3]

            def by_expert(t):
                return t[:, :, :].rearrange("p t e -> p (t e)").rearrange("p (e t) -> p e t", e=E)

            link(dve.tensor_copy(by_expert(per), pR[1][:, 0:T * E].rearrange("p (t e) -> p e t", e=E)))
            link(dve.memset(by_expert(reset), 1.0))
            link(dve.memset(by_expert(reset)[:, :, 0:1], 0.0))
            link(dve.tensor_tensor_scan(run[:, :, :].rearrange("p t e -> p (t e)"), reset[:, :, :].rearrange("p t e -> p (t e)"),
                                        per[:, :, :].rearrange("p t e -> p (t e)"), 0.0, ALU.mult, ALU.add))
            link(dve.tensor_tensor(ahead[:, :, :], run[:, :, :], per[:, :, :], ALU.subtract))
            link(dve.tensor_scalar(smalli[:, 0, :], by_expert(run)[:, :, T - 1:T].rearrange("p e a -> p (e a)"), float(P - 1), None, ALU.add))
            link(dve.tensor_scalar(smalli[:, 1, :], smalli[:, 0, :], P.bit_length() - 1, None, ALU.logical_shift_right))
            link(dve.tensor_copy(small[:, 0, :], smalli[:, 1, :]))
            link(dve.memset(small[:, 1, :], 1.0))
            link(dve.tensor_tensor_scan(small[:, 2, :], small[:, 1, :], small[:, 0, :], 0.0, ALU.mult, ALU.add))
            link(dve.tensor_tensor(small[:, 3, :], small[:, 2, :], small[:, 0, :], ALU.subtract))
            link(dve.tensor_scalar(small[:, 4, :], small[:, 3, :], float(P), None, ALU.mult))
            link(dve.tensor_tensor(by_expert(run), by_expert(ahead),
                                   small[:, 4, :].rearrange("p (e a) -> p e a", a=1).to_broadcast([P, E, T]), ALU.add))
            slot_all = work[4]
            link(dve.tensor_tensor(slot_all[:, :, :], pR[0][:, 0:T * E].rearrange("p (t e) -> p t e", e=E),
                                   by_expert(run).rearrange("p e t -> p t e"), ALU.add))
            for k in range(TOP):
                link(dve.tensor_tensor(work[5][:, :, :], slot_all[:, :, :], oh[k][:, :, :], ALU.mult))
                link(dve.tensor_reduce(slotf[:, k * T:(k + 1) * T], work[5][:, :, :], AX.X, ALU.add))
            link(dve.tensor_copy(slots[:, :], slotf[:, :]))
            link(dve.tensor_scalar(parts_i[:, 0, :], slots[:, :], P - 1, None, ALU.bitwise_and))
            link(dve.tensor_scalar(parts_i[:, 1, :], slots[:, :], P.bit_length() - 1, None, ALU.logical_shift_right))
            link(dve.tensor_copy(parts_f[:, :, :], parts_i[:, :, :]))
            link(dve.tensor_copy(iota_bf[:, :], iota_col[:, :]))
            upto = small[:, 2, :].rearrange("p (a e) -> p a e", a=1).to_broadcast([P, NT, E])
            link(dve.tensor_tensor(iota_j[:, :, :], iota_j[:, :, :], upto, ALU.is_ge))
            link(dve.tensor_reduce(expert_f[:, :], iota_j[:, :, :], AX.X, ALU.add))
            link(dve.tensor_scalar(expert_i[:, :], expert_f[:, :], float(E - 1), float(WCOLS), ALU.min, ALU.mult))
            with dve.Fori(0, C // 2) as j:
                for u in range(2):
                    cc = 2 * j + u
                    dve.wait_ge(oh_used.sem, oh_used.done(cc - 2))
                    lo, hi = parts_f[:, 0, bass.ds(cc, 1)], parts_f[:, 1, bass.ds(cc, 1)]
                    dve.tensor_scalar(ohhi[:, u, :], iota_bf[:, 0:NT], hi, None, ALU.is_equal)
                    dve.tensor_scalar(ohlo[:, u, 0, :], iota_bf[:, :], lo, c["part"][:, 0:1], ALU.is_equal, ALU.mult)
                    dve.tensor_scalar(ohlo[:, u, 1, :], iota_bf[:, :], lo, tnum[:, bass.ds(cc, 1)], ALU.is_equal, ALU.mult).then_inc(oh_built.sem, 1)
            dve.wait_ge(oh_used.sem, oh_used.done(C - 1))
            link(dve.tensor_copy(inv2[0:NT, :], pT[0][0:NT, P:2 * P]))
            dve.scalar_tensor_tensor(inv[0:NT, :], inv2[0:NT, :], float(P), pT[0][0:NT, 0:P], ALU.mult, ALU.add).then_inc(inv_ready, 1)
            dve.wait_ge(invT_ready, 1)
            dve.tensor_copy(token_of[:, :], pT[1][:, 0:NT]).then_inc(routed, 1)

            def split_x(t, u):
                dve.wait_ge(g_T.sem, g_T.done(t))
                dve.wait_ge(h_ready.sem, h_ready.done(t - 2))
                src = pT[u][:, 0:D].rearrange("p (k q) -> p k q", k=KD)
                dve.tensor_copy(xh[:, u, :, :], src).then_inc(g_hi.sem, 1)
                dve.wait_ge(g_hi.sem, g_hi.done(t))
                dve.tensor_tensor(xl[:, u, :, :], src, xh[:, u, :, :].bitcast(F32), ALU.subtract).then_inc(g_split.sem, 1)

            def split_h(t, u):
                dve.wait_ge(sq_done.sem, sq_done.done(t))
                dve.wait_ge(y_ready.sem, y_ready.done(t - 2))
                dve.tensor_copy(h2h[:, u, :, :], h2[:, u, :, :]).then_inc(h2_hi.sem, 1)
                dve.wait_ge(h2_hi.sem, h2_hi.done(t))
                dve.tensor_tensor(h2l[:, u, :, :], h2[:, u, :, :], h2h[:, u, :, :].bitcast(F32), ALU.subtract).then_inc(h2_split.sem, 1)

            def copy_y(t, u, n):
                dve.wait_ge(y_ready.sem, y_ready.done(t))
                dve.wait_ge(y_stored[u].sem, y_stored[u].done(n - 1))
                dve.tensor_copy(y[:, u, :], pY[u][:, 0:D]).then_inc(y_copied.sem, 1)

            split_x(0, 0)
            split_x(1, 1)
            split_x(2, 0)
            split_h(0, 0)
            with dve.Fori(0, NT // 2 - 2) as j:
                for u in range(2):
                    v = 1 - u
                    split_x(2 * j + (3 + u), v)
                    split_h(2 * j + (1 + u), v)
                    copy_y(2 * j + u, u, j)
            split_x(NT - 1, 1)
            split_h(NT - 3, 1)
            copy_y(NT - 4, 0, NT // 2 - 2)
            split_h(NT - 2, 0)
            copy_y(NT - 3, 1, NT // 2 - 2)
            split_h(NT - 1, 1)
            copy_y(NT - 2, 0, NT // 2 - 1)
            copy_y(NT - 1, 1, NT // 2 - 1)

            if out is not None:
                for s in (e_first, e_done):
                    s.open(dve)
                with dve.Fori(0, T // 2) as j:
                    for u in range(2):
                        i = 2 * j + u
                        dve.wait_ge(e_loaded[u].sem, e_loaded[u].done(j))
                        dve.wait_ge(e_gath[u].sem, e_gath[u].done(2 * j + 1))
                        dve.scalar_tensor_tensor(xa[:, u, :], yg[:, u, 0, :], gates[:, bass.ds(i, 1)], xa[:, u, :], ALU.mult, ALU.add).then_inc(e_first.sem, 1)
                        dve.wait_ge(e_first.sem, e_first.done(i))
                        dve.scalar_tensor_tensor(xa[:, u, :], yg[:, u, 1, :], gates[:, bass.ds(T + i, 1)], xa[:, u, :], ALU.mult, ALU.add).then_inc(e_done.sem, 1)


def make_keep(nc, ctx, tokens):
    def sb(name, shape, dt):
        return ctx.enter_context(nc.sbuf_tensor(name, shape, dt))
    return {
        "gathers": Gathers(nc, ctx),
        "w1h": sb("w1h", [P, E * WCOLS], F32R),
        "w2h": sb("w2h", [P, E * WCOLS], F32R),
        "slots": sb("slots", [P, TOP * tokens // P], U32),
        "gates": sb("gates", [P, TOP * tokens // P], F32),
    }

DIN = 512
KI = DIN // P
NS = 64
H = 8
HD = DIN // H
CONV = 4
NB = (DIN + 2 * NS) // P
GC = 4
GT = GC * P
ATANH = [1.0 / n for n in (15, 13, 11, 9, 7, 5, 3)]


def mamba_block(nc, c, keep, x, ys_d, w_in, conv_w, conv_b, dt_bias, a_log, d_skip, norm_w, w_out, x2, batches):
    TOK = x.shape[0]
    T = TOK // P
    NG = TOK // GT
    PER = NG // batches
    CR = 2 * GC
    with ExitStack() as ctx:
        def sb(name, shape, dt=F32):
            return ctx.enter_context(nc.sbuf_tensor(name, shape, dt))

        sem = Sems(nc, ctx)

        def step(name, unit=1):
            return Step(sem(name), unit, CR)

        ident, tri = c["ident"], c["incl_tri"]
        slots, gates = keep["slots"], keep["gates"]
        NIN = w_in.shape[1]
        wih, wil = sb("wih", [P, KD, NIN], F32R), sb("wil", [P, KD, NIN], F32R)
        woh, wol = sb("woh", [P, KI, D], F32R), sb("wol", [P, KI, D], F32R)
        cw, cb, nw = sb("cw", [P, NB, CONV]), sb("cb", [P, NB]), sb("nw", [P, KI])
        cwh, cbh = sb("cwh", [P, NB, CONV]), sb("cbh", [P, NB])
        heads = sb("heads", [P, 3, H])
        negA = sb("negA", [P, GC, H])
        dwide = sb("dwide", [P, DIN])
        flags = sb("flags", [P, NG + 1])
        blk = sb("blk", [P, H, P])
        ident_bf = sb("ident_bf", [P, P], BF16)
        future = sb("future", [P, GC, P], BF16)
        U, V = sb("U", [P, P], F32R), sb("V", [P, H, P], F32R)
        HL = sb("HL", [64, P], F32R)
        xr = sb("xr", [P, 2 * GC, D])
        yg = sb("m_yg", [P, 2, TOP, D])
        idx = sb("m_idx", [P, 2, TOP], U32)
        st, mv, ve, rstd = sb("m_st", [P, 2, 6]), sb("m_mv", [P, 2, 2]), sb("m_ve", [P, 2]), sb("m_rstd", [P, 2])
        xn = sb("m_xn", [P, 2, D])
        xTh, xTl = sb("xTh", [P, KD, GT], F32R), sb("xTl", [P, KD, GT], F32R)
        tz = sb("tz", [P, 2, DIN])
        sz = sb("sz", [P, GC, DIN])
        dts = sb("dts", [P, 14, GC * H])
        raw = sb("raw", [P, NB, CONV - 1 + GT])
        acc = sb("acc", [P, NB, GT])
        tb = sb("tb", [P, 2, GT])
        CT = sb("CT", [NS, GT])
        S, S1 = sb("S", [NS, DIN]), sb("S1", [NS, DIN])
        xt, xdt, xw, xD = (sb(n, [P, DIN]) for n in ("xt", "xdt", "xw", "xD"))
        Bt = sb("Bt", [P, NS])
        ex, M = sb("ex", [P, H, P]), sb("M", [P, H, P])
        t1, t2, t3, yv, sq = (sb(n, [P, DIN]) for n in ("t1", "t2", "t3", "yv", "sq"))
        ss, vr, rs = sb("ss", [P, 1]), sb("vr", [P, 1]), sb("rs", [P, 1])
        yTh, yTl = sb("yTh", [P, KI, P], F32R), sb("yTl", [P, KI, P], F32R)
        xo = sb("xo", [P, 2, D])
        wst = acc[:, :, :].rearrange("p b t -> p (b t)")[:, 0:KD * NIN].rearrange("p (k n) -> p k n", k=KD)
        wost = ex[:, :, :].rearrange("p h t -> p (h t)")[:, 0:KI * D].rearrange("p (k n) -> p k n", k=KI)
        DTR, DPOS, DABS, DU, DS, DS2, DQ, DT, DA, CUM, ECUM, DEC, DECDT, ETOT = range(14)

        bank = [ctx.enter_context(nc.psum_tensor(f"bank{n}", [P, 512], F32)) for n in range(8)]
        pA, pYT = bank[0], bank[0]
        pZ = bank[1]
        pP = [bank[1], bank[2]]
        pO = bank[2]
        pX = bank[3]
        small = bank[4]
        pBt, pCT, pG = small[:, 0:NS], small[0:H, 64:64 + P], small[:, 192:192 + P]
        pDt, pCum, pTot = small[:, 320:320 + H], small[:, 384:384 + GC * H], small[:, 416:416 + GC * H]
        pD = [bank[5], bank[6]]
        pYp, pSt, pI = bank[5], bank[6][0:NS, :], bank[7]

        loads, consts, prep, d_prep, a_prep = (sem(n) for n in ("m_loads", "m_consts", "m_prep", "d_prep", "a_prep"))
        go = sem("m_go")
        x_loaded = [step(f"x_loaded{n}", 16) for n in range(2 * GC)]
        y_gath = keep["gathers"].take(TOP * T // 2)
        i_set, add1, add2, stats, aggr, var_done, pow_done, norm_done = (step("m_" + n) for n in ("i_set", "add1", "add2", "stats", "aggr", "var", "pow", "norm"))
        xT_ready, xT_hi, xT_lo, z_ready, tz_done, sz_done, dt_ready, dt_added = (step("m_" + n) for n in ("xT", "xT_hi", "xT_lo", "z", "tz", "sz", "dt", "dt_added"))
        soft, exp_u, a_done, cum_ready, cum_copied, exps, dec_in, dec_out, decdt, halo, s_sum = (
            step("m_" + n) for n in ("soft", "exp_u", "a", "cum", "cum_copied", "exps", "dec_in", "dec_out", "decdt", "halo", "s_sum"))
        soft_chain = sem("soft_chain")
        p_ready, raw_done, tap0, tap_chain, taps, tb_done, xc_done = (step("m_" + n) for n in ("p", "raw", "tap0", "tap_chain", "taps", "tb", "xc"))
        turned, xt_done, bt_done, sm_ready, hi_done, hl, u_set, v_set, d_ready, ex_done, xdt_done, M_done, xw_done, xD_done = (
            step("m_" + n) for n in ("turned", "xt", "bt", "sm", "hi", "hl", "u", "v", "d", "ex", "xdt", "M", "xw", "xD"))
        i_ready, y_ready, s_ready, s1_done, S_done, t1_done, t2_done, t3_done, yv_done, sq_done, rs_in, rs_done = (
            step("m_" + n) for n in ("i", "y", "s", "s1", "S", "t1", "t2", "t3", "yv", "sq", "rs_in", "rs"))
        yT_ready, yT_hi, yT_lo, o_ready, xo_done = (step("m_" + n) for n in ("yT", "yT_hi", "yT_lo", "o", "xo"))
        o_stored = [step(f"o_stored{u}", 16) for u in range(2)]

        def cols(row, k, n=1):
            return dts[:, row, k * H:(k + n) * H]

        def per_head(ap, width, parts=P):
            return ap.rearrange("p (h a) -> p h a", a=1).to_broadcast([parts, H, width])

        def by_head(ap):
            return ap.rearrange("p (h d) -> p h d", h=H)

        class At:

            def __init__(self, j, q):
                self.j, self.q, self.group = j, q, 2 * j + q

            def chunk(self, k):
                return self.j * (2 * GC) + (self.q * GC + k)

            def nth(self, k):
                return self.j * GC + (self.q * (GC // 2) + k // 2)

            def block(self, b):
                return self.j * (2 * NB) + (self.q * NB + b)

            def tbuf(self, b):
                return (self.q * NB + b) % 2

        ctx.callback(sem.clear)
        block = ctx.enter_context(nc.Block())

        @block.sync
        def _(sp):
            sp.dma_start(wst[:, :, :], w_in.rearrange("(k p) n -> p k n", p=P)).then_inc(loads, 16)
            sp.dma_start(wost[:, :, :], w_out.rearrange("(k p) n -> p k n", p=P)).then_inc(loads, 16)
            sp.dma_start(cw[:, :, :], conv_w.rearrange("(k p) n -> p k n", p=P)).then_inc(loads, 16)
            sp.dma_start(cb[:, :], conv_b.rearrange("(k p) -> p k", p=P), allow_slow_non_contiguous=True).then_inc(loads, 16)
            sp.dma_start(nw[:, :], norm_w.rearrange("(k p) -> p k", p=P), allow_slow_non_contiguous=True).then_inc(loads, 16)
            for n, v in enumerate((dt_bias, a_log, d_skip)):
                sp.dma_start(heads[:, n, :], v.rearrange("(a h) -> a h", a=1).to_broadcast([P, H])).then_inc(loads, 16)
            for s in (*x_loaded, *o_stored):
                s.open(sp)

            def load(g):
                for k in range(GC):
                    n = g.q * GC + k
                    sp.wait_ge(xo_done.sem, xo_done.done(g.chunk(k - 2 * GC)))
                    sp.dma_start(xr[:, n, :], x[bass.ds(g.chunk(k) * P, P), :]).then_inc(x_loaded[n].sem, 16)

            def store(g):
                for k in range(GC):
                    sp.wait_ge(xo_done.sem, xo_done.done(g.chunk(k)))
                    sp.dma_start(x2[bass.ds(g.chunk(k) * P, P), :], xo[:, k % 2, :]).then_inc(o_stored[k % 2].sem, 16)

            load(At(0, 0))
            with sp.Fori(0, NG // 2 - 1) as j:
                load(At(j, 1))
                store(At(j, 0))
                load(At(j + 1, 0))
                store(At(j, 1))
            load(At(NG // 2 - 1, 1))
            store(At(NG // 2 - 1, 0))
            store(At(NG // 2 - 1, 1))
            for u in range(2):
                sp.wait_ge(o_stored[u].sem, o_stored[u].done(T // 2 - 1))

        @block.gpsimd
        def _(pool):
            chain = Chain(pool, consts)
            pool.memset(flags[:, :], 1.0)
            pool.memset(blk[:, :, :], 0.0)
            pool.memset(ident_bf[:, :], 0.0)
            pool.memset(future[:, :, :], 0.0)
            pool.memset(S[:, :], 0.0)
            pool.memset(U[:, :].bitcast(F32), 0.0)
            pool.memset(HL[:, :].bitcast(F32), 0.0)
            chain.link(pool.memset(raw[:, :, 0:CONV - 1], 0.0))
            for b in range(batches):
                pool.memset(flags[:, b * PER:b * PER + 1], 0.0)
            for qd in range(4):
                chain.link(pool.affine_select(out=blk[:, :, :], in_=blk[:, :, :], compare_op=ALU.not_equal, fill=1.0,
                                              base=-32 * qd, pattern=[[-1, H], [0, P]], channel_multiplier=1))
            chain.link(pool.affine_select(out=ident_bf[:, :], in_=ident_bf[:, :], compare_op=ALU.not_equal, fill=1.0,
                                          base=0, pattern=[[-1, P]], channel_multiplier=1))
            chain.link(pool.affine_select(out=future[:, :, :], in_=future[:, :, :], compare_op=ALU.is_ge, fill=-1e30,
                                          base=0, pattern=[[0, GC], [1, P]], channel_multiplier=-1))
            pool.sem_inc(consts, 1)
            for s in (i_set, pow_done, v_set, xw_done, xD_done, s1_done, t3_done, yv_done, rs_done):
                s.open(pool)
            pool.wait_ge(d_prep, 1)

            def gathers(g, k):
                i, u = g.chunk(k), k % 2
                pool.wait_ge(add2.sem, add2.done(i - 2))
                pool.tensor_copy(idx[:, u, 0:1], slots[:, bass.ds(i, 1)])
                pool.tensor_copy(idx[:, u, 1:2], slots[:, bass.ds(i + T, 1)]).then_inc(i_set.sem, 1)
                pool.wait_ge(i_set.sem, i_set.done(i))
                pool.sem_inc(go, 1)
                for r in range(TOP):
                    pool.indirect_dma_start(out=yg[:, u, r, :], out_offset=None, in_=ys_d,
                                            in_offset=bass.IndirectOffsetOnAxis(ap=idx[:, u, r:r + 1], axis=0)).then_inc(y_gath[u].sem, 16)

            def front(g, k):
                i = g.chunk(k)
                pool.wait_ge(var_done.sem, var_done.done(i))
                pool.tensor_tensor(rstd[:, k % 2:k % 2 + 1], ve[:, k % 2:k % 2 + 1], c["neghalf"][:, 0:1], ALU.pow).then_inc(pow_done.sem, 1)

            def chunk(g, k):
                i = g.chunk(k)
                pool.wait_ge(xt_done.sem, xt_done.done(i))
                pool.wait_ge(s_ready.sem, s_ready.done(i - 1))
                pool.wait_ge(decdt.sem, decdt.done(g.group))
                pool.tensor_tensor(by_head(xw[:, :]), by_head(xt[:, :]), per_head(cols(DECDT, k), HD), ALU.mult).then_inc(xw_done.sem, 1)
                pool.wait_ge(hl.sem, hl.done(i))
                pool.wait_ge(d_ready.sem, d_ready.done(i - 1))
                pool.tensor_tensor(V[0:40, :, :], HL[0:40, :].bitcast(F32).rearrange("p (a t) -> p a t", a=1).to_broadcast([40, H, P]),
                                   blk[0:40, :, :], ALU.mult).then_inc(v_set.sem, 1)
                pool.wait_ge(S_done.sem, S_done.done(i - 1))
                pool.tensor_tensor(by_head(S1[:, :]), by_head(S[:, :]), per_head(cols(ETOT, k)[0:NS, :], HD, NS), ALU.mult).then_inc(s1_done.sem, 1)
                pool.wait_ge(t3_done.sem, t3_done.done(i - 1))
                pool.tensor_tensor(xD[:, :], xt[:, :], dwide[:, :], ALU.mult).then_inc(xD_done.sem, 1)
                pool.wait_ge(xD_done.sem, xD_done.done(i))
                pool.wait_ge(t2_done.sem, t2_done.done(i))
                pool.wait_ge(yv_done.sem, yv_done.done(i - 1))
                pool.tensor_tensor(t3[:, :], t2[:, :], xD[:, :], ALU.add).then_inc(t3_done.sem, 1)
                pool.wait_ge(t3_done.sem, t3_done.done(i))
                pool.wait_ge(yT_ready.sem, yT_ready.done(i - 1))
                pool.wait_ge(sq_done.sem, sq_done.done(i - 1))
                pool.wait_ge(sz_done.sem, sz_done.done(i))
                pool.tensor_tensor(yv[:, :], t3[:, :], sz[:, k, :], ALU.mult).then_inc(yv_done.sem, 1)
                pool.wait_ge(rs_in.sem, rs_in.done(i))
                pool.wait_ge(xo_done.sem, xo_done.done(i - 1))
                pool.tensor_tensor(rs[:, :], vr[:, :], c["neghalf"][:, 0:1], ALU.pow).then_inc(rs_done.sem, 1)

            with pool.Fori(0, NG // 2) as j:
                for q in range(2):
                    g = At(j, q)
                    gathers(g, 0)
                    for k in range(GC):
                        if k + 1 < GC:
                            gathers(g, k + 1)
                        front(g, k)
                    for k in range(GC):
                        chunk(g, k)

        @block.scalar
        def _(act):
            for s in (xT_hi, tz_done, exp_u, exps, dec_out, raw_done, tap0, tb_done, xt_done, bt_done, ex_done, sq_done, yT_hi):
                s.open(act)
            act.wait_ge(loads, 8 * 16)
            act.wait_ge(d_prep, 2)
            act.activation(wih[:, :, :], wst[:, :, :], ACT.Copy)
            act.activation(woh[:, :, :], wost[:, :, :], ACT.Copy)
            act.activation(heads[:, 1, :], heads[:, 1, :], ACT.Exp).then_inc(a_prep, 1)

            def front(g, k):
                i = g.chunk(k)
                act.wait_ge(xT_ready.sem, xT_ready.done(i))
                act.wait_ge(p_ready.sem, p_ready.done(g.block(-1)))
                act.activation(xTh[:, :, k * P:(k + 1) * P], pA[:, 0:D].rearrange("p (k q) -> p k q", k=KD), ACT.Copy).then_inc(xT_hi.sem, 1)
                act.wait_ge(z_ready.sem, z_ready.done(i))
                act.wait_ge(sz_done.sem, sz_done.done(i - 2))
                act.activation(tz[:, k % 2, :], pZ[:, :], ACT.Tanh).then_inc(tz_done.sem, 1)

            def group(g):
                G, B0 = g.group, g.block(0)
                act.wait_ge(soft.sem, soft.done(G))
                act.activation(dts[:, DU, :], dts[:, DABS, :], ACT.Exp, scale=-1.0).then_inc(exp_u.sem, 1)
                for b in range(NB):
                    B = B0 + b
                    act.wait_ge(p_ready.sem, p_ready.done(B))
                    act.wait_ge(halo.sem, halo.done(G - 1))
                    act.activation(raw[:, b, CONV - 1:], pP[b % 2][:, :], ACT.Copy).then_inc(raw_done.sem, 1)
                    act.wait_ge(raw_done.sem, raw_done.done(B))
                    act.wait_ge(turned.sem, turned.done(g.chunk(-1)))
                    act.wait_ge(sm_ready.sem, sm_ready.done(g.chunk(-1)))
                    act.activation(acc[:, b, :], raw[:, b, 0:GT], ACT.Identity, bias=cbh[:, b:b + 1], scale=cwh[:, b, 0:1]).then_inc(tap0.sem, 1)
                    if b > 0:
                        tanh(g, b - 1)
                    if b == 2:
                        act.wait_ge(cum_ready.sem, cum_ready.done(G))
                        act.activation(dts[:, ECUM, :], pCum, ACT.Exp)
                        act.activation(dts[:, ETOT, :], pTot, ACT.Exp).then_inc(exps.sem, 1)
                    if b == 4:
                        act.wait_ge(dec_in.sem, dec_in.done(G))
                        act.activation(dts[:, DEC, :], dts[:, DEC, :], ACT.Exp).then_inc(dec_out.sem, 1)
                tanh(g, NB - 1)

            def tanh(g, b):
                B = g.block(b)
                act.wait_ge(taps.sem, taps.done(B))
                act.wait_ge(xc_done.sem, xc_done.done(B - 2))
                act.activation(tb[:, g.tbuf(b), :], acc[:, b, :], ACT.Tanh).then_inc(tb_done.sem, 1)

            def chunk(g, k):
                i = g.chunk(k)
                act.wait_ge(sm_ready.sem, sm_ready.done(i))
                act.wait_ge(s_ready.sem, s_ready.done(i - 1))
                act.activation(Bt[:, :], pBt, ACT.Copy).then_inc(bt_done.sem, 1)
                act.wait_ge(turned.sem, turned.done(i))
                act.wait_ge(xD_done.sem, xD_done.done(i - 1))
                act.wait_ge(xdt_done.sem, xdt_done.done(i - 1))
                act.activation(xt[:, :], pX[:, :], ACT.Copy).then_inc(xt_done.sem, 1)
                act.wait_ge(d_ready.sem, d_ready.done(i))
                act.wait_ge(M_done.sem, M_done.done(i - 1))
                for n in range(2):
                    last = act.activation(ex[:, n * GC:(n + 1) * GC, :], pD[n][:, :].rearrange("p (h t) -> p h t", h=GC), ACT.Exp)
                last.then_inc(ex_done.sem, 1)
                act.wait_ge(yv_done.sem, yv_done.done(i))
                act.wait_ge(rs_in.sem, rs_in.done(i - 1))
                act.activation(sq[:, :], yv[:, :], ACT.Square, accum_out=ss[:, :]).then_inc(sq_done.sem, 1)
                act.wait_ge(yT_ready.sem, yT_ready.done(i))
                act.wait_ge(o_ready.sem, o_ready.done(i - 1))
                act.activation(yTh[:, :, :], pYT[:, :].rearrange("p (k q) -> p k q", k=KI), ACT.Copy).then_inc(yT_hi.sem, 1)

            with act.Fori(0, NG // 2) as j:
                for q in range(2):
                    g = At(j, q)
                    for k in range(GC):
                        front(g, k)
                    group(g)
                    for k in range(GC):
                        chunk(g, k)

        @block.tensor
        def _(pe):
            for s in (xT_ready, z_ready, dt_ready, cum_ready, p_ready, turned, sm_ready, d_ready, i_ready, y_ready, s_ready, yT_ready, o_ready):
                s.open(pe)
            pe.wait_ge(consts, 8)
            pe.wait_ge(d_prep, 4)
            pe.wait_ge(a_prep, 1)

            def product(out, parts, n):
                for m, (a, b) in enumerate(parts):
                    last = pe.matmul(out, a, b, start=(m == 0), stop=(m == n - 1))
                return last

            def front(g, k):
                i = g.chunk(k)
                pe.wait_ge(norm_done.sem, norm_done.done(i))
                pe.wait_ge(xT_lo.sem, xT_lo.done(i - 1))
                pe.wait_ge(yT_lo.sem, yT_lo.done(g.chunk(-1)))
                for n in range(KD):
                    last = pe.transpose(pA[:, n * P:(n + 1) * P], xn[:, k % 2, n * P:(n + 1) * P], ident[:, :])
                last.then_inc(xT_ready.sem, 1)
                pe.wait_ge(xT_lo.sem, xT_lo.done(i))
                pe.wait_ge(sz_done.sem, sz_done.done(i - 1))
                pe.wait_ge(raw_done.sem, raw_done.done(g.block(-1)))
                tok = slice(k * P, (k + 1) * P)
                parts = [(a[:, n, tok], w[:, n, 0:DIN]) for a, w in ((xTh, wih), (xTh, wil), (xTl, wih)) for n in range(KD)]
                product(pZ[:, :], parts, 3 * KD).then_inc(z_ready.sem, 1)
                pe.wait_ge(dt_added.sem, dt_added.done(i - 1))
                pe.wait_ge(M_done.sem, M_done.done(g.chunk(-1)))
                parts = [(a[:, n, tok], w[:, n, NIN - H:NIN]) for a, w in ((xTh, wih), (xTh, wil), (xTl, wih)) for n in range(KD)]
                product(pDt, parts, 3 * KD).then_inc(dt_ready.sem, 1)

            def group(g):
                G, B0, i0 = g.group, g.block(0), g.chunk(0)
                for b in range(NB):
                    B = B0 + b
                    pe.wait_ge(raw_done.sem, raw_done.done(B - (2 if b > 1 else 1)))
                    pe.wait_ge(sz_done.sem, sz_done.done(i0 + (GC - 1)))
                    pe.wait_ge(xo_done.sem, xo_done.done(i0 - 1))
                    ch = slice(DIN + b * P, DIN + (b + 1) * P)
                    parts = [(w[:, n, ch], a[:, n, :]) for w, a in ((wih, xTh), (wih, xTl), (wil, xTh)) for n in range(KD)]
                    product(pP[b % 2][:, :], parts, 3 * KD).then_inc(p_ready.sem, 1)
                    if b == 2:
                        pe.wait_ge(a_done.sem, a_done.done(G))
                        pe.matmul(pCum, tri[:, :], dts[:, DA, :], start=True, stop=True)
                        pe.matmul(pTot, c["ones_f"][:, :], dts[:, DA, :], start=True, stop=True).then_inc(cum_ready.sem, 1)

            def chunk(g, k):
                i, G, B0 = g.chunk(k), g.group, g.block(0)
                tok = slice(k * P, (k + 1) * P)
                if k == 0:
                    pe.wait_ge(xc_done.sem, xc_done.done(B0 + (NB - 1)))
                    pe.wait_ge(dec_in.sem, dec_in.done(G))
                pe.wait_ge(xt_done.sem, xt_done.done(i - 1))
                pe.wait_ge(M_done.sem, M_done.done(i - 1))
                pe.matmul(pCT, cols(DA, k), tri[:, :], start=True, stop=True)
                pe.matmul(pG, acc[0:NS, KI, tok], CT[:, tok], start=True, stop=True)
                pe.transpose(pBt, acc[0:NS, KI, tok], ident[0:NS, 0:NS]).then_inc(sm_ready.sem, 1)
                for n in range(KI):
                    last = pe.transpose(pX[:, n * P:(n + 1) * P], acc[:, n, tok], ident[:, :])
                last.then_inc(turned.sem, 1)
                pe.wait_ge(S_done.sem, S_done.done(i - 1))
                pe.wait_ge(t1_done.sem, t1_done.done(i - 1))
                pe.matmul(pI[:, :], CT[:, tok], S[:, :], start=True, stop=True).then_inc(i_ready.sem, 1)
                pe.wait_ge(u_set.sem, u_set.done(i))
                pe.wait_ge(v_set.sem, v_set.done(i))
                pe.wait_ge(t2_done.sem, t2_done.done(i - 1))
                for n in range(2):
                    pe.matmul(pD[n][:, :], U[:, :], V[:, n * GC:(n + 1) * GC, :].rearrange("p h t -> p (h t)"), start=True, stop=False)
                    last = pe.matmul(pD[n][:, :], ident_bf[:, :], future[:, :, :].rearrange("p h t -> p (h t)"), start=False, stop=True)
                last.then_inc(d_ready.sem, 1)
                pe.wait_ge(M_done.sem, M_done.done(i))
                pe.wait_ge(xdt_done.sem, xdt_done.done(i))
                for h in range(H):
                    last = pe.matmul(pYp[:, h * HD:(h + 1) * HD], M[:, h, :], xdt[:, h * HD:(h + 1) * HD], start=True, stop=True)
                last.then_inc(y_ready.sem, 1)
                pe.wait_ge(xw_done.sem, xw_done.done(i))
                pe.matmul(pSt, Bt[:, :], xw[:, :], start=True, stop=True).then_inc(s_ready.sem, 1)
                pe.wait_ge(yv_done.sem, yv_done.done(i))
                pe.wait_ge(yT_lo.sem, yT_lo.done(i - 1))
                for n in range(KI):
                    last = pe.transpose(pYT[:, n * P:(n + 1) * P], yv[:, n * P:(n + 1) * P], ident[:, :])
                last.then_inc(yT_ready.sem, 1)
                pe.wait_ge(yT_lo.sem, yT_lo.done(i))
                pe.wait_ge(xo_done.sem, xo_done.done(i - 1))
                parts = [(a[:, n, :], w[:, n, :]) for a, w in ((yTh, woh), (yTh, wol), (yTl, woh)) for n in range(KI)]
                product(pO[:, 0:D], parts, 3 * KI).then_inc(o_ready.sem, 1)

            with pe.Fori(0, NG // 2) as j:
                for q in range(2):
                    g = At(j, q)
                    for k in range(GC):
                        front(g, k)
                    group(g)
                    for k in range(GC):
                        chunk(g, k)

        @block.vector
        def _(dve):
            for s in (add1, add2, stats, aggr, var_done, norm_done, xT_lo, sz_done, dt_added, soft, a_done, cum_copied, decdt, dec_in, halo, tap_chain, hi_done, s_sum,
                      taps, xc_done, hl, u_set, xdt_done, M_done, S_done, t1_done, t2_done, rs_in, yT_lo, xo_done):
                s.open(dve)
            dve.wait_ge(loads, 8 * 16)
            dve.wait_ge(consts, 8)
            chain = Chain(dve, prep)
            link = chain.link
            link(dve.tensor_copy(by_head(dwide[:, :]), per_head(heads[:, 2, :], HD)))
            dve.sem_inc(d_prep, 1)
            link(dve.tensor_scalar(wst[:, :, 0:DIN], wst[:, :, 0:DIN], 0.5, None, ALU.mult))
            for n in range(KI):
                link(dve.tensor_scalar(wost[:, n, :], wost[:, n, :], nw[:, n:n + 1], None, ALU.mult))
            dve.sem_inc(d_prep, 1)
            link(dve.tensor_scalar(cwh[:, :, :], cw[:, :, :], 0.5, None, ALU.mult))
            link(dve.tensor_scalar(cbh[:, :], cb[:, :], 0.5, None, ALU.mult))
            for q in range(2):
                link(dve.memset(U[32 * q:32 * q + H, :].bitcast(F32), 1.0))
            link(dve.tensor_copy(V[:, :, :], blk[:, :, :]))
            dve.wait_ge(a_prep, 1)
            for k in range(GC):
                link(dve.tensor_scalar(negA[:, k, :], heads[:, 1, :], -1.0, None, ALU.mult))
            link(dve.tensor_tensor(wil[:, :, :], wst[:, :, :], wih[:, :, :].bitcast(F32), ALU.subtract))
            link(dve.tensor_tensor(wol[:, :, :], wost[:, :, :], woh[:, :, :].bitcast(F32), ALU.subtract))
            dve.sem_inc(d_prep, 2)

            def front1(g, k):
                i, n, u = g.chunk(k), g.q * GC + k, k % 2
                dve.wait_ge(x_loaded[n].sem, x_loaded[n].done(g.j))
                dve.wait_ge(y_gath[u].sem, y_gath[u].done(g.nth(k) * TOP + (TOP - 1)))
                dve.scalar_tensor_tensor(xr[:, n, :], yg[:, u, 0, :], gates[:, bass.ds(i, 1)], xr[:, n, :], ALU.mult, ALU.add).then_inc(add1.sem, 1)
                dve.wait_ge(add1.sem, add1.done(i))
                dve.scalar_tensor_tensor(xr[:, n, :], yg[:, u, 1, :], gates[:, bass.ds(i + T, 1)], xr[:, n, :], ALU.mult, ALU.add).then_inc(add2.sem, 1)
                dve.wait_ge(add2.sem, add2.done(i))
                dve.bn_stats(st[:, u, :], xr[:, n, :]).then_inc(stats.sem, 1)
                dve.wait_ge(stats.sem, stats.done(i))
                dve.sem_inc(go, 1)
                dve.bn_aggr(mv[:, u, :], st[:, u, :]).then_inc(aggr.sem, 1)
                dve.wait_ge(aggr.sem, aggr.done(i))
                dve.wait_ge(pow_done.sem, pow_done.done(i - 2))
                dve.tensor_scalar(ve[:, u:u + 1], mv[:, u, 1:2], EPS, None, ALU.add).then_inc(var_done.sem, 1)

            def front2(g, k):
                i, n, u = g.chunk(k), g.q * GC + k, k % 2
                dve.wait_ge(pow_done.sem, pow_done.done(i))
                dve.wait_ge(xT_ready.sem, xT_ready.done(i - 2))
                dve.tensor_scalar(xn[:, u, :], xr[:, n, :], mv[:, u, 0:1], rstd[:, u:u + 1], ALU.subtract, ALU.mult).then_inc(norm_done.sem, 1)
                dve.wait_ge(xT_hi.sem, xT_hi.done(i))
                dve.tensor_tensor(xTl[:, :, k * P:(k + 1) * P], pA[:, 0:D].rearrange("p (k q) -> p k q", k=KD),
                                  xTh[:, :, k * P:(k + 1) * P].bitcast(F32), ALU.subtract).then_inc(xT_lo.sem, 1)
                dve.wait_ge(tz_done.sem, tz_done.done(i))
                dve.wait_ge(yv_done.sem, yv_done.done(i - GC))
                dve.scalar_tensor_tensor(sz[:, k, :], tz[:, u, :], 1.0, pZ[:, :], ALU.add, ALU.mult).then_inc(sz_done.sem, 1)
                dve.wait_ge(dt_ready.sem, dt_ready.done(i))
                dve.tensor_tensor(cols(DTR, k), pDt, heads[:, 0, :], ALU.add).then_inc(dt_added.sem, 1)

            NCH = 1 + 5 + (len(ATANH) - 1) + 2

            def softplus(g):
                G, m = g.group, [0]

                def linked(ins):
                    m[0] += 1
                    ins.then_inc(soft_chain, 1)
                    dve.wait_ge(soft_chain, G * NCH + m[0])

                dve.wait_ge(dt_added.sem, dt_added.done(g.chunk(GC - 1)))
                linked(dve.tensor_scalar(dts[:, DPOS, :], dts[:, DTR, :], 0.0, None, ALU.max))
                dve.scalar_tensor_tensor(dts[:, DABS, :], dts[:, DPOS, :], 2.0, dts[:, DTR, :], ALU.mult, ALU.subtract).then_inc(soft.sem, 1)
                dve.wait_ge(exp_u.sem, exp_u.done(G))
                linked(dve.tensor_scalar(dts[:, DS2, :], dts[:, DU, :], 2.0, None, ALU.add))
                linked(dve.reciprocal(dts[:, DQ, :], dts[:, DS2, :]))
                linked(dve.tensor_tensor(dts[:, DS, :], dts[:, DU, :], dts[:, DQ, :], ALU.mult))
                linked(dve.tensor_tensor(dts[:, DS2, :], dts[:, DS, :], dts[:, DS, :], ALU.mult))
                linked(dve.tensor_scalar(dts[:, DQ, :], dts[:, DS2, :], ATANH[0], None, ALU.mult))
                for a in ATANH[1:]:
                    linked(dve.scalar_tensor_tensor(dts[:, DQ, :], dts[:, DQ, :], a, dts[:, DS2, :], ALU.add, ALU.mult))
                linked(dve.scalar_tensor_tensor(dts[:, DQ, :], dts[:, DQ, :], 1.0, dts[:, DS, :], ALU.add, ALU.mult))
                linked(dve.scalar_tensor_tensor(dts[:, DT, :], dts[:, DQ, :], 2.0, dts[:, DPOS, :], ALU.mult, ALU.add))
                dve.tensor_tensor(dts[:, DA, :], dts[:, DT, :], negA[:, :, :].rearrange("p k h -> p (k h)"), ALU.mult).then_inc(a_done.sem, 1)
                assert m[0] == NCH

            def decays(G):
                dve.wait_ge(cum_ready.sem, cum_ready.done(G))
                dve.wait_ge(exps.sem, exps.done(G))
                dve.tensor_copy(dts[:, CUM, :], pCum).then_inc(cum_copied.sem, 1)
                dve.wait_ge(cum_copied.sem, cum_copied.done(G))
                dve.tensor_tensor(dts[:, DEC, :], pTot, dts[:, CUM, :], ALU.subtract).then_inc(dec_in.sem, 1)

            def decays2(G):
                dve.wait_ge(dec_out.sem, dec_out.done(G))
                dve.tensor_tensor(dts[:, DECDT, :], dts[:, DEC, :], dts[:, DT, :], ALU.mult).then_inc(decdt.sem, 1)

            def conv(g):
                G, B0 = g.group, g.block(0)
                for b in range(NB):
                    B = B0 + b
                    dve.wait_ge(tap0.sem, tap0.done(B))
                    for n in range(1, CONV):
                        if n > 1:
                            dve.wait_ge(tap_chain.sem, tap_chain.done(B * 2 + (n - 2)))
                        ins = dve.scalar_tensor_tensor(acc[:, b, :], raw[:, b, n:n + GT], cwh[:, b, n:n + 1], acc[:, b, :], ALU.mult, ALU.add)
                        ins.then_inc(taps.sem if n == CONV - 1 else tap_chain.sem, 1)
                    if b > 0:
                        silu(g, b - 1)
                    if b == 3:
                        decays(G)
                    if b == 4:
                        decays2(G)
                dve.wait_ge(taps.sem, taps.done(B0 + (NB - 1)))
                dve.tensor_scalar(raw[:, :, 0:CONV - 1], raw[:, :, GT:GT + CONV - 1], flags[:, bass.ds(G + 1, 1)], None, ALU.mult).then_inc(halo.sem, 1)
                silu(g, NB - 1)

            def silu(g, b):
                dve.wait_ge(tb_done.sem, tb_done.done(g.block(b)))
                if b < KI:
                    dve.scalar_tensor_tensor(acc[:, b, :], tb[:, g.tbuf(b), :], 1.0, acc[:, b, :], ALU.add, ALU.mult).then_inc(xc_done.sem, 1)
                else:
                    dve.scalar_tensor_tensor(CT[:, :], tb[NS:P, g.tbuf(b), :], 1.0, acc[NS:P, b, :], ALU.add, ALU.mult)
                    dve.scalar_tensor_tensor(acc[0:NS, b, :], tb[0:NS, g.tbuf(b), :], 1.0, acc[0:NS, b, :], ALU.add, ALU.mult).then_inc(xc_done.sem, 1)

            def chunk(g, k):
                i, G, n = g.chunk(k), g.group, g.q * GC + k
                dve.wait_ge(sm_ready.sem, sm_ready.done(i))
                dve.wait_ge(bt_done.sem, bt_done.done(i))
                dve.wait_ge(v_set.sem, v_set.done(i - 1))
                dve.tensor_copy(HL[0:H, :], pCT).then_inc(hi_done.sem, 1)
                dve.wait_ge(hi_done.sem, hi_done.done(i))
                dve.tensor_tensor(HL[32:32 + H, :], pCT, HL[0:H, :].bitcast(F32), ALU.subtract).then_inc(hl.sem, 1)
                dve.wait_ge(hl.sem, hl.done(i))
                dve.wait_ge(d_ready.sem, d_ready.done(i - 1))
                dve.tensor_scalar(U[64:64 + H, :], HL[0:H, :].bitcast(F32), -1.0, None, ALU.mult)
                dve.tensor_scalar(U[96:96 + H, :], HL[32:32 + H, :].bitcast(F32), -1.0, None, ALU.mult).then_inc(u_set.sem, 1)
                dve.wait_ge(xt_done.sem, xt_done.done(i))
                dve.wait_ge(y_ready.sem, y_ready.done(i - 1))
                dve.tensor_tensor(by_head(xdt[:, :]), by_head(xt[:, :]), per_head(cols(DT, k), HD), ALU.mult).then_inc(xdt_done.sem, 1)
                dve.wait_ge(i_ready.sem, i_ready.done(i))
                dve.tensor_tensor(by_head(t1[:, :]), by_head(pI[:, :]), per_head(cols(ECUM, k), HD), ALU.mult).then_inc(t1_done.sem, 1)
                dve.wait_ge(ex_done.sem, ex_done.done(i))
                dve.tensor_tensor(M[:, :, :], ex[:, :, :], pG.rearrange("p (a t) -> p a t", a=1).to_broadcast([P, H, P]), ALU.mult).then_inc(M_done.sem, 1)
                dve.wait_ge(y_ready.sem, y_ready.done(i))
                dve.wait_ge(t1_done.sem, t1_done.done(i))
                dve.wait_ge(t3_done.sem, t3_done.done(i - 1))
                dve.tensor_tensor(t2[:, :], t1[:, :], pYp[:, :], ALU.add).then_inc(t2_done.sem, 1)
                dve.wait_ge(s_ready.sem, s_ready.done(i))
                dve.wait_ge(s1_done.sem, s1_done.done(i))
                if k == GC - 1:
                    dve.tensor_tensor(S[:, :], S1[:, :], pSt, ALU.add).then_inc(s_sum.sem, 1)
                    dve.wait_ge(s_sum.sem, s_sum.done(G))
                    dve.tensor_scalar(S[:, :], S[:, :], flags[0:NS, bass.ds(G + 1, 1)], None, ALU.mult).then_inc(S_done.sem, 1)
                else:
                    dve.tensor_tensor(S[:, :], S1[:, :], pSt, ALU.add).then_inc(S_done.sem, 1)
                dve.wait_ge(sq_done.sem, sq_done.done(i))
                dve.wait_ge(rs_done.sem, rs_done.done(i - 1))
                dve.tensor_scalar(vr[:, :], ss[:, :], 1.0 / DIN, EPS, ALU.mult, ALU.add).then_inc(rs_in.sem, 1)
                dve.wait_ge(yT_hi.sem, yT_hi.done(i))
                dve.tensor_tensor(yTl[:, :, :], pYT[:, :].rearrange("p (k q) -> p k q", k=KI), yTh[:, :, :].bitcast(F32), ALU.subtract).then_inc(yT_lo.sem, 1)
                dve.wait_ge(o_ready.sem, o_ready.done(i))
                dve.wait_ge(rs_done.sem, rs_done.done(i))
                dve.wait_ge(o_stored[k % 2].sem, o_stored[k % 2].done(g.nth(k) - 1))
                dve.scalar_tensor_tensor(xo[:, k % 2, :], pO[:, 0:D], rs[:, 0:1], xr[:, n, :], ALU.mult, ALU.add).then_inc(xo_done.sem, 1)

            with dve.Fori(0, NG // 2) as j:
                for q in range(2):
                    g = At(j, q)
                    for k in range(GC):
                        front1(g, k)
                        front2(g, k)
                    softplus(g)
                    conv(g)
                    for k in range(GC):
                        chunk(g, k)


def program(nc, x, w_in, conv_w, conv_b, dt_bias, a_log, d_skip, norm_w, w_out, router_w, w1, w2, out):
    with ExitStack() as ctx:
        batches, tokens = x.shape[0], x.shape[0] * x.shape[1]
        xf, of = x.rearrange("b t d -> (b t) d"), out.rearrange("b t d -> (b t) d")
        nt = (TOP * tokens + E * (P - 1)) // P + 1
        xn_d = nc.dram_tensor("xn_d", (tokens, D), F32, kind="Internal").ap()
        ys_d = nc.dram_tensor("ys_d", (nt * P, D), F32, kind="Internal").ap()
        x2_d = nc.dram_tensor("x2_d", (tokens, D), F32, kind="Internal").ap()
        lo_d = nc.dram_tensor("lo_d", (2, P, E * WCOLS), F32, kind="Internal").ap()
        c = make_constants(nc, ctx)
        keep = make_keep(nc, ctx, tokens)
        build_constants(nc, c)
        ffn_block(nc, c, keep, xf, router_w, w1, w2, xn_d, ys_d, lo_d, None, True)
        mamba_block(nc, c, keep, xf, ys_d, w_in, conv_w, conv_b, dt_bias, a_log, d_skip, norm_w, w_out, x2_d, batches)
        ffn_block(nc, c, keep, x2_d, router_w, w1, w2, xn_d, ys_d, lo_d, of, False)


_INS = ["L0_attn_x", "L0_attn_W_in", "L0_attn_conv_w", "L0_attn_conv_b", "L0_attn_dt_bias", "L0_attn_A_log", "L0_attn_D",
        "L0_attn_norm_weight", "L0_attn_W_out", "L0_ffn_router_w", "L0_ffn_w1", "L0_ffn_w2"]


def kernel(**inputs):
    import numpy as _np
    import concourse.bacc as _bacc
    from concourse import mybir as _mybir
    from concourse.bass_utils import run_bass_kernel_spmd as _run

    nc = _bacc.Bacc("TRN2", target_bir_lowering=False, num_devices=1)
    arrays, args = {}, []
    for name in _INS:
        a = _np.ascontiguousarray(inputs[name])
        arrays[f"in_{name}_dram"] = a
        args.append(nc.dram_tensor(f"in_{name}_dram", a.shape, _mybir.dt.from_np(a.dtype), kind="ExternalInput").ap())
    shape = inputs["L0_attn_x"].shape
    args.append(nc.dram_tensor("out_0_dram", shape, _mybir.dt.float32, kind="ExternalOutput").ap())
    program(nc, *args)
    r = _run(nc, [arrays], core_ids=[0])
    return r.results[0]["out_0_dram"]
```

```python
from contextlib import ExitStack

import concourse.bass as bass
from concourse import mybir

F32 = mybir.dt.float32
F32R = mybir.dt.float32r
BF16 = mybir.dt.bfloat16
I32 = mybir.dt.int32
U32 = mybir.dt.uint32
ALU = mybir.AluOpType
ACT = mybir.ActivationFunctionType
AX = mybir.AxisListType

P = 128
D = 256
KD = D // P
E = 8
HID = 512
KH = HID // P
TOP = 2
EPS = 1e-5
BIG = 3.0e38
WCOLS = KD * HID
AG = 4
PC = 8
EB = 4

CREDIT = 2


class Step:

    def __init__(self, sem, unit=1, credit=CREDIT):
        self.sem, self.unit, self.credit = sem, unit, credit

    def open(self, eng):
        eng.sem_inc(self.sem, self.credit * self.unit)

    def done(self, item):
        return (item + (1 + self.credit)) * self.unit


class Gathers:

    def __init__(self, nc, ctx, name):
        self.sems = [ctx.enter_context(nc.semaphore(f"{name}{u}")) for u in range(2)]
        self.before = 0

    def take(self, n):
        steps = [Step(s, 16, self.before) for s in self.sems]
        self.before += n
        return steps


class Chain:

    def __init__(self, eng, sem):
        self.eng, self.sem, self.n = eng, sem, 0

    def link(self, ins):
        self.n += 1
        ins.then_inc(self.sem, 1)
        self.eng.wait_ge(self.sem, self.n)


class Sems:

    def __init__(self, nc, ctx):
        self.nc, self.ctx, self.all = nc, ctx, []

    def __call__(self, name):
        self.all.append(self.ctx.enter_context(self.nc.semaphore(name)))
        return self.all[-1]

    def clear(self):
        with self.nc.Block() as block:
            @block.sync
            def _(sp):
                for s in self.all:
                    sp.sem_clear(s)


def make_constants(nc, ctx):
    def sb(name, shape, dt):
        return ctx.enter_context(nc.sbuf_tensor(name, shape, dt))
    return {
        "ident": sb("ident", [P, P], F32),
        "incl_tri": sb("incl_tri", [P, P], F32),
        "strict_tri": sb("strict_tri", [P, P], BF16),
        "ones_bf": sb("ones_bf", [P, P], BF16),
        "ones_f": sb("ones_f", [P, P], F32),
        "part": sb("part", [P, 1], F32),
        "neghalf": sb("neghalf", [P, 8], F32),
    }


def build_constants(nc, c):
    with ExitStack() as ctx:
        sems = Sems(nc, ctx)
        s_set = sems("s_const")
        ctx.callback(sems.clear)
        block = ctx.enter_context(nc.Block())

        @block.gpsimd
        def _(pool):
            chain = Chain(pool, s_set)
            pool.memset(c["ident"][:, :], 0.0)
            pool.memset(c["incl_tri"][:, :], 1.0)
            pool.memset(c["strict_tri"][:, :], 1.0)
            pool.memset(c["ones_bf"][:, :], 1.0)
            pool.memset(c["ones_f"][:, :], 1.0)
            pool.memset(c["neghalf"][:, :], -0.5)
            chain.link(pool.iota(c["part"][:, :], pattern=[[0, 1]], base=0, channel_multiplier=1,
                                 allow_small_or_imprecise_dtypes=True))
            for name, op, fill, sign in (("ident", ALU.not_equal, 1.0, -1), ("incl_tri", ALU.is_ge, 0.0, 1),
                                         ("strict_tri", ALU.is_gt, 0.0, 1)):
                chain.link(pool.affine_select(out=c[name][:, :], in_=c[name][:, :], compare_op=op, fill=fill,
                                              base=0, pattern=[[sign, P]], channel_multiplier=-sign))


def ffn_block(nc, c, keep, x, router_w, w1, w2, xn_d, ys_d, lo_d, out, first):
    TOK = x.shape[0]
    T = TOK // P
    NT = (TOP * TOK + E * (P - 1)) // P
    NT += NT % 2
    C = TOP * T
    with ExitStack() as ctx:
        def sb(name, shape, dt):
            return ctx.enter_context(nc.sbuf_tensor(name, shape, dt))

        def psum(name, dt=F32, n=512):
            return ctx.enter_context(nc.psum_tensor(name, [P, n], dt))

        sem = Sems(nc, ctx)

        def step(name, unit=1):
            return Step(sem(name), unit)


        tag = "1" if first else "2"
        ident = c["ident"]
        w1h, w2h, gates = keep["w1h"], keep["w2h"], keep["gates"]
        w1l = sb("w1l" + tag, [P, E * WCOLS], F32R)
        w2l = sb("w2l" + tag, [P, E * WCOLS], F32R)
        wst = sb("wst" + tag, [P, 2, WCOLS], F32) if first else None
        xs = sb("xs" + tag, [P, EB * (1 + TOP), D], F32)
        xa, xn = xs[:, 0:2 * AG, :], xs[:, 2 * AG:3 * AG, :]
        ea = xs[:, :, :].rearrange("p (u r) d -> p u r d", r=1 + TOP)
        st = sb("st" + tag, [P, AG, 6], F32)
        mv = sb("mv" + tag, [P, 2 * AG, 2], F32)
        ve = sb("ve" + tag, [P, 2, AG], F32)
        rstd = sb("rstd" + tag, [P, 2, AG], F32)
        xT = sb("xT" + tag, [P, 2, KD, P], F32)
        rw = sb("rw" + tag, [E, D], F32)
        rwT = sb("rwT" + tag, [P, KD, E], F32)
        logits = sb("logits" + tag, [P, T, E], F32)
        iota_e = sb("iota_e" + tag, [P, T, E], F32)
        iota_col = sb("iota_col" + tag, [P, P], F32)
        iota_bf = sb("iota_bf" + tag, [P, P], BF16)
        iota_j = sb("iota_j" + tag, [P, NT, E], F32)
        colnum = sb("colnum" + tag, [P, C], F32)
        slots = sb("slots" + tag, [P, C], U32)
        work = [sb(f"work{n}_{tag}", [P, T, E], F32) for n in range(6)]
        oh = [sb(f"oh{n}_{tag}", [P, T, E], F32) for n in range(TOP)]
        top = sb("top" + tag, [P, 6, T], F32)
        both = sb("both" + tag, [P, T * E], BF16)
        small = sb("small" + tag, [P, 8, E], F32)
        smalli = sb("smalli" + tag, [P, 2, E], I32)
        slotf = sb("slotf" + tag, [P, C], F32)
        parts_i = sb("parts_i" + tag, [P, 2, C], U32)
        parts_b = sb("parts_b" + tag, [P, 2, C], BF16)
        expert_f = sb("expert_f" + tag, [P, NT], F32)
        expert_i = sb("expert_i" + tag, [P, NT], I32)
        ohhi, ohhi_c, ohhi_p = (sb(n + tag, [P, 2, PC, NT], BF16) for n in ("ohhi", "ohhi_c", "ohhi_p"))
        ohlo = sb("ohlo" + tag, [P, 2, PC, P], BF16)
        inv = sb("inv" + tag, [P, P], F32)
        inv2 = sb("inv2" + tag, [P, P], F32)
        row_f = sb("row_f" + tag, [P, 2, NT], F32)
        spare = sb("spare" + tag, [P, NT], F32)
        row_of = sb("row_of" + tag, [P, NT], U32)
        row_t = sb("row_t" + tag, [P, NT], U32)
        token_of = sb("token_of" + tag, [P, NT], U32)
        idx = sb("idx" + tag, [P, 2, 1], U32)
        ridx = sb("ridx" + tag, [P, 2, 1], U32)
        xg = sb("xg" + tag, [P, 2, D], F32)
        xh = sb("xh" + tag, [P, 2, KD, P], F32R)
        xl = sb("xl" + tag, [P, 2, KD, P], F32R)
        r = sb("r" + tag, [P, 2, HID], F32)
        h2 = sb("h2" + tag, [P, 2, KH, P], F32)
        h2h = sb("h2h" + tag, [P, 2, KH, P], F32R)
        h2l = sb("h2l" + tag, [P, 2, KH, P], F32R)
        y = sb("y" + tag, [P, 2, D], F32)


        pT = [psum(f"pT{u}{tag}") for u in range(2)]
        pH = [psum(f"pH{u}{tag}") for u in range(2)]
        pR = [psum(f"pR{u}{tag}") for u in range(2)]
        pY = [psum(f"pY{u}{tag}") for u in range(2)]

        w_loaded = [sem(f"w_loaded{u}") for u in range(2)]
        w_hi, w_lo = step("w_hi"), step("w_lo")
        w_spilt, rw_loaded = sem("w_spilt"), sem("rw_loaded")
        xa_loaded = [step(f"xa_loaded{n}", 16) for n in range(2 * AG)]
        var_done, pow_done, norm_done, mv_done = step("var_done"), step("pow_done"), step("norm_done"), step("mv_done")
        st_chain, aggr_go = step("st_chain"), sem("aggr_go")
        xn_stored = [step(f"xn_stored{n}", 16) for n in range(AG)]
        xT_ready, xT_copied, logit_ready, logit_copied = (step(n) for n in ("xT_ready", "xT_copied", "logit_ready", "logit_copied"))
        iotas, b_chain, exp_in, exp_out, counts_in, counts_out = (sem(n) for n in ("iotas", "b_chain", "exp_in", "exp_out", "counts_in", "counts_out"))
        rwT_ready = sem("rwT_ready")
        oh_built, oh_used = step("oh_built"), step("oh_used")
        inv_ready, invT_ready, routed = sem("inv_ready"), sem("invT_ready"), sem("routed")
        idx_set, dma_go, gathered = step("idx_set"), sem("dma_go"), keep["gathers"].take(NT // 2)
        ridx_set, scattered = step("ridx_set"), keep["scatters"].take(NT // 2)
        g_T, g_hi, g_split, h_ready, relu_done, rT_ready, sq_done, h2_hi, h2_split, y_ready, y_copied = (
            step(n) for n in ("g_T", "g_hi", "g_split", "h_ready", "relu_done", "rT_ready", "sq_done", "h2_hi", "h2_split", "y_ready", "y_copied"))
        e_loaded = [step(f"e_loaded{u}", 16 * (1 + TOP)) for u in range(EB)]
        e_stored = [step(f"e_stored{u}", 16) for u in range(EB)]
        e_first, e_done = step("e_first"), step("e_done")

        def wsrc(n):
            return (w1 if n % 2 == 0 else w2)[n // 2].rearrange("(k p) n -> p k n", p=P)

        def whi(n):
            return (w1h if n % 2 == 0 else w2h)[:, (n // 2) * WCOLS:(n // 2 + 1) * WCOLS]

        def wlo(n):
            return (w1l if n % 2 == 0 else w2l)[:, (n // 2) * WCOLS:(n // 2 + 1) * WCOLS]

        NW = 2 * E
        ctx.callback(sem.clear)
        block = ctx.enter_context(nc.Block())

        @block.sync
        def _(sp):
            sp.dma_start(rw[:, :], router_w).then_inc(rw_loaded, 16)
            if not first:
                sp.dma_start(w1l[:, :].bitcast(F32), lo_d[0]).then_inc(w_loaded[0], 16)
                sp.dma_start(w2l[:, :].bitcast(F32), lo_d[1]).then_inc(w_loaded[1], 16)
            for s in (*xa_loaded, *xn_stored):
                s.open(sp)

            def load(j, h, before=True):
                if before:
                    sp.wait_ge(norm_done.sem, norm_done.done((2 * j + (h - 1)) * AG - 1))
                for n in range(AG):
                    sp.dma_start(xa[:, h * AG + n, :], x[bass.ds(((2 * j + h) * AG + n) * P, P), :]).then_inc(xa_loaded[h * AG + n].sem, 16)

            def store(j, h):
                for n in range(AG):
                    i = (2 * j + h) * AG + n
                    sp.wait_ge(norm_done.sem, norm_done.done(i))
                    sp.dma_start(xn_d[bass.ds(i * P, P), :], xn[:, n, :]).then_inc(xn_stored[n].sem, 16)

            load(0, 0, False)
            load(0, 1, False)
            with sp.Fori(0, T // (2 * AG) - 1) as j:
                for h in range(2):
                    store(j, h)
                    load(j + 1, h)
            store(T // (2 * AG) - 1, 0)
            store(T // (2 * AG) - 1, 1)
            if first:
                sp.wait_ge(w_lo.sem, w_lo.done(NW - 1))
                sp.dma_start(lo_d[0], w1l[:, :].bitcast(F32)).then_inc(w_spilt, 16)
                sp.dma_start(lo_d[1], w2l[:, :].bitcast(F32)).then_inc(w_spilt, 16)
                sp.wait_ge(w_spilt, 32)
            if out is not None:
                for s in e_loaded:
                    s.open(sp)
                for u in range(2):
                    sp.wait_ge(scattered[u].sem, scattered[u].done(NT // 2 - 1))
                with sp.Fori(0, T // EB) as j:
                    for u in range(EB):
                        i = EB * j + u
                        sp.wait_ge(e_stored[u].sem, e_stored[u].done(j - 1))
                        sp.dma_start(ea[:, u, 0, :], x[bass.ds(i * P, P), :]).then_inc(e_loaded[u].sem, 16)
                        for k in range(TOP):
                            sp.dma_start(ea[:, u, 1 + k, :], ys_d[bass.ds((i + (1 + k * T)) * P, P), :]).then_inc(e_loaded[u].sem, 16)

        @block.gpsimd
        def _(pool):
            pool.iota(iota_e[:, :, :], pattern=[[0, T], [1, E]], base=0, channel_multiplier=0,
                      allow_small_or_imprecise_dtypes=True)
            pool.iota(iota_col[:, :], pattern=[[1, P]], base=0, channel_multiplier=0,
                      allow_small_or_imprecise_dtypes=True).then_inc(iotas, 1)
            pool.iota(iota_j[:, :, :], pattern=[[1, NT], [0, E]], base=0, channel_multiplier=0,
                      allow_small_or_imprecise_dtypes=True)
            pool.iota(colnum[:, :], pattern=[[1, C]], base=1, channel_multiplier=0,
                      allow_small_or_imprecise_dtypes=True)
            pool.iota(spare[:, :], pattern=[[0, NT // 2], [(C + 1) * P, 2]], base=0, channel_multiplier=1,
                      allow_small_or_imprecise_dtypes=True).then_inc(iotas, 1)
            pow_done.open(pool)
            w_lo.open(pool)

            def lo_weights(n):
                pool.wait_ge(w_hi.sem, w_hi.done(n))
                pool.tensor_tensor(wlo(n), wst[:, n % 2, :], whi(n).bitcast(F32), ALU.subtract).then_inc(w_lo.sem, 1)

            def pows(j):
                for h in range(2):
                    pool.wait_ge(var_done.sem, var_done.done(2 * j + h))
                    pool.tensor_tensor(rstd[:, h, :], ve[:, h, :], c["neghalf"][:, 0:AG], ALU.pow).then_inc(pow_done.sem, 1)

            steps = T // (2 * AG)
            if first:
                assert steps * AG == NW
                for j in range(steps):
                    pows(j)
                    for n in range(AG * j, AG * (j + 1)):
                        lo_weights(n)
            else:
                with pool.Fori(0, steps) as j:
                    pows(j)
            pool.wait_ge(routed, 1)
            for s in xn_stored:
                pool.wait_ge(s.sem, s.done(T // AG - 1))
            idx_set.open(pool)
            ridx_set.open(pool)

            def column(table, t):
                return table[:, t:t + 1] if isinstance(t, int) else table[:, bass.ds(t, 1)]

            def gather(t, u):
                pool.wait_ge(g_T.sem, g_T.done(t - 2))
                pool.tensor_copy(idx[:, u, :], column(token_of, t)).then_inc(idx_set.sem, 1)
                pool.wait_ge(idx_set.sem, idx_set.done(t))
                pool.sem_inc(dma_go, 1)
                pool.indirect_dma_start(out=xg[:, u, :], out_offset=None, in_=xn_d,
                                        in_offset=bass.IndirectOffsetOnAxis(ap=idx[:, u, :], axis=0)).then_inc(gathered[u].sem, 16)

            def scatter(t, u):
                pool.wait_ge(y_copied.sem, y_copied.done(t))
                pool.tensor_copy(ridx[:, u, :], column(row_of, t)).then_inc(ridx_set.sem, 1)
                pool.wait_ge(ridx_set.sem, ridx_set.done(t))
                pool.sem_inc(dma_go, 1)
                pool.indirect_dma_start(out=ys_d, out_offset=bass.IndirectOffsetOnAxis(ap=ridx[:, u, :], axis=0),
                                        in_=y[:, u, :], in_offset=None).then_inc(scattered[u].sem, 16)

            for t in range(5):
                gather(t, t % 2)
            with pool.Fori(0, NT // 2 - 3) as j:
                for u in range(2):
                    gather(2 * j + (5 + u), 1 - u)
                    scatter(2 * j + u, u)
            gather(NT - 1, 1)
            for t in range(NT - 6, NT):
                scatter(t, t % 2)
            for u in range(2):
                pool.wait_ge(scattered[u].sem, scattered[u].done(NT // 2 - 1))

        @block.scalar
        def _(act):
            for s in (w_hi, xT_copied, logit_copied, relu_done, sq_done):
                s.open(act)

            def hi_weights(n):
                act.wait_ge(w_loaded[n % 2], 16 * (n // 2 + 1))
                act.activation(whi(n), wst[:, n % 2, :], ACT.Copy).then_inc(w_hi.sem, 1)

            def load_weights(n):
                if n >= 2:
                    act.wait_ge(w_lo.sem, w_lo.done(n - 2))
                act.dma_start(wst[:, n % 2, :].rearrange("p (k n) -> p k n", k=KD if n % 2 == 0 else KH), wsrc(n)).then_inc(w_loaded[n % 2], 16)

            def stage_a(j):
                for u in range(2):
                    i = 2 * j + u
                    act.wait_ge(xT_ready.sem, xT_ready.done(i))
                    act.activation(xT[:, u, :, :], pT[u][:, 0:D].rearrange("p (k q) -> p k q", k=KD), ACT.Copy).then_inc(xT_copied.sem, 1)
                for u in range(2):
                    i = 2 * j + u
                    act.wait_ge(logit_ready.sem, logit_ready.done(i))
                    dst = logits[:, i, :] if isinstance(i, int) else logits[:, bass.ds(i, 1), :].rearrange("p a e -> p (a e)")
                    act.activation(dst, pY[u][:, 0:E], ACT.Copy).then_inc(logit_copied.sem, 1)

            if first:
                load_weights(0)
                for n in range(NW):
                    if n + 1 < NW:
                        load_weights(n + 1)
                    hi_weights(n)
                    stage_a(n)
                for j in range(NW, T // 2):
                    stage_a(j)
            else:
                with act.Fori(0, T // 2) as j:
                    stage_a(j)
            act.wait_ge(exp_in, 1)
            act.activation(top[:, 3, :], top[:, 2, :], ACT.Exp).then_inc(exp_out, 1)

            def relu(t, u):
                act.wait_ge(h_ready.sem, h_ready.done(t))
                act.activation(r[:, u, :], pH[u][:, :], ACT.Relu).then_inc(relu_done.sem, 1)

            def square(t, u):
                act.wait_ge(rT_ready.sem, rT_ready.done(t))
                act.wait_ge(h2_split.sem, h2_split.done(t - 2))
                act.activation(h2[:, u, :, :], pR[u][:, :].rearrange("p (k q) -> p k q", k=KH), ACT.Square).then_inc(sq_done.sem, 1)

            relu(0, 0)
            with act.Fori(0, NT // 2 - 1) as j:
                for u in range(2):
                    relu(2 * j + (u + 1), 1 - u)
                    square(2 * j + u, u)
            relu(NT - 1, 1)
            square(NT - 2, 0)
            square(NT - 1, 1)
            if out is not None:
                for s in e_stored:
                    s.open(act)
                with act.Fori(0, T // EB) as j:
                    for u in range(EB):
                        act.wait_ge(e_done.sem, e_done.done(EB * j + u))
                        act.dma_start(out[bass.ds((EB * j + u) * P, P), :], ea[:, u, 0, :]).then_inc(e_stored[u].sem, 16)
                for s in e_stored:
                    act.wait_ge(s.sem, s.done(T // EB - 1))

        @block.tensor
        def _(pe):
            for s in (xT_ready, logit_ready, oh_used, g_T, h_ready, rT_ready, y_ready):
                s.open(pe)
            pe.wait_ge(rw_loaded, 16)
            for k in range(KD):
                last = pe.transpose(pR[0][:, k * E:(k + 1) * E], rw[:, k * P:(k + 1) * P], ident[0:E, 0:E])
            last.then_inc(rwT_ready, 1)
            pe.wait_ge(rwT_ready, 2)
            with pe.Fori(0, T // AG) as j:
                for m in range(0, AG, 2):
                    for u in range(2):
                        i = AG * j + (m + u)
                        pe.wait_ge(norm_done.sem, norm_done.done(i))
                        pe.wait_ge(xT_copied.sem, xT_copied.done(i - 2))
                        for k in range(KD):
                            last = pe.transpose(pT[u][:, k * P:(k + 1) * P], xn[:, m + u, k * P:(k + 1) * P], ident[:, :])
                        last.then_inc(xT_ready.sem, 1)
                    for u in range(2):
                        i = AG * j + (m + u)
                        pe.wait_ge(xT_copied.sem, xT_copied.done(i))
                        pe.wait_ge(logit_copied.sem, logit_copied.done(i - 2))
                        for k in range(KD):
                            last = pe.matmul(pY[u][:, 0:E], xT[:, u, k, :], rwT[:, k, :], start=(k == 0), stop=(k == KD - 1))
                        last.then_inc(logit_ready.sem, 1)
            pe.wait_ge(counts_in, 1)
            pe.matmul(pR[0][:, 0:T * E], c["strict_tri"][:, :], both[:, :], start=True, stop=True)
            pe.matmul(pR[1][:, 0:T * E], c["ones_bf"][:, :], both[:, :], start=True, stop=True).then_inc(counts_out, 1)

            for piece in range(C // PC):
                pe.wait_ge(oh_built.sem, oh_built.done(piece))
                for n in range(PC):
                    ends = dict(start=(piece == 0 and n == 0), stop=(piece == C // PC - 1 and n == PC - 1))
                    pe.matmul(pT[0][0:NT, 0:P], ohhi_p[:, piece % 2, n, :], ohlo[:, piece % 2, n, :], **ends)
                    last = pe.matmul(pT[1][0:NT, 0:P], ohhi_c[:, piece % 2, n, :], ohlo[:, piece % 2, n, :], **ends)
                last.then_inc(oh_used.sem, 1)
            pe.wait_ge(inv_ready, 1)
            pe.transpose(pY[0][:, 0:NT], inv[0:NT, :], ident[0:NT, 0:NT]).then_inc(invT_ready, 1)

            def expert_columns(t):
                return pe.value_load(expert_i[0:1, t:t + 1] if isinstance(t, int) else expert_i[0:1, bass.ds(t, 1)],
                                     min_val=0, max_val=(E - 1) * WCOLS)

            def turn_x(t, u):
                pe.wait_ge(gathered[u].sem, gathered[u].done(half(t, u)))
                for k in range(KD):
                    last = pe.transpose(pT[u][:, k * P:(k + 1) * P], xg[:, u, k * P:(k + 1) * P], ident[:, :])
                last.then_inc(g_T.sem, 1)

            def up(t, u):
                at = expert_columns(t)
                pe.wait_ge(g_split.sem, g_split.done(t))
                n = 0
                for a, w in ((xh, w1h), (xh, w1l), (xl, w1h)):
                    for k in range(KD):
                        last = pe.matmul(pH[u][:, :], a[:, u, k, :], w[:, bass.ds(at + k * HID, HID)],
                                         start=(n == 0), stop=(n == 3 * KD - 1))
                        n += 1
                last.then_inc(h_ready.sem, 1)

            def turn_h(t, u):
                pe.wait_ge(relu_done.sem, relu_done.done(t))
                for k in range(KH):
                    last = pe.transpose(pR[u][:, k * P:(k + 1) * P], r[:, u, k * P:(k + 1) * P], ident[:, :])
                last.then_inc(rT_ready.sem, 1)

            def down(t, u):
                at = expert_columns(t)
                pe.wait_ge(h2_split.sem, h2_split.done(t))
                pe.wait_ge(y_copied.sem, y_copied.done(t - 2))
                n = 0
                for a, w in ((h2h, w2h), (h2h, w2l), (h2l, w2h)):
                    for k in range(KH):
                        last = pe.matmul(pY[u][:, 0:D], a[:, u, k, :], w[:, bass.ds(at + k * D, D)],
                                         start=(n == 0), stop=(n == 3 * KH - 1))
                        n += 1
                last.then_inc(y_ready.sem, 1)

            def half(t, u):
                return (t - u) // 2 if isinstance(t, int) else t

            if not first:
                for s in w_loaded:
                    pe.wait_ge(s, 16)
            turn_x(0, 0)
            turn_x(1, 1)
            up(0, 0)
            turn_x(2, 0)
            up(1, 1)
            turn_h(0, 0)
            with pe.Fori(0, NT // 2 - 2) as j:
                for u in range(2):
                    v = 1 - u
                    up(2 * j + (2 + u), u)
                    pe.wait_ge(gathered[v].sem, gathered[v].done(j + 1 + u))
                    for k in range(KD):
                        last = pe.transpose(pT[v][:, k * P:(k + 1) * P], xg[:, v, k * P:(k + 1) * P], ident[:, :])
                    last.then_inc(g_T.sem, 1)
                    turn_h(2 * j + (1 + u), v)
                    down(2 * j + u, u)
            t = NT - 3
            turn_x(t + 2, 1)
            up(t + 1, 0)
            turn_h(t, 1)
            down(t - 1, 0)
            up(t + 2, 1)
            turn_h(t + 1, 0)
            down(t, 1)
            turn_h(t + 2, 1)
            down(t + 1, 0)
            down(t + 2, 1)

        @block.vector
        def _(dve):
            for s in (st_chain, mv_done, var_done, norm_done, oh_built, g_hi, g_split, h2_hi, h2_split, y_copied):
                s.open(dve)
            dve.wait_ge(rwT_ready, 1)
            dve.tensor_copy(rwT[:, :, :], pR[0][:, 0:KD * E].rearrange("p (k e) -> p k e", k=KD)).then_inc(rwT_ready, 1)

            def moments(j, h):
                for n in range(AG):
                    dve.wait_ge(xa_loaded[h * AG + n].sem, xa_loaded[h * AG + n].done(j))
                    last = dve.bn_stats(st[:, n, :], xa[:, h * AG + n, :])
                last.then_inc(st_chain.sem, 1)
                dve.wait_ge(st_chain.sem, st_chain.done(2 * j + h))
                dve.sem_inc(aggr_go, 1)
                for n in range(AG):
                    last = dve.bn_aggr(mv[:, h * AG + n, :], st[:, n, :])
                last.then_inc(mv_done.sem, 1)
                dve.wait_ge(mv_done.sem, mv_done.done(2 * j + h))
                dve.tensor_scalar(ve[:, h, :], mv[:, h * AG:(h + 1) * AG, 1], EPS, None, ALU.add).then_inc(var_done.sem, 1)

            def normalise(j, h, before=True):
                dve.wait_ge(pow_done.sem, pow_done.done(2 * j + h))
                for n in range(AG):
                    i = (2 * j + h) * AG + n
                    if before:
                        dve.wait_ge(xT_ready.sem, xT_ready.done(i - AG))
                        dve.wait_ge(xn_stored[n].sem, xn_stored[n].done(2 * j + (h - 1)))
                    dve.tensor_scalar(xn[:, n, :], xa[:, h * AG + n, :], mv[:, h * AG + n, 0:1], rstd[:, h, n:n + 1],
                                      ALU.subtract, ALU.mult).then_inc(norm_done.sem, 1)

            moments(0, 0)
            moments(0, 1)
            normalise(0, 0, False)
            with dve.Fori(0, T // (2 * AG) - 1) as j:
                moments(j + 1, 0)
                normalise(j, 1)
                moments(j + 1, 1)
                normalise(j + 1, 0)
            normalise(T // (2 * AG) - 1, 1)

            chain = Chain(dve, b_chain)
            link = chain.link
            dve.wait_ge(iotas, 2)
            dve.wait_ge(logit_copied.sem, logit_copied.done(T - 1))

            def wide(ap):
                return ap.rearrange("p (t a) -> p t a", a=1).to_broadcast([P, T, E])

            def first_largest(scores, best, num, onehot):
                link(dve.tensor_reduce(best, scores, AX.X, ALU.max))
                link(dve.tensor_tensor(work[0][:, :, :], scores, wide(best), ALU.not_equal))
                link(dve.scalar_tensor_tensor(work[1][:, :, :], work[0][:, :, :], float(E), iota_e[:, :, :], ALU.mult, ALU.add))
                link(dve.tensor_reduce(num, work[1][:, :, :], AX.X, ALU.min))
                link(dve.tensor_tensor(onehot, iota_e[:, :, :], wide(num), ALU.is_equal))

            first_largest(logits[:, :, :], top[:, 0, :], top[:, 4, :], oh[0][:, :, :])
            link(dve.tensor_scalar(work[2][:, :, :], oh[0][:, :, :], -2.0, 1.0, ALU.mult, ALU.add))
            link(dve.scalar_tensor_tensor(work[3][:, :, :], work[2][:, :, :], BIG, logits[:, :, :], ALU.mult, ALU.min))
            first_largest(work[3][:, :, :], top[:, 1, :], top[:, 5, :], oh[1][:, :, :])
            link(dve.tensor_tensor(top[:, 2, :], top[:, 1, :], top[:, 0, :], ALU.subtract))
            dve.tensor_tensor(both[:, :].rearrange("p (t e) -> p t e", e=E), oh[0][:, :, :], oh[1][:, :, :], ALU.add).then_inc(counts_in, 1)
            dve.sem_inc(exp_in, 1)
            dve.wait_ge(exp_out, 1)
            link(dve.tensor_scalar(top[:, 4, :], top[:, 3, :], 1.0, None, ALU.add))
            link(dve.reciprocal(top[:, 5, :], top[:, 4, :]))
            link(dve.tensor_scalar(gates[:, 0:T], top[:, 5, :], 0.5, None, ALU.mult))
            link(dve.tensor_tensor(gates[:, T:2 * T], gates[:, 0:T], top[:, 3, :], ALU.mult))
            dve.wait_ge(counts_out, 1)
            per, run, ahead = work[0], work[1], work[2]
            reset = work[3]

            def by_expert(t):
                return t[:, :, :].rearrange("p t e -> p (t e)").rearrange("p (e t) -> p e t", e=E)

            link(dve.tensor_copy(by_expert(per), pR[1][:, 0:T * E].rearrange("p (t e) -> p e t", e=E)))
            link(dve.memset(by_expert(reset), 1.0))
            link(dve.memset(by_expert(reset)[:, :, 0:1], 0.0))
            link(dve.tensor_tensor_scan(run[:, :, :].rearrange("p t e -> p (t e)"), reset[:, :, :].rearrange("p t e -> p (t e)"),
                                        per[:, :, :].rearrange("p t e -> p (t e)"), 0.0, ALU.mult, ALU.add))
            link(dve.tensor_tensor(ahead[:, :, :], run[:, :, :], per[:, :, :], ALU.subtract))
            link(dve.tensor_scalar(smalli[:, 0, :], by_expert(run)[:, :, T - 1:T].rearrange("p e a -> p (e a)"), float(P - 1), None, ALU.add))
            link(dve.tensor_scalar(smalli[:, 1, :], smalli[:, 0, :], P.bit_length() - 1, None, ALU.logical_shift_right))
            link(dve.tensor_copy(small[:, 0, :], smalli[:, 1, :]))
            link(dve.memset(small[:, 1, :], 1.0))
            link(dve.tensor_tensor_scan(small[:, 2, :], small[:, 1, :], small[:, 0, :], 0.0, ALU.mult, ALU.add))
            link(dve.tensor_tensor(small[:, 3, :], small[:, 2, :], small[:, 0, :], ALU.subtract))
            link(dve.tensor_scalar(small[:, 4, :], small[:, 3, :], float(P), None, ALU.mult))
            link(dve.tensor_tensor(by_expert(run), by_expert(ahead),
                                   small[:, 4, :].rearrange("p (e a) -> p e a", a=1).to_broadcast([P, E, T]), ALU.add))
            slot_all = work[4]
            link(dve.tensor_tensor(slot_all[:, :, :], pR[0][:, 0:T * E].rearrange("p (t e) -> p t e", e=E),
                                   by_expert(run).rearrange("p e t -> p t e"), ALU.add))
            for k in range(TOP):
                link(dve.tensor_tensor(work[5][:, :, :], slot_all[:, :, :], oh[k][:, :, :], ALU.mult))
                link(dve.tensor_reduce(slotf[:, k * T:(k + 1) * T], work[5][:, :, :], AX.X, ALU.add))
            link(dve.tensor_copy(slots[:, :], slotf[:, :]))
            link(dve.tensor_scalar(parts_i[:, 0, :], slots[:, :], P - 1, None, ALU.bitwise_and))
            link(dve.tensor_scalar(parts_i[:, 1, :], slots[:, :], P.bit_length() - 1, None, ALU.logical_shift_right))
            link(dve.tensor_copy(parts_b[:, :, :], parts_i[:, :, :]))
            link(dve.tensor_copy(iota_bf[:, :], iota_col[:, :]))
            upto = small[:, 2, :].rearrange("p (a e) -> p a e", a=1).to_broadcast([P, NT, E])
            link(dve.tensor_tensor(iota_j[:, :, :], iota_j[:, :, :], upto, ALU.is_ge))
            link(dve.tensor_reduce(expert_f[:, :], iota_j[:, :, :], AX.X, ALU.add))
            link(dve.tensor_scalar(expert_i[:, :], expert_f[:, :], float(E - 1), float(WCOLS), ALU.min, ALU.mult))
            def across(ap, n):
                return ap.rearrange("p (a q) -> p a q", a=1).to_broadcast([P, PC, n])

            def along(ap, n):
                return ap.rearrange("p (c a) -> p c a", a=1).to_broadcast([P, PC, n])

            for piece in range(C // PC):
                at, u = slice(piece * PC, (piece + 1) * PC), piece % 2
                if piece >= 2:
                    dve.wait_ge(oh_used.sem, oh_used.done(piece - 2))
                link(dve.tensor_tensor(ohhi[:, u, :, :], across(iota_bf[:, 0:NT], NT), along(parts_b[:, 1, at], NT), ALU.is_equal))
                dve.tensor_tensor(ohlo[:, u, :, :], across(iota_bf[:, :], P), along(parts_b[:, 0, at], P), ALU.is_equal)
                dve.tensor_scalar(ohhi_p[:, u, :, :], ohhi[:, u, :, :], c["part"][:, 0:1], None, ALU.mult)
                dve.tensor_tensor(ohhi_c[:, u, :, :], ohhi[:, u, :, :], along(colnum[:, at], NT), ALU.mult).then_inc(oh_built.sem, 1)
            dve.wait_ge(oh_used.sem, oh_used.done(C // PC - 1))
            link(dve.tensor_copy(inv2[0:NT, :], pT[1][0:NT, 0:P]))
            dve.scalar_tensor_tensor(inv[0:NT, :], inv2[0:NT, :], float(P), pT[0][0:NT, 0:P], ALU.mult, ALU.add).then_inc(inv_ready, 1)
            dve.wait_ge(invT_ready, 1)
            link(dve.tensor_copy(row_f[:, 0, :], pY[0][:, 0:NT]))
            link(dve.scalar_tensor_tensor(row_f[:, 1, :], row_f[:, 0, :], 0.0, spare[:, :], ALU.is_equal, ALU.mult))
            link(dve.tensor_tensor(row_of[:, :], row_f[:, 0, :], row_f[:, 1, :], ALU.add))
            link(dve.tensor_scalar(row_f[:, 1, :], row_f[:, 0, :], float(TOK - P), None, ALU.add))
            link(dve.tensor_copy(row_t[:, :], row_f[:, 1, :]))
            dve.tensor_scalar(token_of[:, :], row_t[:, :], TOK - 1, None, ALU.bitwise_and).then_inc(routed, 1)

            def split_x(t, u):
                dve.wait_ge(g_T.sem, g_T.done(t))
                dve.wait_ge(h_ready.sem, h_ready.done(t - 2))
                src = pT[u][:, 0:D].rearrange("p (k q) -> p k q", k=KD)
                dve.tensor_copy(xh[:, u, :, :], src).then_inc(g_hi.sem, 1)
                dve.wait_ge(g_hi.sem, g_hi.done(t))
                dve.tensor_tensor(xl[:, u, :, :], src, xh[:, u, :, :].bitcast(F32), ALU.subtract).then_inc(g_split.sem, 1)

            def split_h(t, u):
                dve.wait_ge(sq_done.sem, sq_done.done(t))
                dve.wait_ge(y_ready.sem, y_ready.done(t - 2))
                dve.tensor_copy(h2h[:, u, :, :], h2[:, u, :, :]).then_inc(h2_hi.sem, 1)
                dve.wait_ge(h2_hi.sem, h2_hi.done(t))
                dve.tensor_tensor(h2l[:, u, :, :], h2[:, u, :, :], h2h[:, u, :, :].bitcast(F32), ALU.subtract).then_inc(h2_split.sem, 1)

            def copy_y(t, u, n):
                dve.wait_ge(y_ready.sem, y_ready.done(t))
                if n is not None:
                    dve.wait_ge(scattered[u].sem, scattered[u].done(n - 1))
                dve.tensor_copy(y[:, u, :], pY[u][:, 0:D]).then_inc(y_copied.sem, 1)

            split_x(0, 0)
            split_x(1, 1)
            split_x(2, 0)
            split_h(0, 0)
            for t in (1, 2):
                split_x(t + 2, t % 2)
                split_h(t, t % 2)
                copy_y(t - 1, (t - 1) % 2, None)
            with dve.Fori(1, NT // 2 - 2) as j:
                for u in range(2):
                    v = 1 - u
                    split_x(2 * j + (3 + u), v)
                    split_h(2 * j + (1 + u), v)
                    copy_y(2 * j + u, u, j)
            split_x(NT - 1, 1)
            split_h(NT - 3, 1)
            copy_y(NT - 4, 0, NT // 2 - 2)
            split_h(NT - 2, 0)
            copy_y(NT - 3, 1, NT // 2 - 2)
            split_h(NT - 1, 1)
            copy_y(NT - 2, 0, NT // 2 - 1)
            copy_y(NT - 1, 1, NT // 2 - 1)

            if out is not None:
                for s in (e_first, e_done):
                    s.open(dve)
                with dve.Fori(0, T // EB) as j:
                    for k in range(TOP):
                        for u in range(EB):
                            i = EB * j + u
                            if k == 0:
                                dve.wait_ge(e_loaded[u].sem, e_loaded[u].done(j))
                            else:
                                dve.wait_ge(e_first.sem, e_first.done(i))
                            dve.scalar_tensor_tensor(ea[:, u, 0, :], ea[:, u, 1 + k, :], gates[:, bass.ds(i + k * T, 1)], ea[:, u, 0, :],
                                                     ALU.mult, ALU.add).then_inc((e_first, e_done)[k].sem, 1)


def make_keep(nc, ctx, tokens):
    def sb(name, shape, dt):
        return ctx.enter_context(nc.sbuf_tensor(name, shape, dt))
    return {
        "gathers": Gathers(nc, ctx, "gather"),
        "scatters": Gathers(nc, ctx, "scatter"),
        "w1h": sb("w1h", [P, E * WCOLS], F32R),
        "w2h": sb("w2h", [P, E * WCOLS], F32R),
        "gates": sb("gates", [P, TOP * tokens // P], F32),
    }

DIN = 512
KI = DIN // P
NS = 64
H = 8
HD = DIN // H
CONV = 4
NB = (DIN + 2 * NS) // P
GC = 4
GT = GC * P
ATANH = [1.0 / n for n in (15, 13, 11, 9, 7, 5, 3)]


def mamba_block(nc, c, keep, x, ys_d, w_in, conv_w, conv_b, dt_bias, a_log, d_skip, norm_w, w_out, x2, batches):
    TOK = x.shape[0]
    T = TOK // P
    NG = TOK // GT
    PER = NG // batches
    CR = 2 * GC
    with ExitStack() as ctx:
        def sb(name, shape, dt=F32):
            return ctx.enter_context(nc.sbuf_tensor(name, shape, dt))

        sem = Sems(nc, ctx)

        def step(name, unit=1):
            return Step(sem("m_" + name), unit, CR)

        ident, tri = c["ident"], c["incl_tri"]
        gates = keep["gates"]
        NIN = w_in.shape[1]
        wih, wil = sb("wih", [P, KD, NIN], F32R), sb("wil", [P, KD, NIN], F32R)
        woh, wol = sb("woh", [P, KI, D], F32R), sb("wol", [P, KI, D], F32R)
        cw, cb, nw = sb("cw", [P, NB, CONV]), sb("cb", [P, NB]), sb("nw", [P, KI])
        cwh, cbh = sb("cwh", [P, NB, CONV]), sb("cbh", [P, NB])
        heads = sb("heads", [P, 3, H])
        negA = sb("negA", [P, GC, H])
        diag_d = sb("diag_d", [P, KI, P])
        flags = sb("flags", [P, NG + 1])
        ident_bf, tri_bf = sb("ident_bf", [P, P], BF16), sb("tri_bf", [P, P], BF16)
        future = sb("future", [P, GC, P], BF16)
        xr = sb("xr", [P, 2 * GC, D])
        yg = sb("m_yg", [P, 2, TOP, D])
        st, mv, ve, rstd = sb("m_st", [P, 6]), sb("m_mv", [P, 2]), sb("m_ve", [P, 1]), sb("m_rstd", [P, 1])
        xn = sb("m_xn", [P, D])
        xTh, xTl = sb("xTh", [P, KD, GT], F32R), sb("xTl", [P, KD, GT], F32R)
        tz = sb("tz", [P, DIN])
        sz = sb("sz", [P, GC, DIN])
        NR = 14
        dts = sb("dts", [P, 2, NR, GC * H])
        al = sb("al", [P, 2, 3, GC * H], BF16)
        raw = sb("raw", [P, NB, CONV - 1 + GT])
        acc = sb("acc", [P, 2, NB, GT])
        tb = sb("tb", [P, 2, GT])
        CT = sb("CT", [NS, 2, GT])
        S, S1 = sb("S", [NS, DIN]), sb("S1", [NS, DIN])
        xt, xdt, xw = (sb(n, [P, DIN]) for n in ("xt", "xdt", "xw"))
        Bt = sb("Bt", [P, NS])
        ex, M = sb("ex", [P, H, P]), sb("M", [P, H, P])
        t1, t2, yv, sq = (sb(n, [P, DIN]) for n in ("t1", "t2", "yv", "sq"))
        ss, vr, rs = sb("ss", [P, 1]), sb("vr", [P, 1]), sb("rs", [P, 1])
        yTh, yTl = sb("yTh", [P, KI, P], F32R), sb("yTl", [P, KI, P], F32R)
        xo = sb("xo", [P, 2, D])
        wst = acc[:, :, :, :].rearrange("p q b t -> p (q b t)")[:, 0:KD * NIN].rearrange("p (k n) -> p k n", k=KD)
        wost = ex[:, :, :].rearrange("p h t -> p (h t)")[:, 0:KI * D].rearrange("p (k n) -> p k n", k=KI)
        DTR, DPOS, DABS, DU, DS, DS2, DQ, DT, DA, NCUM, ECUM, DEC, DECDT, ETOT = range(NR)

        pX, pYT, small, pE, pY, pS, pZ, pO = (ctx.enter_context(nc.psum_tensor(f"bank{n}", [P, 512], F32)) for n in range(8))
        pG, pBt = small[:, 0:P], small[:, P:P + NS]
        pCum, pTot = small[:, 256:256 + GC * H], small[:, 320:320 + GC * H]
        pXN, pDt = pO[:, D:2 * D], pO[:, D:D + H]
        pP = [pZ, pO]

        loads, consts, d_prep, a_prep, prep = (sem(n) for n in ("m_loads", "m_consts", "d_prep", "a_prep", "m_prep"))
        go, soft_chain = sem("m_go"), sem("soft_chain")
        x_loaded = [step(f"x_loaded{n}", 16) for n in range(2 * GC)]
        y_loaded = [Step(sem(f"y_loaded{u}"), 16 * TOP) for u in range(2)]
        o_stored = [step(f"o_stored{u}", 16) for u in range(2)]
        add1, add2, stats, aggr, var_done, pow_done, norm_done, xT_ready, xT_hi, xT_lo, z_ready, tz_done, sz_done, dt_ready, dt_added = (
            step(n) for n in ("add1", "add2", "stats", "aggr", "var", "pow", "norm", "xT", "xT_hi", "xT_lo", "z", "tz", "sz", "dt", "dt_added"))
        soft, exp_u, a_done, cum_ready, cum_copied, exps, dec_in, dec_out, decdt, halo, s_sum = (
            step(n) for n in ("soft", "exp_u", "a", "cum", "cum_copied", "exps", "dec_in", "dec_out", "decdt", "halo", "s_sum"))
        p_ready, raw_done, tap0, tap_chain, taps, tb_done, xc_done = (step(n) for n in ("p", "raw", "tap0", "tap_chain", "taps", "tb", "xc"))
        sm_ready, bt_done, turned, xt_done, e0_ready, ex0_done, e1_ready, ex_done, xdt_done, M_done, xw_done = (
            step(n) for n in ("sm", "bt", "turned", "xt", "e0", "ex0", "e1", "ex", "xdt", "M", "xw"))
        i_ready, y_ready, s_ready, s1_done, S_done, t1_done, t2_done, yv_done, sq_done, rs_in, rs_done = (
            step(n) for n in ("i", "y", "s", "s1", "S", "t1", "t2", "yv", "sq", "rs_in", "rs"))
        yT_ready, yT_hi, yT_lo, o_ready, xo_done = (step(n) for n in ("yT", "yT_hi", "yT_lo", "o", "xo"))

        def row(g, n, k=0, chunks=GC):
            return dts[:, g.q, n, k * H:(k + chunks) * H]

        def per_head(ap, width, parts=P):
            return ap.rearrange("p (h a) -> p h a", a=1).to_broadcast([parts, ap.shape[1], width])

        def by_head(ap, heads=H):
            return ap.rearrange("p (h d) -> p h d", h=heads)

        class At:

            def __init__(self, j, q):
                self.j, self.q, self.group = j, q, 2 * j + q

            def chunk(self, k):
                return self.j * (2 * GC) + (self.q * GC + k)

            def nth(self, k):
                return self.j * GC + (self.q * (GC // 2) + k // 2)

            def block(self, b):
                return self.j * (2 * NB) + (self.q * NB + b)

            def tbuf(self, b):
                return (self.q * NB + b) % 2

        LAST = NG // 2 - 1

        def run(eng, front, convolve, slot, finish):
            for k in range(GC):
                front(At(0, 0), k)
            convolve(At(0, 0), None)
            with eng.Fori(0, LAST) as j:
                for g, following in ((At(j, 0), At(j, 1)), (At(j, 1), At(j + 1, 0))):
                    for k in range(GC):
                        slot(g, k, following)
                    convolve(following, g)
            g, following = At(LAST, 0), At(LAST, 1)
            for k in range(GC):
                slot(g, k, following)
            convolve(following, g)
            for k in range(GC):
                slot(following, k, None)
            finish(following)

        ctx.callback(sem.clear)
        block = ctx.enter_context(nc.Block())

        @block.sync
        def _(sp):
            sp.dma_start(wst[:, :, :], w_in.rearrange("(k p) n -> p k n", p=P)).then_inc(loads, 16)
            sp.dma_start(wost[:, :, :], w_out.rearrange("(k p) n -> p k n", p=P)).then_inc(loads, 16)
            sp.dma_start(cw[:, :, :], conv_w.rearrange("(k p) n -> p k n", p=P)).then_inc(loads, 16)
            sp.dma_start(cb[:, :], conv_b.rearrange("(k p) -> p k", p=P), allow_slow_non_contiguous=True).then_inc(loads, 16)
            sp.dma_start(nw[:, :], norm_w.rearrange("(k p) -> p k", p=P), allow_slow_non_contiguous=True).then_inc(loads, 16)
            for n, v in enumerate((dt_bias, a_log, d_skip)):
                sp.dma_start(heads[:, n, :], v.rearrange("(a h) -> a h", a=1).to_broadcast([P, H])).then_inc(loads, 16)
            for s in (*x_loaded, *y_loaded, *o_stored):
                s.open(sp)

            def load(g, k):
                n, u = (g.q * GC + k) % (2 * GC), k % 2
                sp.wait_ge(xo_done.sem, xo_done.done(g.chunk(k - 2 * GC)))
                sp.dma_start(xr[:, n, :], x[bass.ds(g.chunk(k) * P, P), :]).then_inc(x_loaded[n].sem, 16)
                sp.wait_ge(add2.sem, add2.done(g.chunk(k - 2)))
                for r in range(TOP):
                    sp.dma_start(yg[:, u, r, :], ys_d[bass.ds(g.chunk(k) * P + (1 + r * T) * P, P), :]).then_inc(y_loaded[u].sem, 16)

            def store(g, k):
                sp.wait_ge(xo_done.sem, xo_done.done(g.chunk(k)))
                sp.dma_start(x2[bass.ds(g.chunk(k) * P, P), :], xo[:, k % 2, :]).then_inc(o_stored[k % 2].sem, 16)

            def front(g, k):
                if k == 0:
                    load(g, 0)
                load(g, k + 1)

            def slot(g, k, following):
                if following is not None and not (isinstance(following.j, int) and k == GC - 1):
                    load(following, k + 1)
                if k > 0:
                    store(g, k - 1)

            def convolve(g, before):
                if before is not None:
                    store(before, GC - 1)

            run(sp, front, convolve, slot, lambda g: store(g, GC - 1))
            for u in range(2):
                sp.wait_ge(o_stored[u].sem, o_stored[u].done(T // 2 - 1))

        @block.gpsimd
        def _(pool):
            chain = Chain(pool, consts)
            pool.memset(flags[:, :], 1.0)
            pool.memset(ident_bf[:, :], 0.0)
            pool.memset(future[:, :, :], 0.0)
            pool.memset(S[:, :], 0.0)
            chain.link(pool.memset(raw[:, :, 0:CONV - 1], 0.0))
            for b in range(batches):
                pool.memset(flags[:, b * PER:b * PER + 1], 0.0)
            chain.link(pool.affine_select(out=ident_bf[:, :], in_=ident_bf[:, :], compare_op=ALU.not_equal, fill=1.0,
                                          base=0, pattern=[[-1, P]], channel_multiplier=1))
            chain.link(pool.affine_select(out=future[:, :, :], in_=future[:, :, :], compare_op=ALU.is_ge, fill=-1e30,
                                          base=0, pattern=[[0, GC], [1, P]], channel_multiplier=-1))
            for s in (pow_done, xdt_done, xw_done, s1_done, yv_done, rs_done):
                s.open(pool)

            def front(g, k):
                i = g.chunk(k)
                pool.wait_ge(var_done.sem, var_done.done(i))
                pool.tensor_tensor(rstd[:, :], ve[:, :], c["neghalf"][:, 0:1], ALU.pow).then_inc(pow_done.sem, 1)

            def scale_x(g, k):
                i = g.chunk(k)
                pool.wait_ge(xt_done.sem, xt_done.done(i))
                pool.wait_ge(s_ready.sem, s_ready.done(i - 1))
                pool.tensor_tensor(by_head(xdt[:, :]), by_head(xt[:, :]), per_head(row(g, DT, k, 1), HD), ALU.mult).then_inc(xdt_done.sem, 1)
                pool.tensor_tensor(by_head(xw[:, :]), by_head(xt[:, :]), per_head(row(g, DECDT, k, 1), HD), ALU.mult).then_inc(xw_done.sem, 1)

            def slot(g, k, following):
                i = g.chunk(k)
                pool.wait_ge(S_done.sem, S_done.done(i - 1))
                pool.tensor_tensor(by_head(S1[:, :]), by_head(S[:, :]), per_head(dts[0:NS, g.q, ETOT, k * H:(k + 1) * H], HD, NS), ALU.mult).then_inc(s1_done.sem, 1)
                if following is not None:
                    front(following, k)
                pool.wait_ge(sz_done.sem, sz_done.done(i))
                pool.wait_ge(t2_done.sem, t2_done.done(i))
                pool.tensor_tensor(yv[:, :], t2[:, :], sz[:, k, :], ALU.mult).then_inc(yv_done.sem, 1)
                if k + 1 < GC:
                    scale_x(g, k + 1)
                pool.wait_ge(rs_in.sem, rs_in.done(i))
                pool.tensor_tensor(rs[:, :], vr[:, :], c["neghalf"][:, 0:1], ALU.pow).then_inc(rs_done.sem, 1)

            def convolve(g, before):
                pool.wait_ge(decdt.sem, decdt.done(g.group))
                scale_x(g, 0)

            run(pool, front, convolve, slot, lambda g: None)

        @block.scalar
        def _(act):
            for s in (xT_hi, tz_done, exp_u, exps, dec_out, raw_done, tap0, tb_done, xt_done, bt_done, ex0_done, ex_done, sq_done, yT_hi):
                s.open(act)
            act.wait_ge(loads, 8 * 16)
            act.wait_ge(d_prep, 1)
            act.activation(heads[:, 1, :], heads[:, 1, :], ACT.Exp).then_inc(a_prep, 1)
            act.activation(wih[:, :, :], wst[:, :, :], ACT.Copy)
            act.activation(woh[:, :, :], wost[:, :, :], ACT.Copy).then_inc(a_prep, 1)

            def turn_x(g, k):
                act.wait_ge(xT_ready.sem, xT_ready.done(g.chunk(k)))
                act.activation(xTh[:, :, k * P:(k + 1) * P], by_head(pXN, KD), ACT.Copy).then_inc(xT_hi.sem, 1)

            def tanh_z(g, k):
                act.wait_ge(z_ready.sem, z_ready.done(g.chunk(k)))
                act.activation(tz[:, :], pZ[:, :], ACT.Tanh).then_inc(tz_done.sem, 1)

            def front(g, k):
                turn_x(g, k)
                tanh_z(g, k)

            def tanh(g, b):
                B = g.block(b)
                act.wait_ge(taps.sem, taps.done(B))
                act.wait_ge(xc_done.sem, xc_done.done(B - 2))
                act.activation(tb[:, g.tbuf(b), :], acc[:, g.q, b, :], ACT.Tanh).then_inc(tb_done.sem, 1)

            def copies(g, k):
                i = g.chunk(k)
                act.wait_ge(sm_ready.sem, sm_ready.done(i))
                act.activation(Bt[:, :], pBt, ACT.Copy).then_inc(bt_done.sem, 1)
                act.wait_ge(turned.sem, turned.done(i))
                act.activation(xt[:, :], pX[:, :], ACT.Copy).then_inc(xt_done.sem, 1)

            def decay(g, k, half):
                i = g.chunk(k)
                ready, done = ((e0_ready, ex0_done), (e1_ready, ex_done))[half]
                act.wait_ge(ready.sem, ready.done(i))
                for n in range(GC):
                    h = half * GC + n
                    at = k * H + h
                    last = act.activation(ex[:, h, :], pE[:, n * P:(n + 1) * P], ACT.Exp, bias=dts[:, g.q, NCUM, at:at + 1])
                last.then_inc(done.sem, 1)

            def convolve(g, before):
                G, B0 = g.group, g.block(0)
                act.wait_ge(soft.sem, soft.done(G))
                act.activation(row(g, DU), row(g, DABS), ACT.Exp, scale=-1.0).then_inc(exp_u.sem, 1)
                act.wait_ge(halo.sem, halo.done(G - 1))
                for b in range(NB):
                    B = B0 + b
                    act.wait_ge(p_ready.sem, p_ready.done(B))
                    act.activation(raw[:, b, CONV - 1:], pP[b % 2][:, :], ACT.Copy).then_inc(raw_done.sem, 1)
                    act.wait_ge(raw_done.sem, raw_done.done(B))
                    act.activation(acc[:, g.q, b, :], raw[:, b, 0:GT], ACT.Identity, bias=cbh[:, b:b + 1], scale=cwh[:, b, 0:1]).then_inc(tap0.sem, 1)
                    if b > 0:
                        tanh(g, b - 1)
                    if b == 3:
                        act.wait_ge(cum_ready.sem, cum_ready.done(G))
                        act.activation(row(g, ECUM), pCum, ACT.Exp)
                        act.activation(row(g, ETOT), pTot, ACT.Exp).then_inc(exps.sem, 1)
                    if b == 4:
                        act.wait_ge(dec_in.sem, dec_in.done(G))
                        act.activation(row(g, DEC), row(g, DEC), ACT.Exp).then_inc(dec_out.sem, 1)
                tanh(g, NB - 1)
                copies(g, 0)
                decay(g, 0, 0)
                decay(g, 0, 1)

            def slot(g, k, following):
                i = g.chunk(k)
                if k + 1 < GC:
                    copies(g, k + 1)
                    decay(g, k + 1, 0)
                if following is not None:
                    turn_x(following, k)
                act.wait_ge(yv_done.sem, yv_done.done(i))
                act.activation(sq[:, :], yv[:, :], ACT.Square, accum_out=ss[:, :]).then_inc(sq_done.sem, 1)
                act.wait_ge(yT_ready.sem, yT_ready.done(i))
                act.activation(yTh[:, :, :], by_head(pYT[:, :], KI), ACT.Copy).then_inc(yT_hi.sem, 1)
                if k + 1 < GC:
                    decay(g, k + 1, 1)
                if following is not None:
                    tanh_z(following, k)

            run(act, front, convolve, slot, lambda g: None)

        @block.tensor
        def _(pe):
            for s in (xT_ready, z_ready, dt_ready, cum_ready, p_ready, turned, sm_ready, e0_ready, e1_ready, i_ready, y_ready, s_ready, yT_ready, o_ready):
                s.open(pe)
            pe.wait_ge(consts, 3)
            pe.wait_ge(d_prep, 2)

            def product(out, parts):
                for m, (a, b) in enumerate(parts):
                    last = pe.matmul(out, a, b, start=(m == 0), stop=(m == len(parts) - 1))
                return last

            def turn_x(g, k):
                pe.wait_ge(norm_done.sem, norm_done.done(g.chunk(k)))
                for n in range(KD):
                    last = pe.transpose(pXN[:, n * P:(n + 1) * P], xn[:, n * P:(n + 1) * P], ident[:, :])
                last.then_inc(xT_ready.sem, 1)

            def project(g, k):
                i = g.chunk(k)
                pe.wait_ge(xT_lo.sem, xT_lo.done(i))
                tok = slice(k * P, (k + 1) * P)
                turns = ((xTh, wih), (xTh, wil), (xTl, wih))
                product(pDt, [(a[:, n, tok], w[:, n, NIN - H:NIN]) for a, w in turns for n in range(KD)]).then_inc(dt_ready.sem, 1)
                pe.wait_ge(sz_done.sem, sz_done.done(i - 1))
                product(pZ[:, :], [(a[:, n, tok], w[:, n, 0:DIN]) for a, w in turns for n in range(KD)]).then_inc(z_ready.sem, 1)

            def front(g, k):
                turn_x(g, k)
                project(g, k)

            def out_product(g, k):
                pe.wait_ge(yT_lo.sem, yT_lo.done(g.chunk(k)))
                product(pO[:, 0:D], [(a[:, n, :], w[:, n, :]) for a, w in ((yTh, woh), (yTh, wol), (yTl, woh)) for n in range(KI)]).then_inc(o_ready.sem, 1)

            def prepare(g, k):
                tok = slice(k * P, (k + 1) * P)
                pe.matmul(pG, acc[0:NS, g.q, KI, tok], CT[:, g.q, tok], start=True, stop=True)
                pe.transpose(pBt, acc[0:NS, g.q, KI, tok], ident[0:NS, 0:NS]).then_inc(sm_ready.sem, 1)
                for n in range(KI):
                    last = pe.transpose(pX[:, n * P:(n + 1) * P], acc[:, g.q, n, tok], ident[:, :])
                last.then_inc(turned.sem, 1)

            def sums(g, k, half):
                i = g.chunk(k)
                if half == 1:
                    pe.wait_ge(ex0_done.sem, ex0_done.done(i))
                for n in range(GC):
                    at = k * H + half * GC + n
                    for part in range(3):
                        pe.matmul(pE[:, n * P:(n + 1) * P], al[:, g.q, part, at:at + 1].to_broadcast([P, P]), tri_bf[:, :],
                                  start=(n == 0 and part == 0), stop=False, skip_group_check=True)
                pe.matmul(pE[:, :], ident_bf[:, :], future[:, :, :].rearrange("p h t -> p (h t)"),
                          start=False, stop=True, skip_group_check=True).then_inc((e0_ready, e1_ready)[half].sem, 1)

            def convolve(g, before):
                G, B0 = g.group, g.block(0)
                pe.wait_ge(dt_added.sem, dt_added.done(g.chunk(GC - 1)))
                if before is not None:
                    out_product(before, GC - 1)
                for b in range(NB):
                    B = B0 + b
                    if b == 0:
                        pe.wait_ge(sz_done.sem, sz_done.done(g.chunk(GC - 1)))
                    elif b == 1:
                        if before is not None:
                            pe.wait_ge(xo_done.sem, xo_done.done(before.chunk(GC - 1)))
                    else:
                        pe.wait_ge(raw_done.sem, raw_done.done(B - 2))
                    ch = slice(DIN + b * P, DIN + (b + 1) * P)
                    parts = [(w[:, n, ch], a[:, n, :]) for w, a in ((wih, xTh), (wih, xTl), (wil, xTh)) for n in range(KD)]
                    product(pP[b % 2][:, :], parts).then_inc(p_ready.sem, 1)
                    if b == 3:
                        pe.wait_ge(a_done.sem, a_done.done(G))
                        pe.matmul(pCum, tri[:, :], row(g, DA), start=True, stop=True)
                        pe.matmul(pTot, c["ones_f"][:, :], row(g, DA), start=True, stop=True).then_inc(cum_ready.sem, 1)
                pe.wait_ge(xc_done.sem, xc_done.done(B0 + (NB - 1)))
                prepare(g, 0)
                sums(g, 0, 0)
                sums(g, 0, 1)

            def slot(g, k, following):
                i = g.chunk(k)
                tok = slice(k * P, (k + 1) * P)
                pe.wait_ge(S_done.sem, S_done.done(i - 1))
                pe.matmul(pS[:, :], CT[:, g.q, tok], S[:, :], start=True, stop=True).then_inc(i_ready.sem, 1)
                for n in range(KI):
                    pe.matmul(pY[:, n * P:(n + 1) * P], acc[:, g.q, n, tok], diag_d[:, n, :], start=(n == 0), stop=False, skip_group_check=True)
                if k > 0:
                    if following is not None:
                        pe.wait_ge(dt_added.sem, dt_added.done(following.chunk(k - 1)))
                    out_product(g, k - 1)
                pe.wait_ge(xdt_done.sem, xdt_done.done(i))
                pe.wait_ge(M_done.sem, M_done.done(i))
                for h in range(H):
                    last = pe.matmul(pY[:, h * HD:(h + 1) * HD], M[:, h, :], xdt[:, h * HD:(h + 1) * HD], start=False, stop=(h == H - 1), skip_group_check=True)
                last.then_inc(y_ready.sem, 1)
                pe.wait_ge(xw_done.sem, xw_done.done(i))
                pe.wait_ge(t1_done.sem, t1_done.done(i))
                pe.matmul(pS[0:NS, :], Bt[:, :], xw[:, :], start=True, stop=True).then_inc(s_ready.sem, 1)
                if k + 1 < GC:
                    prepare(g, k + 1)
                    sums(g, k + 1, 0)
                if following is not None:
                    turn_x(following, k)
                pe.wait_ge(yv_done.sem, yv_done.done(i))
                for n in range(KI):
                    last = pe.transpose(pYT[:, n * P:(n + 1) * P], yv[:, n * P:(n + 1) * P], ident[:, :])
                last.then_inc(yT_ready.sem, 1)
                if k + 1 < GC:
                    sums(g, k + 1, 1)
                if following is not None:
                    project(following, k)

            run(pe, front, convolve, slot, lambda g: out_product(g, GC - 1))

        @block.vector
        def _(dve):
            for s in (add1, add2, stats, aggr, var_done, norm_done, xT_lo, sz_done, dt_added, soft, a_done, cum_copied, decdt, dec_in, halo, tap_chain, s_sum,
                      taps, xc_done, M_done, S_done, t1_done, t2_done, rs_in, yT_lo, xo_done):
                s.open(dve)
            dve.wait_ge(loads, 8 * 16)
            dve.wait_ge(consts, 3)
            link = Chain(dve, prep).link
            link(dve.tensor_scalar(wst[:, :, 0:DIN], wst[:, :, 0:DIN], 0.5, None, ALU.mult))
            for n in range(KI):
                link(dve.tensor_scalar(wost[:, n, :], wost[:, n, :], nw[:, n:n + 1], None, ALU.mult))
            dve.sem_inc(d_prep, 1)
            link(dve.tensor_scalar(cwh[:, :, :], cw[:, :, :], 0.5, None, ALU.mult))
            link(dve.tensor_scalar(cbh[:, :], cb[:, :], 0.5, None, ALU.mult))
            link(dve.tensor_copy(tri_bf[:, :], tri[:, :]))
            for n in range(KI):
                per = H // KI
                link(dve.tensor_tensor(by_head(diag_d[:, n, :], per), by_head(ident[:, :], per), per_head(heads[:, 2, n * per:(n + 1) * per], HD), ALU.mult))
            dve.wait_ge(a_prep, 2)
            for k in range(GC):
                link(dve.tensor_scalar(negA[:, k, :], heads[:, 1, :], -1.0, None, ALU.mult))
            link(dve.tensor_tensor(wil[:, :, :], wst[:, :, :], wih[:, :, :].bitcast(F32), ALU.subtract))
            link(dve.tensor_tensor(wol[:, :, :], wost[:, :, :], woh[:, :, :].bitcast(F32), ALU.subtract))
            dve.sem_inc(d_prep, 1)

            def moments(g, k):
                i, n, u = g.chunk(k), g.q * GC + k, k % 2
                dve.wait_ge(x_loaded[n].sem, x_loaded[n].done(g.j))
                dve.wait_ge(y_loaded[u].sem, y_loaded[u].done(g.nth(k)))
                dve.scalar_tensor_tensor(xr[:, n, :], yg[:, u, 0, :], gates[:, bass.ds(i, 1)], xr[:, n, :], ALU.mult, ALU.add).then_inc(add1.sem, 1)
                dve.wait_ge(add1.sem, add1.done(i))
                dve.scalar_tensor_tensor(xr[:, n, :], yg[:, u, 1, :], gates[:, bass.ds(i + T, 1)], xr[:, n, :], ALU.mult, ALU.add).then_inc(add2.sem, 1)
                dve.wait_ge(add2.sem, add2.done(i))
                dve.bn_stats(st[:, :], xr[:, n, :]).then_inc(stats.sem, 1)
                dve.wait_ge(stats.sem, stats.done(i))
                dve.sem_inc(go, 1)
                dve.bn_aggr(mv[:, :], st[:, :]).then_inc(aggr.sem, 1)
                dve.wait_ge(aggr.sem, aggr.done(i))
                dve.tensor_scalar(ve[:, :], mv[:, 1:2], EPS, None, ALU.add).then_inc(var_done.sem, 1)

            def normalise(g, k):
                i, n = g.chunk(k), g.q * GC + k
                dve.wait_ge(pow_done.sem, pow_done.done(i))
                dve.tensor_scalar(xn[:, :], xr[:, n, :], mv[:, 0:1], rstd[:, 0:1], ALU.subtract, ALU.mult).then_inc(norm_done.sem, 1)

            def gate(g, k):
                i = g.chunk(k)
                dve.wait_ge(tz_done.sem, tz_done.done(i))
                dve.scalar_tensor_tensor(sz[:, k, :], tz[:, :], 1.0, pZ[:, :], ALU.add, ALU.mult).then_inc(sz_done.sem, 1)

            def split_x(g, k):
                i = g.chunk(k)
                dve.wait_ge(xT_hi.sem, xT_hi.done(i))
                dve.tensor_tensor(xTl[:, :, k * P:(k + 1) * P], by_head(pXN, KD), xTh[:, :, k * P:(k + 1) * P].bitcast(F32), ALU.subtract).then_inc(xT_lo.sem, 1)

            def add_bias(g, k):
                i = g.chunk(k)
                dve.wait_ge(dt_ready.sem, dt_ready.done(i))
                dve.tensor_tensor(row(g, DTR, k, 1), pDt, heads[:, 0, :], ALU.add).then_inc(dt_added.sem, 1)

            def front(g, k):
                moments(g, k)
                normalise(g, k)
                if k > 0:
                    gate(g, k - 1)
                split_x(g, k)
                add_bias(g, k)

            NCH = 1 + 5 + (len(ATANH) - 1) + 2 + 4

            def softplus(g):
                G, m = g.group, [0]

                def linked(ins):
                    m[0] += 1
                    ins.then_inc(soft_chain, 1)
                    dve.wait_ge(soft_chain, G * NCH + m[0])

                dve.wait_ge(dt_added.sem, dt_added.done(g.chunk(GC - 1)))
                linked(dve.tensor_scalar(row(g, DPOS), row(g, DTR), 0.0, None, ALU.max))
                dve.scalar_tensor_tensor(row(g, DABS), row(g, DPOS), 2.0, row(g, DTR), ALU.mult, ALU.subtract).then_inc(soft.sem, 1)
                gate(g, GC - 1)
                dve.wait_ge(exp_u.sem, exp_u.done(G))
                linked(dve.tensor_scalar(row(g, DS2), row(g, DU), 2.0, None, ALU.add))
                linked(dve.reciprocal(row(g, DQ), row(g, DS2)))
                linked(dve.tensor_tensor(row(g, DS), row(g, DU), row(g, DQ), ALU.mult))
                linked(dve.tensor_tensor(row(g, DS2), row(g, DS), row(g, DS), ALU.mult))
                linked(dve.tensor_scalar(row(g, DQ), row(g, DS2), ATANH[0], None, ALU.mult))
                for a in ATANH[1:]:
                    linked(dve.scalar_tensor_tensor(row(g, DQ), row(g, DQ), a, row(g, DS2), ALU.add, ALU.mult))
                linked(dve.scalar_tensor_tensor(row(g, DQ), row(g, DQ), 1.0, row(g, DS), ALU.add, ALU.mult))
                linked(dve.scalar_tensor_tensor(row(g, DT), row(g, DQ), 2.0, row(g, DPOS), ALU.mult, ALU.add))
                dve.tensor_tensor(row(g, DA), row(g, DT), negA[:, :, :].rearrange("p k h -> p (k h)"), ALU.mult).then_inc(a_done.sem, 1)
                dve.wait_ge(a_done.sem, a_done.done(G))
                linked(dve.tensor_copy(al[:, g.q, 0, :], row(g, DA)))
                linked(dve.tensor_tensor(row(g, DS), row(g, DA), al[:, g.q, 0, :], ALU.subtract))
                linked(dve.tensor_copy(al[:, g.q, 1, :], row(g, DS)))
                linked(dve.tensor_tensor(row(g, DS2), row(g, DS), al[:, g.q, 1, :], ALU.subtract))
                dve.tensor_copy(al[:, g.q, 2, :], row(g, DS2))
                assert m[0] == NCH

            def silu(g, b):
                a = acc[:, g.q, b, :]
                dve.wait_ge(tb_done.sem, tb_done.done(g.block(b)))
                if b < KI:
                    dve.scalar_tensor_tensor(a, tb[:, g.tbuf(b), :], 1.0, a, ALU.add, ALU.mult).then_inc(xc_done.sem, 1)
                else:
                    dve.scalar_tensor_tensor(CT[:, g.q, :], tb[NS:P, g.tbuf(b), :], 1.0, acc[NS:P, g.q, b, :], ALU.add, ALU.mult)
                    dve.scalar_tensor_tensor(acc[0:NS, g.q, b, :], tb[0:NS, g.tbuf(b), :], 1.0, acc[0:NS, g.q, b, :], ALU.add, ALU.mult).then_inc(xc_done.sem, 1)

            def convolve(g, before):
                G, B0 = g.group, g.block(0)
                if before is not None:
                    add_residual(before, GC - 1)
                softplus(g)
                for b in range(NB):
                    B = B0 + b
                    dve.wait_ge(tap0.sem, tap0.done(B))
                    for n in range(1, CONV):
                        if n > 1:
                            dve.wait_ge(tap_chain.sem, tap_chain.done(B * 2 + (n - 2)))
                        ins = dve.scalar_tensor_tensor(acc[:, g.q, b, :], raw[:, b, n:n + GT], cwh[:, b, n:n + 1], acc[:, g.q, b, :], ALU.mult, ALU.add)
                        ins.then_inc(taps.sem if n == CONV - 1 else tap_chain.sem, 1)
                    if b > 0:
                        silu(g, b - 1)
                    if b == 3:
                        dve.wait_ge(exps.sem, exps.done(G))
                        dve.tensor_scalar(row(g, NCUM), pCum, -1.0, None, ALU.mult).then_inc(cum_copied.sem, 1)
                        dve.wait_ge(cum_copied.sem, cum_copied.done(G))
                        dve.tensor_tensor(row(g, DEC), pTot, row(g, NCUM), ALU.add).then_inc(dec_in.sem, 1)
                    if b == 4:
                        dve.wait_ge(dec_out.sem, dec_out.done(G))
                        dve.tensor_tensor(row(g, DECDT), row(g, DEC), row(g, DT), ALU.mult).then_inc(decdt.sem, 1)
                dve.wait_ge(taps.sem, taps.done(B0 + (NB - 1)))
                dve.tensor_scalar(raw[:, :, 0:CONV - 1], raw[:, :, GT:GT + CONV - 1], flags[:, bass.ds(G + 1, 1)], None, ALU.mult).then_inc(halo.sem, 1)
                silu(g, NB - 1)

            def add_residual(g, k):
                i, n = g.chunk(k), g.q * GC + k
                dve.wait_ge(o_ready.sem, o_ready.done(i))
                dve.wait_ge(rs_done.sem, rs_done.done(i))
                dve.wait_ge(o_stored[k % 2].sem, o_stored[k % 2].done(g.nth(k) - 1))
                dve.scalar_tensor_tensor(xo[:, k % 2, :], pO[:, 0:D], rs[:, 0:1], xr[:, n, :], ALU.mult, ALU.add).then_inc(xo_done.sem, 1)

            def slot(g, k, following):
                i, G = g.chunk(k), g.group
                dve.wait_ge(ex_done.sem, ex_done.done(i))
                dve.tensor_tensor(M[:, :, :], ex[:, :, :], pG.rearrange("p (a t) -> p a t", a=1).to_broadcast([P, H, P]), ALU.mult).then_inc(M_done.sem, 1)
                dve.wait_ge(i_ready.sem, i_ready.done(i))
                dve.tensor_tensor(by_head(t1[:, :]), by_head(pS[:, :]), per_head(row(g, ECUM, k, 1), HD), ALU.mult).then_inc(t1_done.sem, 1)
                if k > 0:
                    add_residual(g, k - 1)
                if following is not None:
                    moments(following, k)
                dve.wait_ge(t1_done.sem, t1_done.done(i))
                dve.wait_ge(y_ready.sem, y_ready.done(i))
                dve.tensor_tensor(t2[:, :], t1[:, :], pY[:, :], ALU.add).then_inc(t2_done.sem, 1)
                dve.wait_ge(s1_done.sem, s1_done.done(i))
                dve.wait_ge(s_ready.sem, s_ready.done(i))
                if k == GC - 1:
                    dve.tensor_tensor(S[:, :], S1[:, :], pS[0:NS, :], ALU.add).then_inc(s_sum.sem, 1)
                    dve.wait_ge(s_sum.sem, s_sum.done(G))
                    dve.tensor_scalar(S[:, :], S[:, :], flags[0:NS, bass.ds(G + 1, 1)], None, ALU.mult).then_inc(S_done.sem, 1)
                else:
                    dve.tensor_tensor(S[:, :], S1[:, :], pS[0:NS, :], ALU.add).then_inc(S_done.sem, 1)
                if following is not None:
                    normalise(following, k)
                    if k > 0:
                        gate(following, k - 1)
                    split_x(following, k)
                dve.wait_ge(yT_hi.sem, yT_hi.done(i))
                dve.tensor_tensor(yTl[:, :, :], by_head(pYT[:, :], KI), yTh[:, :, :].bitcast(F32), ALU.subtract).then_inc(yT_lo.sem, 1)
                dve.wait_ge(sq_done.sem, sq_done.done(i))
                dve.tensor_scalar(vr[:, :], ss[:, :], 1.0 / DIN, EPS, ALU.mult, ALU.add).then_inc(rs_in.sem, 1)
                if following is not None:
                    add_bias(following, k)

            run(dve, front, convolve, slot, lambda g: add_residual(g, GC - 1))


def program(nc, x, w_in, conv_w, conv_b, dt_bias, a_log, d_skip, norm_w, w_out, router_w, w1, w2, out):
    with ExitStack() as ctx:
        batches, tokens = x.shape[0], x.shape[0] * x.shape[1]
        xf, of = x.rearrange("b t d -> (b t) d"), out.rearrange("b t d -> (b t) d")

        xn_d = nc.dram_tensor("xn_d", (tokens, D), F32, kind="Internal").ap()
        ys_d = nc.dram_tensor("ys_d", ((TOP * (tokens // P) + 2) * P, D), F32, kind="Internal").ap()
        x2_d = nc.dram_tensor("x2_d", (tokens, D), F32, kind="Internal").ap()
        lo_d = nc.dram_tensor("lo_d", (2, P, E * WCOLS), F32, kind="Internal").ap()
        c = make_constants(nc, ctx)
        keep = make_keep(nc, ctx, tokens)
        build_constants(nc, c)
        ffn_block(nc, c, keep, xf, router_w, w1, w2, xn_d, ys_d, lo_d, None, True)
        mamba_block(nc, c, keep, xf, ys_d, w_in, conv_w, conv_b, dt_bias, a_log, d_skip, norm_w, w_out, x2_d, batches)
        ffn_block(nc, c, keep, x2_d, router_w, w1, w2, xn_d, ys_d, lo_d, of, False)


_INS = ["L0_attn_x", "L0_attn_W_in", "L0_attn_conv_w", "L0_attn_conv_b", "L0_attn_dt_bias", "L0_attn_A_log", "L0_attn_D",
        "L0_attn_norm_weight", "L0_attn_W_out", "L0_ffn_router_w", "L0_ffn_w1", "L0_ffn_w2"]


def kernel(**inputs):
    import numpy as _np
    import concourse.bacc as _bacc
    from concourse import mybir as _mybir
    from concourse.bass_utils import run_bass_kernel_spmd as _run

    nc = _bacc.Bacc("TRN2", target_bir_lowering=False, num_devices=1)
    arrays, args = {}, []
    for name in _INS:
        a = _np.ascontiguousarray(inputs[name])
        arrays[f"in_{name}_dram"] = a
        args.append(nc.dram_tensor(f"in_{name}_dram", a.shape, _mybir.dt.from_np(a.dtype), kind="ExternalInput").ap())
    shape = inputs["L0_attn_x"].shape
    args.append(nc.dram_tensor("out_0_dram", shape, _mybir.dt.float32, kind="ExternalOutput").ap())
    program(nc, *args)
    r = _run(nc, [arrays], core_ids=[0])
    return r.results[0]["out_0_dram"]
```

```python
from contextlib import ExitStack

import concourse.bass as bass
from concourse import mybir

F32 = mybir.dt.float32
F32R = mybir.dt.float32r
BF16 = mybir.dt.bfloat16
I32 = mybir.dt.int32
U32 = mybir.dt.uint32
ALU = mybir.AluOpType
ACT = mybir.ActivationFunctionType
AX = mybir.AxisListType

P = 128
D = 256
KD = D // P
E = 8
HID = 512
KH = HID // P
TOP = 2
EPS = 1e-5
BIG = 3.0e38
WCOLS = KD * HID
AG = 4
EG = AG
NRAW = 4
NA = 4
PC = 8

CREDIT = 2


class Step:

    def __init__(self, sem, unit=1, credit=CREDIT):
        self.sem, self.unit, self.credit = sem, unit, credit

    def open(self, eng):
        eng.sem_inc(self.sem, self.credit * self.unit)

    def done(self, item):
        return (item + (1 + self.credit)) * self.unit


class Gathers:

    def __init__(self, nc, ctx, name):
        self.sems = [ctx.enter_context(nc.semaphore(f"{name}{u}")) for u in range(2)]
        self.before = 0

    def take(self, n):
        steps = [Step(s, 16, self.before) for s in self.sems]
        self.before += n
        return steps


class Chain:

    def __init__(self, eng, sem):
        self.eng, self.sem, self.n = eng, sem, 0

    def link(self, ins):
        self.n += 1
        ins.then_inc(self.sem, 1)
        self.eng.wait_ge(self.sem, self.n)


class Sems:

    def __init__(self, nc, ctx):
        self.nc, self.ctx, self.all = nc, ctx, []

    def __call__(self, name):
        self.all.append(self.ctx.enter_context(self.nc.semaphore(name)))
        return self.all[-1]

    def clear(self):
        with self.nc.Block() as block:
            @block.sync
            def _(sp):
                for s in self.all:
                    sp.sem_clear(s)


def make_constants(nc, ctx):
    def sb(name, shape, dt):
        return ctx.enter_context(nc.sbuf_tensor(name, shape, dt))
    return {
        "ident": sb("ident", [P, P], F32),
        "incl_tri": sb("incl_tri", [P, P], F32),
        "strict_tri": sb("strict_tri", [P, P], BF16),
        "ones_bf": sb("ones_bf", [P, P], BF16),
        "ones_f": sb("ones_f", [P, P], F32),
        "part": sb("part", [P, 1], F32),
        "neghalf": sb("neghalf", [P, 8], F32),
    }


def build_constants(nc, c):
    with ExitStack() as ctx:
        sems = Sems(nc, ctx)
        s_set = sems("s_const")
        ctx.callback(sems.clear)
        block = ctx.enter_context(nc.Block())

        @block.gpsimd
        def _(pool):
            chain = Chain(pool, s_set)
            pool.memset(c["ident"][:, :], 0.0)
            pool.memset(c["incl_tri"][:, :], 1.0)
            pool.memset(c["strict_tri"][:, :], 1.0)
            pool.memset(c["ones_bf"][:, :], 1.0)
            pool.memset(c["ones_f"][:, :], 1.0)
            pool.memset(c["neghalf"][:, :], -0.5)
            chain.link(pool.iota(c["part"][:, :], pattern=[[0, 1]], base=0, channel_multiplier=1,
                                 allow_small_or_imprecise_dtypes=True))
            for name, op, fill, sign in (("ident", ALU.not_equal, 1.0, -1), ("incl_tri", ALU.is_ge, 0.0, 1),
                                         ("strict_tri", ALU.is_gt, 0.0, 1)):
                chain.link(pool.affine_select(out=c[name][:, :], in_=c[name][:, :], compare_op=op, fill=fill,
                                              base=0, pattern=[[sign, P]], channel_multiplier=-sign))


def ffn_block(nc, c, keep, x, router_w, w1, w2, xn_d, ys_d, lo_d, out, first):
    TOK = x.shape[0]
    T = TOK // P
    NT = (TOP * TOK + E * (P - 1)) // P
    NT += NT % 2
    C = TOP * T
    with ExitStack() as ctx:
        def sb(name, shape, dt):
            return ctx.enter_context(nc.sbuf_tensor(name, shape, dt))

        def psum(name, dt=F32, n=512):
            return ctx.enter_context(nc.psum_tensor(name, [P, n], dt))

        sem = Sems(nc, ctx)

        def step(name, unit=1):
            return Step(sem(name), unit)

        tag = "1" if first else "2"
        ident = c["ident"]
        w1h, w2h, gates = keep["w1h"], keep["w2h"], keep["gates"]
        w1l = sb("w1l" + tag, [P, E * WCOLS], F32R)
        w2l = sb("w2l" + tag, [P, E * WCOLS], F32R)
        wst = sb("wst" + tag, [P, 2, WCOLS], F32) if first else None
        xs = sb("xs" + tag, [P, max(NA * AG, 2 * EG * TOP), D], F32)
        xa = xs[:, 0:NA * AG, :]
        xg, y = xs[:, 0:2, :], xs[:, 2:4, :]
        er = xs[:, 0:2 * EG * TOP, :].rearrange("p (h r n) d -> p h r n d", h=2, r=TOP)
        st = sb("st" + tag, [P, AG, 6], F32)
        mv = sb("mv" + tag, [P, 2 * AG, 2], F32)
        ve = sb("ve" + tag, [P, 2, AG], F32)
        rstd = sb("rstd" + tag, [P, 2, AG], F32)
        rw = sb("rw" + tag, [E, D], F32)
        rwT = sb("rwT" + tag, [P, KD, E], F32)
        logits = sb("logits" + tag, [P, T, E], F32)
        iota_e = sb("iota_e" + tag, [P, T, E], F32)
        iota_col = sb("iota_col" + tag, [P, P], F32)
        iota_bf = sb("iota_bf" + tag, [P, P], BF16)
        iota_j = sb("iota_j" + tag, [P, NT, E], F32)
        colnum = sb("colnum" + tag, [P, C], F32)
        slots = sb("slots" + tag, [P, C], U32)
        work_all = sb("work" + tag, [P, 6 * T * E], F32)
        work = [work_all[:, n * T * E:(n + 1) * T * E].rearrange("p (t e) -> p t e", e=E) for n in range(6)]
        xT = work_all[:, 0:4 * D].rearrange("p (m k q) -> p m k q", m=4, k=KD)
        oh = [sb(f"oh{n}_{tag}", [P, T, E], F32) for n in range(TOP)]
        top = sb("top" + tag, [P, 6, T], F32)
        both = sb("both" + tag, [P, T * E], BF16)
        small = sb("small" + tag, [P, 8, E], F32)
        smalli = sb("smalli" + tag, [P, 2, E], I32)
        slotf = sb("slotf" + tag, [P, C], F32)
        parts_i = sb("parts_i" + tag, [P, 2, C], U32)
        parts_b = sb("parts_b" + tag, [P, 2, C], BF16)
        expert_f = sb("expert_f" + tag, [P, NT], F32)
        expert_i = sb("expert_i" + tag, [P, NT], I32)
        ohhi, ohhi_c, ohhi_p = (sb(n + tag, [P, 2, PC, NT], BF16) for n in ("ohhi", "ohhi_c", "ohhi_p"))
        ohlo = sb("ohlo" + tag, [P, 2, PC, P], BF16)
        inv = sb("inv" + tag, [P, P], F32)
        inv2 = sb("inv2" + tag, [P, P], F32)
        row_f = sb("row_f" + tag, [P, 3, NT], F32)
        spare = sb("spare" + tag, [P, NT], F32)
        row_of = sb("row_of" + tag, [P, NT], U32)
        row_t = sb("row_t" + tag, [P, NT], U32)
        token_of = sb("token_of" + tag, [P, NT], U32)
        idx = sb("idx" + tag, [P, 2, 1], U32)
        ridx = sb("ridx" + tag, [P, 2, 1], U32)
        xh = sb("xh" + tag, [P, 2, KD, P], F32R)
        xl = sb("xl" + tag, [P, 2, KD, P], F32R)
        hs = sb("hs" + tag, [P, 4 * HID], F32)
        r = hs[:, 0:2 * HID].rearrange("p (u n) -> p u n", u=2)
        h2 = hs[:, 2 * HID:4 * HID].rearrange("p (u k q) -> p u k q", u=2, k=KH)
        ex = hs[:, 0:2 * EG * D].rearrange("p (h n d) -> p h n d", h=2, d=D)
        h2h = sb("h2h" + tag, [P, 2, KH, P], F32R)
        h2l = sb("h2l" + tag, [P, 2, KH, P], F32R)

        pT = [psum(f"pT{u}{tag}") for u in range(2)]
        pH = [psum(f"pH{u}{tag}") for u in range(2)]
        pR = [psum(f"pR{u}{tag}") for u in range(2)]
        pY = [psum(f"pY{u}{tag}") for u in range(2)]

        turned = [*pT, *pH]

        w_loaded = [sem(f"w_loaded{u}") for u in range(NRAW)]
        w_hi, w_lo = step("w_hi"), step("w_lo")
        w_spilt, rw_loaded = sem("w_spilt"), sem("rw_loaded")
        xa_loaded = [step(f"xa_loaded{h}", 16) for h in range(NA)]
        var_done, pow_done, mv_done = step("var_done"), step("pow_done"), step("mv_done")
        norm_done = Step(sem("norm_done"), credit=2 * AG)
        st_chain, aggr_go = step("st_chain"), sem("aggr_go")
        xn_stored = [step(f"xn_stored{h}", 16) for h in range(NA)]
        xT_ready, logit_copied = step("xT_ready"), step("logit_copied")
        xT_copied, logit_ready = (Step(sem(n), credit=4) for n in ("xT_copied", "logit_ready"))
        iotas, b_chain, exp_in, exp_out, counts_in, counts_out = (sem(n) for n in ("iotas", "b_chain", "exp_in", "exp_out", "counts_in", "counts_out"))
        rwT_ready = sem("rwT_ready")
        oh_hi, oh_lo, oh_part, oh_col, oh_used = (step(n) for n in ("oh_hi", "oh_lo", "oh_part", "oh_col", "oh_used"))
        experts_known = sem("experts_known")
        inv_ready, invT_ready, routed = sem("inv_ready"), sem("invT_ready"), sem("routed")
        idx_set, dma_go, gathered = step("idx_set"), sem("dma_go"), keep["gathers"].take(NT // 2)
        ridx_set, scattered = step("ridx_set"), keep["scatters"].take(NT // 2)
        g_T, g_hi, g_split, h_ready, relu_done, rT_ready, sq_done, h2_hi, h2_split, y_ready, y_copied = (
            step(n) for n in ("g_T", "g_hi", "g_split", "h_ready", "relu_done", "rT_ready", "sq_done", "h2_hi", "h2_split", "y_ready", "y_copied"))
        e_loaded = [step(f"e_loaded{u}", 16 * (1 + TOP)) for u in range(2)]
        e_stored = [step(f"e_stored{u}", 16) for u in range(2)]
        e_first, e_done = step("e_first"), Step(sem("e_done"), credit=2 * EG)

        def across(ap, n):
            return ap.rearrange("p (a q) -> p a q", a=1).to_broadcast([P, PC, n])

        def along(ap, n):
            return ap.rearrange("p (c a) -> p c a", a=1).to_broadcast([P, PC, n])

        def wsrc(n):
            return (w1 if n % 2 == 0 else w2)[n // 2].rearrange("(k p) n -> p k n", p=P)

        def whi(n):
            return (w1h if n % 2 == 0 else w2h)[:, (n // 2) * WCOLS:(n // 2 + 1) * WCOLS]

        def wraw(n):
            m = n % NRAW
            return wst[:, m, :] if m < 2 else hs[:, (m - 2) * WCOLS:(m - 1) * WCOLS]

        def wlo(n):
            return (w1l if n % 2 == 0 else w2l)[:, (n // 2) * WCOLS:(n // 2 + 1) * WCOLS]

        def tiles(rows, at):
            return rows[bass.ds(at, AG * P), :].rearrange("(n p) d -> p n d", p=P)

        NW = 2 * E

        def step_weights(s):
            return range(max(0, NW * s // (T // AG)), NW * (s + 1) // (T // AG))

        ctx.callback(sem.clear)
        block = ctx.enter_context(nc.Block())

        @block.sync
        def _(sp):
            sp.dma_start(rw[:, :], router_w).then_inc(rw_loaded, 16)
            for s in (*xa_loaded, *xn_stored):
                s.open(sp)

            def load(j, h, before=True):
                if before:
                    sp.wait_ge(xT_ready.sem, xT_ready.done((NA * j + (h - NA + 1)) * AG - 1))
                    sp.wait_ge(xn_stored[h].sem, xn_stored[h].done(j - 1))
                sp.dma_start(xa[:, h * AG:(h + 1) * AG, :], tiles(x, (NA * j + h) * (AG * P))).then_inc(xa_loaded[h].sem, 16)

            def store(j, h):
                sp.wait_ge(norm_done.sem, norm_done.done((NA * j + h) * AG + (AG - 1)))
                sp.dma_start(tiles(xn_d, (NA * j + h) * (AG * P)), xa[:, h * AG:(h + 1) * AG, :]).then_inc(xn_stored[h].sem, 16)

            def load_lo(m):
                n = E * WCOLS // NA
                for i, w in enumerate((w1l, w2l)):
                    sp.dma_start(w[:, m * n:(m + 1) * n].bitcast(F32), lo_d[i, :, m * n:(m + 1) * n]).then_inc(w_loaded[i], 16)

            rounds = T // (NA * AG)
            for h in range(NA):
                load(0, h, False)
            store(0, 0)
            with sp.Fori(0, rounds - 1) as j:
                for h in range(NA):
                    if h + 1 < NA:
                        store(j, h + 1)
                    else:
                        store(j + 1, 0)
                    load(j + 1, h)
            for h in range(1, NA):
                store(rounds - 1, h)
                if not first:
                    load_lo(h - 1)
            if not first:
                load_lo(NA - 1)
            if first:
                sp.wait_ge(w_lo.sem, w_lo.done(NW - 1))
                sp.dma_start(lo_d[0], w1l[:, :].bitcast(F32)).then_inc(w_spilt, 16)
                sp.dma_start(lo_d[1], w2l[:, :].bitcast(F32)).then_inc(w_spilt, 16)
                sp.wait_ge(w_spilt, 32)
            if out is not None:
                for s in e_loaded:
                    s.open(sp)
                for u in range(2):
                    sp.wait_ge(scattered[u].sem, scattered[u].done(NT // 2 - 1))
                with sp.Fori(0, T // (2 * EG)) as j:
                    for h in range(2):
                        row = (2 * j + h) * (EG * P)
                        sp.wait_ge(e_done.sem, e_done.done((2 * j + (h - 1)) * EG - 1))
                        for k in range(TOP):
                            sp.dma_start(er[:, h, k, :, :], tiles(ys_d, row + (1 + k * T) * P)).then_inc(e_loaded[h].sem, 16)
                        sp.wait_ge(e_stored[h].sem, e_stored[h].done(j - 1))
                        sp.dma_start(ex[:, h, :, :], tiles(x, row)).then_inc(e_loaded[h].sem, 16)

        @block.gpsimd
        def _(pool):
            pool.iota(iota_e[:, :, :], pattern=[[0, T], [1, E]], base=0, channel_multiplier=0,
                      allow_small_or_imprecise_dtypes=True)
            pool.iota(iota_col[:, :], pattern=[[1, P]], base=0, channel_multiplier=0,
                      allow_small_or_imprecise_dtypes=True).then_inc(iotas, 1)
            pool.iota(iota_j[:, :, :], pattern=[[1, NT], [0, E]], base=0, channel_multiplier=0,
                      allow_small_or_imprecise_dtypes=True)
            pool.iota(colnum[:, :], pattern=[[1, C]], base=1, channel_multiplier=0,
                      allow_small_or_imprecise_dtypes=True)
            pool.iota(spare[:, :], pattern=[[0, NT // 2], [(C + 1) * P, 2]], base=0, channel_multiplier=1,
                      allow_small_or_imprecise_dtypes=True).then_inc(iotas, 1)
            pow_done.open(pool)
            w_lo.open(pool)

            def lo_weights(n):
                pool.wait_ge(w_hi.sem, w_hi.done(n))
                pool.tensor_tensor(wlo(n), wraw(n), whi(n).bitcast(F32), ALU.subtract).then_inc(w_lo.sem, 1)

            def pows(j, h):
                pool.wait_ge(var_done.sem, var_done.done(2 * j + h))
                pool.tensor_tensor(rstd[:, h, :], ve[:, h, :], c["neghalf"][:, 0:AG], ALU.pow).then_inc(pow_done.sem, 1)

            if first:
                for s in range(T // AG + 1):
                    if s < T // AG:
                        pows(s // 2, s % 2)
                    for n in step_weights(s - 1):
                        lo_weights(n)
            else:
                with pool.Fori(0, T // (2 * AG)) as j:
                    pows(j, 0)
                    pows(j, 1)
            oh_col.open(pool)
            for piece in range(C // PC):
                at, u = slice(piece * PC, (piece + 1) * PC), piece % 2
                pool.wait_ge(oh_hi.sem, oh_hi.done(piece))
                pool.tensor_tensor(ohhi_c[:, u, :, :], ohhi[:, u, :, :], along(colnum[:, at], NT), ALU.mult).then_inc(oh_col.sem, 1)
            pool.wait_ge(routed, 1)
            for s in xn_stored:
                pool.wait_ge(s.sem, s.done(T // (NA * AG) - 1))
            idx_set.open(pool)
            ridx_set.open(pool)

            def column(table, t):
                return table[:, t:t + 1] if isinstance(t, int) else table[:, bass.ds(t, 1)]

            def gather(t, u):
                pool.wait_ge(g_T.sem, g_T.done(t - 2))
                pool.tensor_copy(idx[:, u, :], column(token_of, t)).then_inc(idx_set.sem, 1)
                pool.wait_ge(idx_set.sem, idx_set.done(t))
                pool.sem_inc(dma_go, 1)
                pool.indirect_dma_start(out=xg[:, u, :], out_offset=None, in_=xn_d,
                                        in_offset=bass.IndirectOffsetOnAxis(ap=idx[:, u, :], axis=0)).then_inc(gathered[u].sem, 16)

            def scatter(t, u):
                pool.wait_ge(y_copied.sem, y_copied.done(t))
                pool.tensor_copy(ridx[:, u, :], column(row_of, t)).then_inc(ridx_set.sem, 1)
                pool.wait_ge(ridx_set.sem, ridx_set.done(t))
                pool.sem_inc(dma_go, 1)
                pool.indirect_dma_start(out=ys_d, out_offset=bass.IndirectOffsetOnAxis(ap=ridx[:, u, :], axis=0),
                                        in_=y[:, u, :], in_offset=None).then_inc(scattered[u].sem, 16)

            for t in range(5):
                gather(t, t % 2)
            pool.wait_ge(routed, 2)
            with pool.Fori(0, NT // 2 - 3) as j:
                for u in range(2):
                    gather(2 * j + (5 + u), 1 - u)
                    scatter(2 * j + u, u)
            gather(NT - 1, 1)
            for t in range(NT - 6, NT):
                scatter(t, t % 2)
            for u in range(2):
                pool.wait_ge(scattered[u].sem, scattered[u].done(NT // 2 - 1))

        @block.scalar
        def _(act):
            for s in (xT_copied, logit_copied, oh_part, relu_done, sq_done):
                s.open(act)

            def load_weights(n):
                if n >= NRAW:
                    act.wait_ge(w_lo.sem, w_lo.done(n - NRAW))
                act.dma_start(wraw(n).rearrange("p (k n) -> p k n", k=KD if n % 2 == 0 else KH), wsrc(n)).then_inc(w_loaded[n % NRAW], 16)

            def copy_xT(j, q):
                for u in range(2):
                    act.wait_ge(xT_ready.sem, xT_ready.done(2 * j + u))
                    act.wait_ge(logit_ready.sem, logit_ready.done(2 * j + (u - 4)))
                    act.activation(xT[:, 2 * q + u, :, :], turned[2 * q + u][:, 0:D].rearrange("p (k q) -> p k q", k=KD), ACT.Copy).then_inc(xT_copied.sem, 1)

            def copy_logits(j):
                for u in range(2):
                    i = 2 * j + u
                    act.wait_ge(logit_ready.sem, logit_ready.done(i))
                    dst = logits[:, i, :] if isinstance(i, int) else logits[:, bass.ds(i, 1), :].rearrange("p a e -> p (a e)")
                    act.activation(dst, pY[u][:, 0:E], ACT.Copy).then_inc(logit_copied.sem, 1)

            if first:
                for n in range(NRAW - 1):
                    load_weights(n)
                copy_xT(0, 0)
                for j in range(T // 2):
                    if j + NRAW - 1 < NW:
                        load_weights(j + NRAW - 1)
                    if j + 1 < T // 2:
                        copy_xT(j + 1, (j + 1) % 2)
                    copy_logits(j)
            else:
                copy_xT(0, 0)
                with act.Fori(0, T // 4 - 1) as j:
                    for q in range(2):
                        copy_xT(2 * j + (q + 1), 1 - q)
                        copy_logits(2 * j + q)
                copy_xT(T // 2 - 1, 1)
                copy_logits(T // 2 - 2)
                copy_logits(T // 2 - 1)
            act.wait_ge(exp_in, 1)
            act.activation(top[:, 3, :], top[:, 2, :], ACT.Exp).then_inc(exp_out, 1)
            for piece in range(C // PC):
                u = piece % 2
                act.wait_ge(oh_hi.sem, oh_hi.done(piece))
                act.activation(ohhi_p[:, u, :, :], ohhi[:, u, :, :], ACT.Copy, scale=c["part"][:, 0:1]).then_inc(oh_part.sem, 1)

            def relu(t, u):
                act.wait_ge(h_ready.sem, h_ready.done(t))
                act.activation(r[:, u, :], pH[u][:, :], ACT.Relu).then_inc(relu_done.sem, 1)

            def square(t, u):
                act.wait_ge(rT_ready.sem, rT_ready.done(t))
                act.wait_ge(h2_split.sem, h2_split.done(t - 2))
                act.activation(h2[:, u, :, :], pR[u][:, :].rearrange("p (k q) -> p k q", k=KH), ACT.Square).then_inc(sq_done.sem, 1)

            relu(0, 0)
            with act.Fori(0, NT // 2 - 1) as j:
                for u in range(2):
                    relu(2 * j + (u + 1), 1 - u)
                    square(2 * j + u, u)
            relu(NT - 1, 1)
            square(NT - 2, 0)
            square(NT - 1, 1)
            if out is not None:
                for s in e_stored:
                    s.open(act)
                with act.Fori(0, T // (2 * EG)) as j:
                    for h in range(2):
                        act.wait_ge(e_done.sem, e_done.done((2 * j + h) * EG + (EG - 1)))
                        act.dma_start(tiles(out, (2 * j + h) * (EG * P)), ex[:, h, :, :]).then_inc(e_stored[h].sem, 16)
                for s in e_stored:
                    act.wait_ge(s.sem, s.done(T // (2 * EG) - 1))

        @block.tensor
        def _(pe):
            for s in (xT_ready, logit_ready, oh_used, g_T, h_ready, rT_ready, y_ready):
                s.open(pe)
            pe.wait_ge(rw_loaded, 16)
            for k in range(KD):
                last = pe.transpose(pR[0][:, k * E:(k + 1) * E], rw[:, k * P:(k + 1) * P], ident[0:E, 0:E])
            last.then_inc(rwT_ready, 1)
            pe.wait_ge(rwT_ready, 2)
            with pe.Fori(0, T // (NA * AG)) as j:
                def turn(m):
                    i = NA * AG * j + m
                    pe.wait_ge(norm_done.sem, norm_done.done(i))
                    pe.wait_ge(xT_copied.sem, xT_copied.done(i - 4))
                    for k in range(KD):
                        last = pe.transpose(turned[m % 4][:, k * P:(k + 1) * P], xa[:, m, k * P:(k + 1) * P], ident[:, :])
                    last.then_inc(xT_ready.sem, 1)

                def score(m):
                    i = NA * AG * j + m
                    pe.wait_ge(xT_copied.sem, xT_copied.done(i))
                    pe.wait_ge(logit_copied.sem, logit_copied.done(i - 2))
                    for k in range(KD):
                        last = pe.matmul(pY[m % 2][:, 0:E], xT[:, m % 4, k, :], rwT[:, k, :], start=(k == 0), stop=(k == KD - 1))
                    last.then_inc(logit_ready.sem, 1)

                turn(0)
                turn(1)
                for m in range(0, NA * AG, 2):
                    if m + 2 < NA * AG:
                        turn(m + 2)
                        turn(m + 3)
                    score(m)
                    score(m + 1)
            pe.wait_ge(counts_in, 1)
            pe.matmul(pR[0][:, 0:T * E], c["strict_tri"][:, :], both[:, :], start=True, stop=True)
            pe.matmul(pR[1][:, 0:T * E], c["ones_bf"][:, :], both[:, :], start=True, stop=True).then_inc(counts_out, 1)

            for piece in range(C // PC):
                pe.wait_ge(oh_lo.sem, oh_lo.done(piece))
                pe.wait_ge(oh_part.sem, oh_part.done(piece))
                pe.wait_ge(oh_col.sem, oh_col.done(piece))
                for n in range(PC):
                    ends = dict(start=(piece == 0 and n == 0), stop=(piece == C // PC - 1 and n == PC - 1))
                    pe.matmul(pT[0][0:NT, 0:P], ohhi_p[:, piece % 2, n, :], ohlo[:, piece % 2, n, :], **ends)
                    last = pe.matmul(pT[1][0:NT, 0:P], ohhi_c[:, piece % 2, n, :], ohlo[:, piece % 2, n, :], **ends)
                last.then_inc(oh_used.sem, 1)
            pe.wait_ge(inv_ready, 1)
            pe.transpose(pY[0][:, 0:NT], inv[0:NT, :], ident[0:NT, 0:NT]).then_inc(invT_ready, 1)

            def expert_columns(t):
                return pe.value_load(expert_i[0:1, t:t + 1] if isinstance(t, int) else expert_i[0:1, bass.ds(t, 1)],
                                     min_val=0, max_val=(E - 1) * WCOLS)

            def turn_x(t, u):
                pe.wait_ge(gathered[u].sem, gathered[u].done(half(t, u)))
                for k in range(KD):
                    last = pe.transpose(pT[u][:, k * P:(k + 1) * P], xg[:, u, k * P:(k + 1) * P], ident[:, :])
                last.then_inc(g_T.sem, 1)

            def of_expert(w, at):
                return w[:, bass.ds(at, WCOLS)]

            def up(t, u, at=None):
                at = expert_columns(t) if at is None else at
                pe.wait_ge(g_split.sem, g_split.done(t))
                n = 0
                hi, lo = of_expert(w1h, at), of_expert(w1l, at)
                for a, w in ((xh, hi), (xh, lo), (xl, hi)):
                    for k in range(KD):
                        last = pe.matmul(pH[u][:, :], a[:, u, k, :], w[:, k * HID:(k + 1) * HID],
                                         start=(n == 0), stop=(n == 3 * KD - 1))
                        n += 1
                last.then_inc(h_ready.sem, 1)

            def turn_h(t, u):
                pe.wait_ge(relu_done.sem, relu_done.done(t))
                for k in range(KH):
                    last = pe.transpose(pR[u][:, k * P:(k + 1) * P], r[:, u, k * P:(k + 1) * P], ident[:, :])
                last.then_inc(rT_ready.sem, 1)

            def down(t, u, at=None):
                at = expert_columns(t) if at is None else at
                pe.wait_ge(h2_split.sem, h2_split.done(t))
                pe.wait_ge(y_copied.sem, y_copied.done(t - 2))
                n = 0
                hi, lo = of_expert(w2h, at), of_expert(w2l, at)
                for a, w in ((h2h, hi), (h2h, lo), (h2l, hi)):
                    for k in range(KH):
                        last = pe.matmul(pY[u][:, 0:D], a[:, u, k, :], w[:, k * D:(k + 1) * D],
                                         start=(n == 0), stop=(n == 3 * KH - 1))
                        n += 1
                last.then_inc(y_ready.sem, 1)

            def half(t, u):
                return (t - u) // 2 if isinstance(t, int) else t

            if not first:
                for s in w_loaded[0:2]:
                    pe.wait_ge(s, 16 * NA)
            turn_x(0, 0)
            turn_x(1, 1)
            pe.wait_ge(experts_known, 1)
            up(0, 0)
            turn_x(2, 0)
            up(1, 1)
            turn_h(0, 0)
            with pe.Fori(0, NT // 2 - 2) as j:
                following = None
                for u in range(2):
                    v = 1 - u
                    up(2 * j + (2 + u), u, following)
                    current = expert_columns(2 * j + u)
                    pe.wait_ge(gathered[v].sem, gathered[v].done(j + 1 + u))
                    for k in range(KD):
                        last = pe.transpose(pT[v][:, k * P:(k + 1) * P], xg[:, v, k * P:(k + 1) * P], ident[:, :])
                    last.then_inc(g_T.sem, 1)
                    following = expert_columns(2 * j + 3) if u == 0 else None
                    turn_h(2 * j + (1 + u), v)
                    down(2 * j + u, u, current)
            t = NT - 3
            turn_x(t + 2, 1)
            up(t + 1, 0)
            turn_h(t, 1)
            down(t - 1, 0)
            up(t + 2, 1)
            turn_h(t + 1, 0)
            down(t, 1)
            turn_h(t + 2, 1)
            down(t + 1, 0)
            down(t + 2, 1)

        @block.vector
        def _(dve):
            for s in (w_hi, st_chain, mv_done, var_done, norm_done, oh_hi, oh_lo, g_hi, g_split, h2_hi, h2_split, y_copied):
                s.open(dve)
            dve.wait_ge(rwT_ready, 1)
            dve.tensor_copy(rwT[:, :, :], pR[0][:, 0:KD * E].rearrange("p (k e) -> p k e", k=KD)).then_inc(rwT_ready, 1)

            def moments(j, h):
                s, v = NA * j + h, h % 2
                dve.wait_ge(xa_loaded[h].sem, xa_loaded[h].done(j))
                for n in range(AG):
                    last = dve.bn_stats(st[:, n, :], xa[:, h * AG + n, :])
                last.then_inc(st_chain.sem, 1)
                dve.wait_ge(norm_done.sem, norm_done.done((s - 1) * AG - 1))
                dve.wait_ge(st_chain.sem, st_chain.done(s))
                dve.sem_inc(aggr_go, 1)
                for n in range(AG):
                    last = dve.bn_aggr(mv[:, v * AG + n, :], st[:, n, :])
                last.then_inc(mv_done.sem, 1)
                dve.wait_ge(mv_done.sem, mv_done.done(s))
                dve.tensor_scalar(ve[:, v, :], mv[:, v * AG:(v + 1) * AG, 1], EPS, None, ALU.add).then_inc(var_done.sem, 1)

            def normalise(j, h):
                v = h % 2
                dve.wait_ge(pow_done.sem, pow_done.done(NA * j + h))
                for n in range(AG):
                    a = xa[:, h * AG + n, :]
                    dve.tensor_scalar(a, a, mv[:, v * AG + n, 0:1], rstd[:, v, n:n + 1], ALU.subtract, ALU.mult).then_inc(norm_done.sem, 1)

            def hi_weights(n):
                dve.wait_ge(w_loaded[n % NRAW], 16 * (n // NRAW + 1))
                dve.tensor_copy(whi(n), wraw(n)).then_inc(w_hi.sem, 1)

            rounds = T // (NA * AG)
            moments(0, 0)
            if first:
                for s in range(T // AG):
                    if s + 1 < T // AG:
                        moments((s + 1) // NA, (s + 1) % NA)
                    normalise(s // NA, s % NA)
                    for n in step_weights(s):
                        hi_weights(n)
            else:
                with dve.Fori(0, rounds - 1) as j:
                    for h in range(NA):
                        if h + 1 < NA:
                            moments(j, h + 1)
                        else:
                            moments(j + 1, 0)
                        normalise(j, h)
                for h in range(NA):
                    if h + 1 < NA:
                        moments(rounds - 1, h + 1)
                    normalise(rounds - 1, h)

            chain = Chain(dve, b_chain)
            link = chain.link
            dve.wait_ge(iotas, 2)
            link(dve.tensor_copy(iota_bf[:, :], iota_col[:, :]))
            dve.wait_ge(logit_copied.sem, logit_copied.done(T - 1))

            def wide(ap):
                return ap.rearrange("p (t a) -> p t a", a=1).to_broadcast([P, T, E])

            def first_largest(scores, best, num, onehot):
                link(dve.tensor_reduce(best, scores, AX.X, ALU.max))
                link(dve.tensor_tensor(work[0][:, :, :], scores, wide(best), ALU.not_equal))
                link(dve.scalar_tensor_tensor(work[1][:, :, :], work[0][:, :, :], float(E), iota_e[:, :, :], ALU.mult, ALU.add))
                link(dve.tensor_reduce(num, work[1][:, :, :], AX.X, ALU.min))
                link(dve.tensor_tensor(onehot, iota_e[:, :, :], wide(num), ALU.is_equal))

            first_largest(logits[:, :, :], top[:, 0, :], top[:, 4, :], oh[0][:, :, :])
            link(dve.tensor_scalar(work[2][:, :, :], oh[0][:, :, :], -2.0, 1.0, ALU.mult, ALU.add))
            link(dve.scalar_tensor_tensor(work[3][:, :, :], work[2][:, :, :], BIG, logits[:, :, :], ALU.mult, ALU.min))
            first_largest(work[3][:, :, :], top[:, 1, :], top[:, 5, :], oh[1][:, :, :])
            link(dve.tensor_tensor(top[:, 2, :], top[:, 1, :], top[:, 0, :], ALU.subtract))
            dve.tensor_tensor(both[:, :].rearrange("p (t e) -> p t e", e=E), oh[0][:, :, :], oh[1][:, :, :], ALU.add).then_inc(counts_in, 1)
            dve.sem_inc(exp_in, 1)
            per, run, ahead = work[0], work[1], work[2]
            reset = work[3]

            def by_expert(t):
                return t[:, :, :].rearrange("p t e -> p (t e)").rearrange("p (e t) -> p e t", e=E)

            link(dve.memset(by_expert(reset), 1.0))
            link(dve.memset(by_expert(reset)[:, :, 0:1], 0.0))
            dve.wait_ge(counts_out, 1)
            link(dve.tensor_copy(by_expert(per), pR[1][:, 0:T * E].rearrange("p (t e) -> p e t", e=E)))
            link(dve.tensor_tensor_scan(run[:, :, :].rearrange("p t e -> p (t e)"), reset[:, :, :].rearrange("p t e -> p (t e)"),
                                        per[:, :, :].rearrange("p t e -> p (t e)"), 0.0, ALU.mult, ALU.add))
            link(dve.tensor_tensor(ahead[:, :, :], run[:, :, :], per[:, :, :], ALU.subtract))
            link(dve.tensor_scalar(smalli[:, 0, :], by_expert(run)[:, :, T - 1:T].rearrange("p e a -> p (e a)"), float(P - 1), None, ALU.add))
            link(dve.tensor_scalar(smalli[:, 1, :], smalli[:, 0, :], P.bit_length() - 1, None, ALU.logical_shift_right))
            link(dve.tensor_copy(small[:, 0, :], smalli[:, 1, :]))
            link(dve.memset(small[:, 1, :], 1.0))
            link(dve.tensor_tensor_scan(small[:, 2, :], small[:, 1, :], small[:, 0, :], 0.0, ALU.mult, ALU.add))
            link(dve.tensor_tensor(small[:, 3, :], small[:, 2, :], small[:, 0, :], ALU.subtract))
            link(dve.tensor_scalar(small[:, 4, :], small[:, 3, :], float(P), None, ALU.mult))
            link(dve.tensor_tensor(by_expert(run), by_expert(ahead),
                                   small[:, 4, :].rearrange("p (e a) -> p e a", a=1).to_broadcast([P, E, T]), ALU.add))
            slot_all = work[4]
            link(dve.tensor_tensor(slot_all[:, :, :], pR[0][:, 0:T * E].rearrange("p (t e) -> p t e", e=E),
                                   by_expert(run).rearrange("p e t -> p t e"), ALU.add))
            for k in range(TOP):
                link(dve.tensor_tensor(work[5][:, :, :], slot_all[:, :, :], oh[k][:, :, :], ALU.mult))
                link(dve.tensor_reduce(slotf[:, k * T:(k + 1) * T], work[5][:, :, :], AX.X, ALU.add))
            link(dve.tensor_copy(slots[:, :], slotf[:, :]))
            link(dve.tensor_scalar(parts_i[:, 0, :], slots[:, :], P - 1, None, ALU.bitwise_and))
            link(dve.tensor_scalar(parts_i[:, 1, :], slots[:, :], P.bit_length() - 1, None, ALU.logical_shift_right))
            link(dve.tensor_copy(parts_b[:, :, :], parts_i[:, :, :]))
            for piece in range(C // PC):
                at, u = slice(piece * PC, (piece + 1) * PC), piece % 2
                if piece >= 2:
                    dve.wait_ge(oh_used.sem, oh_used.done(piece - 2))
                dve.tensor_tensor(ohhi[:, u, :, :], across(iota_bf[:, 0:NT], NT), along(parts_b[:, 1, at], NT), ALU.is_equal).then_inc(oh_hi.sem, 1)
                dve.tensor_tensor(ohlo[:, u, :, :], across(iota_bf[:, :], P), along(parts_b[:, 0, at], P), ALU.is_equal).then_inc(oh_lo.sem, 1)
            dve.wait_ge(exp_out, 1)
            link(dve.tensor_scalar(top[:, 4, :], top[:, 3, :], 1.0, None, ALU.add))
            link(dve.reciprocal(top[:, 5, :], top[:, 4, :]))
            link(dve.tensor_scalar(gates[:, 0:T], top[:, 5, :], 0.5, None, ALU.mult))
            link(dve.tensor_tensor(gates[:, T:2 * T], gates[:, 0:T], top[:, 3, :], ALU.mult))
            dve.wait_ge(oh_used.sem, oh_used.done(C // PC - 1))
            link(dve.tensor_copy(inv2[0:NT, :], pT[1][0:NT, 0:P]))
            dve.scalar_tensor_tensor(inv[0:NT, :], inv2[0:NT, :], float(P), pT[0][0:NT, 0:P], ALU.mult, ALU.add).then_inc(inv_ready, 1)
            dve.wait_ge(invT_ready, 1)
            link(dve.tensor_copy(row_f[:, 0, :], pY[0][:, 0:NT]))
            link(dve.tensor_scalar(row_f[:, 1, :], row_f[:, 0, :], float(TOK - P), None, ALU.add))
            link(dve.tensor_copy(row_t[:, :], row_f[:, 1, :]))
            dve.tensor_scalar(token_of[:, :], row_t[:, :], TOK - 1, None, ALU.bitwise_and).then_inc(routed, 1)
            link(dve.scalar_tensor_tensor(row_f[:, 2, :], row_f[:, 0, :], 0.0, spare[:, :], ALU.is_equal, ALU.mult))
            dve.tensor_tensor(row_of[:, :], row_f[:, 0, :], row_f[:, 2, :], ALU.add).then_inc(routed, 1)
            upto = small[:, 2, :].rearrange("p (a e) -> p a e", a=1).to_broadcast([P, NT, E])
            link(dve.tensor_tensor(iota_j[:, :, :], iota_j[:, :, :], upto, ALU.is_ge))
            link(dve.tensor_reduce(expert_f[:, :], iota_j[:, :, :], AX.X, ALU.add))
            dve.tensor_scalar(expert_i[:, :], expert_f[:, :], float(E - 1), float(WCOLS), ALU.min, ALU.mult).then_inc(experts_known, 1)

            def split_x(t, u):
                dve.wait_ge(g_T.sem, g_T.done(t))
                dve.wait_ge(h_ready.sem, h_ready.done(t - 2))
                src = pT[u][:, 0:D].rearrange("p (k q) -> p k q", k=KD)
                dve.tensor_copy(xh[:, u, :, :], src).then_inc(g_hi.sem, 1)
                dve.wait_ge(g_hi.sem, g_hi.done(t))
                dve.tensor_tensor(xl[:, u, :, :], src, xh[:, u, :, :].bitcast(F32), ALU.subtract).then_inc(g_split.sem, 1)

            def split_h(t, u):
                dve.wait_ge(sq_done.sem, sq_done.done(t))
                dve.wait_ge(y_ready.sem, y_ready.done(t - 2))
                dve.tensor_copy(h2h[:, u, :, :], h2[:, u, :, :]).then_inc(h2_hi.sem, 1)
                dve.wait_ge(h2_hi.sem, h2_hi.done(t))
                dve.tensor_tensor(h2l[:, u, :, :], h2[:, u, :, :], h2h[:, u, :, :].bitcast(F32), ALU.subtract).then_inc(h2_split.sem, 1)

            def copy_y(t, u, n):
                dve.wait_ge(y_ready.sem, y_ready.done(t))
                if n is not None:
                    dve.wait_ge(scattered[u].sem, scattered[u].done(n - 1))
                dve.tensor_copy(y[:, u, :], pY[u][:, 0:D]).then_inc(y_copied.sem, 1)

            split_x(0, 0)
            split_x(1, 1)
            split_x(2, 0)
            split_h(0, 0)
            for t in (1, 2):
                split_x(t + 2, t % 2)
                split_h(t, t % 2)
                copy_y(t - 1, (t - 1) % 2, None)
            with dve.Fori(1, NT // 2 - 2) as j:
                for u in range(2):
                    v = 1 - u
                    split_x(2 * j + (3 + u), v)
                    split_h(2 * j + (1 + u), v)
                    copy_y(2 * j + u, u, j)
            split_x(NT - 1, 1)
            split_h(NT - 3, 1)
            copy_y(NT - 4, 0, NT // 2 - 2)
            split_h(NT - 2, 0)
            copy_y(NT - 3, 1, NT // 2 - 2)
            split_h(NT - 1, 1)
            copy_y(NT - 2, 0, NT // 2 - 1)
            copy_y(NT - 1, 1, NT // 2 - 1)

            if out is not None:
                for s in (e_first, e_done):
                    s.open(dve)
                with dve.Fori(0, T // (2 * EG)) as j:
                    for h in range(2):
                        dve.wait_ge(e_loaded[h].sem, e_loaded[h].done(j))
                        for k in range(TOP):
                            for n in range(EG):
                                i = (2 * j + h) * EG + n
                                if k > 0:
                                    dve.wait_ge(e_first.sem, e_first.done(i))
                                dve.scalar_tensor_tensor(ex[:, h, n, :], er[:, h, k, n, :], gates[:, bass.ds(i + k * T, 1)], ex[:, h, n, :],
                                                         ALU.mult, ALU.add).then_inc((e_first, e_done)[k].sem, 1)


def make_keep(nc, ctx, tokens):
    def sb(name, shape, dt):
        return ctx.enter_context(nc.sbuf_tensor(name, shape, dt))
    return {
        "gathers": Gathers(nc, ctx, "gather"),
        "scatters": Gathers(nc, ctx, "scatter"),
        "w1h": sb("w1h", [P, E * WCOLS], F32R),
        "w2h": sb("w2h", [P, E * WCOLS], F32R),
        "gates": sb("gates", [P, TOP * tokens // P], F32),
    }

DIN = 512
KI = DIN // P
NS = 64
H = 8
HD = DIN // H
CONV = 4
NB = (DIN + 2 * NS) // P
GC = 4
GT = GC * P
ORDER = (NB - 1, *range(NB - 1))
BY_ACT = (1, 3)
ATANH = [1.0 / n for n in (13, 11, 9, 7, 5, 3)]


def mamba_block(nc, c, keep, x, ys_d, w_in, conv_w, conv_b, dt_bias, a_log, d_skip, norm_w, w_out, x2, batches):
    TOK = x.shape[0]
    T = TOK // P
    NG = TOK // GT
    PER = NG // batches
    CR = 2 * GC
    with ExitStack() as ctx:
        def sb(name, shape, dt=F32):
            return ctx.enter_context(nc.sbuf_tensor(name, shape, dt))

        sem = Sems(nc, ctx)

        def step(name, unit=1):
            return Step(sem("m_" + name), unit, CR)

        ident, tri = c["ident"], c["incl_tri"]
        gates = keep["gates"]
        NIN = w_in.shape[1]
        wih, wil = sb("wih", [P, KD, NIN], F32R), sb("wil", [P, KD, NIN], F32R)
        woh, wol = sb("woh", [P, KI, D], F32R), sb("wol", [P, KI, D], F32R)
        cw, cb, nw = sb("cw", [P, NB, CONV]), sb("cb", [P, NB]), sb("nw", [P, KI])
        cwh, cbh = sb("cwh", [P, NB, CONV]), sb("cbh", [P, NB])
        heads = sb("heads", [P, 3, H])
        negA = sb("negA", [P, GC, H])
        flags = sb("flags", [P, NG + 1])
        ident_bf, tri_bf = sb("ident_bf", [P, P], BF16), sb("tri_bf", [P, P], BF16)
        future = sb("future", [P, GC, P], BF16)
        xr = sb("xr", [P, 2 * GC, D])
        yg = sb("m_yg", [P, 2, TOP, D])
        st, mv, ve, rstd = sb("m_st", [P, 6]), sb("m_mv", [P, 2]), sb("m_ve", [P, 1]), sb("m_rstd", [P, 1])
        xn = sb("m_xn", [P, D])
        xTh, xTl = sb("xTh", [P, KD, GT], F32R), sb("xTl", [P, KD, GT], F32R)
        tz = sb("tz", [P, DIN])
        sz = sb("sz", [P, GC, DIN])
        NR = 14
        dts = sb("dts", [P, 2, NR, GC * H])
        al = sb("al", [P, 2, 3, GC * H], BF16)
        raw = sb("raw", [P, NB, CONV - 1 + GT])
        acc = sb("acc", [P, 2, NB, GT])
        tap = sb("tap", [P, 2, GT])
        tb = sb("tb", [P, 2, GT])
        CT = sb("CT", [NS, 2, GT])
        S, S1 = sb("S", [NS, DIN]), sb("S1", [NS, DIN])
        xt, xdt, xw, xD = (sb(n, [P, DIN]) for n in ("xt", "xdt", "xw", "xD"))
        Bt = sb("Bt", [P, NS])
        ex, M = sb("ex", [P, H, P]), sb("M", [P, H, P])
        t1, td, t2, yv = (sb(n, [P, DIN]) for n in ("t1", "td", "t2", "yv"))
        ss, vr, rs = sb("ss", [P, 1]), sb("vr", [P, 1]), sb("rs", [P, 1])
        yTh, yTl = sb("yTh", [P, KI, P], F32R), sb("yTl", [P, KI, P], F32R)
        xo = sb("xo", [P, 2, D])
        wst = acc[:, :, :, :].rearrange("p q b t -> p (q b t)")[:, 0:KD * NIN].rearrange("p (k n) -> p k n", k=KD)
        wost = ex[:, :, :].rearrange("p h t -> p (h t)")[:, 0:KI * D].rearrange("p (k n) -> p k n", k=KI)
        DTR, DPOS, DABS, DU, DS, DS2, DQ, DT, DA, NCUM, ECUM, DEC, DECDT, ETOT = range(NR)

        pX, pYT, small, pE, pY, pS, pZ, pO = (ctx.enter_context(nc.psum_tensor(f"bank{n}", [P, 512], F32)) for n in range(8))
        pG, pBt = small[:, 0:P], small[:, P:P + NS]
        pCum, pTot = small[:, 256:256 + GC * H], small[:, 320:320 + GC * H]
        pXN, pDt = pO[:, D:2 * D], pO[:, D:D + H]
        pP = [pZ, pO]

        in_loaded, loads, consts, d_prep, a_prep, prep = (sem(n) for n in ("m_in_loaded", "m_loads", "m_consts", "d_prep", "a_prep", "m_prep"))
        go, soft_chain = sem("m_go"), sem("soft_chain")
        x_loaded = [step(f"x_loaded{n}", 16) for n in range(2 * GC)]
        y_loaded = [Step(sem(f"y_loaded{u}"), 16 * TOP) for u in range(2)]
        o_stored = [step(f"o_stored{u}", 16) for u in range(2)]
        add1, add2, stats, aggr, var_done, pow_done, norm_done, xT_ready, xT_hi, xT_lo, z_ready, tz_done, sz_done, dt_ready, dt_added = (
            step(n) for n in ("add1", "add2", "stats", "aggr", "var", "pow", "norm", "xT", "xT_hi", "xT_lo", "z", "tz", "sz", "dt", "dt_added"))
        soft, exp_u, a_done, al_done, cum_ready, cum_copied, exps, dec_in, dec_out, decdt, halo, s_sum = (
            step(n) for n in ("soft", "exp_u", "a", "al", "cum", "cum_copied", "exps", "dec_in", "dec_out", "decdt", "halo", "s_sum"))
        p_ready, raw_done, tap0, tap_made, tap_act, tap_own, tap1, tap_chain, taps, tb_done, xc_done = (
            step(n) for n in ("p", "raw", "tap0", "tap_made", "tap_act", "tap_own", "tap1", "tap_chain", "taps", "tb", "xc"))
        sm_ready, bt_done, turned, xt_done, e0_ready, ex0_done, e1_ready, ex_done, xdt_done, M_done, xw_done = (
            step(n) for n in ("sm", "bt", "turned", "xt", "e0", "ex0", "e1", "ex", "xdt", "M", "xw"))
        i_ready, y_ready, s_ready, s1_done, S_done, t1_done, td_done, t2_done, yv_done, sq_done, rs_in, rs_done = (
            step(n) for n in ("i", "y", "s", "s1", "S", "t1", "td", "t2", "yv", "sq", "rs_in", "rs"))
        yT_ready, yT_hi, yT_lo, o_ready, xo_done = (step(n) for n in ("yT", "yT_hi", "yT_lo", "o", "xo"))

        def row(g, n, k=0, chunks=GC):
            return dts[:, g.q, n, k * H:(k + chunks) * H]

        def per_head(ap, width, parts=P):
            return ap.rearrange("p (h a) -> p h a", a=1).to_broadcast([parts, ap.shape[1], width])

        def by_head(ap, heads=H):
            return ap.rearrange("p (h d) -> p h d", h=heads)

        class At:

            def __init__(self, j, q):
                self.j, self.q, self.group = j, q, 2 * j + q

            def chunk(self, k):
                return self.j * (2 * GC) + (self.q * GC + k)

            def nth(self, k):
                return self.j * GC + (self.q * (GC // 2) + k // 2)

            def block(self, m):
                return self.j * (2 * NB) + (self.q * NB + m)

            def tbuf(self, m):
                return (self.q * NB + m) % 2

        def added(g, m):
            return tap1.done(g.group * (NB - 1) + (m - 1))

        LAST = NG // 2 - 1

        def run(eng, front, convolve, slot, finish):
            for k in range(GC):
                front(At(0, 0), k)
            convolve(At(0, 0), None)
            with eng.Fori(0, LAST) as j:
                for g, following in ((At(j, 0), At(j, 1)), (At(j, 1), At(j + 1, 0))):
                    for k in range(GC):
                        slot(g, k, following)
                    convolve(following, g)
            g, following = At(LAST, 0), At(LAST, 1)
            for k in range(GC):
                slot(g, k, following)
            convolve(following, g)
            for k in range(GC):
                slot(following, k, None)
            finish(following)

        ctx.callback(sem.clear)
        block = ctx.enter_context(nc.Block())

        @block.sync
        def _(sp):
            sp.dma_start(wst[:, :, :], w_in.rearrange("(k p) n -> p k n", p=P)).then_inc(in_loaded, 16)
            sp.dma_start(wost[:, :, :], w_out.rearrange("(k p) n -> p k n", p=P)).then_inc(loads, 16)
            sp.dma_start(cw[:, :, :], conv_w.rearrange("(k p) n -> p k n", p=P)).then_inc(loads, 16)
            sp.dma_start(cb[:, :], conv_b.rearrange("(k p) -> p k", p=P), allow_slow_non_contiguous=True).then_inc(loads, 16)
            sp.dma_start(nw[:, :], norm_w.rearrange("(k p) -> p k", p=P), allow_slow_non_contiguous=True).then_inc(loads, 16)
            for n, v in enumerate((dt_bias, a_log, d_skip)):
                sp.dma_start(heads[:, n, :], v.rearrange("(a h) -> a h", a=1).to_broadcast([P, H])).then_inc(loads, 16)
            for s in (*x_loaded, *y_loaded, *o_stored):
                s.open(sp)

            def load(g, k):
                n, u = (g.q * GC + k) % (2 * GC), k % 2
                sp.wait_ge(xo_done.sem, xo_done.done(g.chunk(k - 2 * GC)))
                sp.dma_start(xr[:, n, :], x[bass.ds(g.chunk(k) * P, P), :]).then_inc(x_loaded[n].sem, 16)
                sp.wait_ge(add2.sem, add2.done(g.chunk(k - 2)))
                for r in range(TOP):
                    sp.dma_start(yg[:, u, r, :], ys_d[bass.ds(g.chunk(k) * P + (1 + r * T) * P, P), :]).then_inc(y_loaded[u].sem, 16)

            def store(g, k):
                sp.wait_ge(xo_done.sem, xo_done.done(g.chunk(k)))
                sp.dma_start(x2[bass.ds(g.chunk(k) * P, P), :], xo[:, k % 2, :]).then_inc(o_stored[k % 2].sem, 16)

            def front(g, k):
                if k == 0:
                    load(g, 0)
                load(g, k + 1)

            def slot(g, k, following):
                if following is not None and not (isinstance(following.j, int) and k == GC - 1):
                    load(following, k + 1)
                if k > 0:
                    store(g, k - 1)

            def convolve(g, before):
                if before is not None:
                    store(before, GC - 1)

            run(sp, front, convolve, slot, lambda g: store(g, GC - 1))
            for u in range(2):
                sp.wait_ge(o_stored[u].sem, o_stored[u].done(T // 2 - 1))

        @block.gpsimd
        def _(pool):
            chain = Chain(pool, consts)
            pool.memset(flags[:, :], 1.0)
            pool.memset(ident_bf[:, :], 0.0)
            pool.memset(future[:, :, :], 0.0)
            pool.memset(S[:, :], 0.0)
            chain.link(pool.memset(raw[:, :, 0:CONV - 1], 0.0))
            for b in range(batches):
                pool.memset(flags[:, b * PER:b * PER + 1], 0.0)
            chain.link(pool.affine_select(out=ident_bf[:, :], in_=ident_bf[:, :], compare_op=ALU.not_equal, fill=1.0,
                                          base=0, pattern=[[-1, P]], channel_multiplier=1))
            chain.link(pool.affine_select(out=future[:, :, :], in_=future[:, :, :], compare_op=ALU.is_ge, fill=-1e30,
                                          base=0, pattern=[[0, GC], [1, P]], channel_multiplier=-1))
            for s in (pow_done, xdt_done, xw_done, s1_done, td_done, yv_done, rs_done, tap_made, tap1):
                s.open(pool)

            def front(g, k):
                i = g.chunk(k)
                pool.wait_ge(var_done.sem, var_done.done(i))
                pool.tensor_tensor(rstd[:, :], ve[:, :], c["neghalf"][:, 0:1], ALU.pow).then_inc(pow_done.sem, 1)

            def scale_x(g, k):
                i = g.chunk(k)
                pool.wait_ge(xt_done.sem, xt_done.done(i))
                pool.wait_ge(s_ready.sem, s_ready.done(i - 1))
                pool.tensor_tensor(by_head(xdt[:, :]), by_head(xt[:, :]), per_head(row(g, DT, k, 1), HD), ALU.mult).then_inc(xdt_done.sem, 1)
                pool.tensor_tensor(by_head(xD[:, :]), by_head(xt[:, :]), per_head(heads[:, 2, :], HD), ALU.mult)
                pool.tensor_tensor(by_head(xw[:, :]), by_head(xt[:, :]), per_head(row(g, DECDT, k, 1), HD), ALU.mult).then_inc(xw_done.sem, 1)

            def decay_state(g, k):
                pool.wait_ge(S_done.sem, S_done.done(g.chunk(k - 1)))
                pool.tensor_tensor(by_head(S1[:, :]), by_head(S[:, :]), per_head(dts[0:NS, g.q, ETOT, k * H:(k + 1) * H], HD, NS), ALU.mult).then_inc(s1_done.sem, 1)

            def slot(g, k, following):
                i = g.chunk(k)
                if k > 0:
                    decay_state(g, k)
                pool.wait_ge(xw_done.sem, xw_done.done(i))
                pool.wait_ge(t1_done.sem, t1_done.done(i))
                pool.tensor_tensor(td[:, :], t1[:, :], xD[:, :], ALU.add).then_inc(td_done.sem, 1)
                if following is not None:
                    front(following, k)
                pool.wait_ge(sz_done.sem, sz_done.done(i))
                pool.wait_ge(t2_done.sem, t2_done.done(i))
                pool.tensor_tensor(yv[:, :], t2[:, :], sz[:, k, :], ALU.mult).then_inc(yv_done.sem, 1)
                if k + 1 < GC:
                    scale_x(g, k + 1)
                pool.wait_ge(rs_in.sem, rs_in.done(i))
                pool.tensor_tensor(rs[:, :], vr[:, :], c["neghalf"][:, 0:1], ALU.pow).then_inc(rs_done.sem, 1)

            def convolve(g, before):
                for m, b in enumerate(ORDER):
                    B = g.block(m)
                    if m == 0:
                        continue
                    if m in BY_ACT:
                        pool.wait_ge(tap_act.sem, tap_act.done(g.group * len(BY_ACT) + BY_ACT.index(m)))
                        pool.tensor_tensor(acc[:, g.q, b, :], acc[:, g.q, b, :], tap[:, g.tbuf(m), :], ALU.add).then_inc(tap1.sem, 1)
                        continue
                    pool.wait_ge(tap1.sem, added(g, m - 2))
                    pool.wait_ge(raw_done.sem, raw_done.done(B))
                    pool.tensor_tensor(tap[:, g.tbuf(m), :], raw[:, b, 1:1 + GT], cwh[:, b, 1:2].to_broadcast([P, GT]), ALU.mult).then_inc(tap_made.sem, 1)
                    pool.wait_ge(tap_made.sem, tap_made.done(g.group * (NB - 1 - len(BY_ACT)) + (m - 1 - sum(n < m for n in BY_ACT))))
                    pool.wait_ge(tap0.sem, tap0.done(B))
                    pool.tensor_tensor(acc[:, g.q, b, :], acc[:, g.q, b, :], tap[:, g.tbuf(m), :], ALU.add).then_inc(tap1.sem, 1)
                pool.wait_ge(exps.sem, exps.done(g.group))
                decay_state(g, 0)
                pool.wait_ge(decdt.sem, decdt.done(g.group))
                scale_x(g, 0)

            run(pool, front, convolve, slot, lambda g: None)

        @block.scalar
        def _(act):
            for s in (xT_hi, tz_done, exp_u, exps, dec_out, raw_done, tap0, tap_act, tb_done, xt_done, bt_done, ex0_done, ex_done, sq_done, yT_hi):
                s.open(act)
            act.wait_ge(d_prep, 1)
            for n in range(KD):
                act.activation(wih[:, n, :], wst[:, n, :], ACT.Copy).then_inc(a_prep, 1)
            act.wait_ge(d_prep, 2)
            act.activation(heads[:, 1, :], heads[:, 1, :], ACT.Exp)
            act.activation(woh[:, :, :], wost[:, :, :], ACT.Copy).then_inc(a_prep, 1)

            def turn_x(g, k):
                act.wait_ge(xT_ready.sem, xT_ready.done(g.chunk(k)))
                act.activation(xTh[:, :, k * P:(k + 1) * P], by_head(pXN, KD), ACT.Copy).then_inc(xT_hi.sem, 1)

            def tanh_z(g, k):
                act.wait_ge(z_ready.sem, z_ready.done(g.chunk(k)))
                act.activation(tz[:, :], pZ[:, :], ACT.Tanh).then_inc(tz_done.sem, 1)

            def front(g, k):
                turn_x(g, k)
                if k + 1 < GC:
                    tanh_z(g, k)

            def first_tap(g, m):
                B, b = g.block(m), ORDER[m]
                act.wait_ge(p_ready.sem, p_ready.done(B))
                act.activation(raw[:, b, CONV - 1:], pP[m % 2][:, :], ACT.Copy).then_inc(raw_done.sem, 1)
                act.wait_ge(raw_done.sem, raw_done.done(B))
                act.activation(acc[:, g.q, b, :], raw[:, b, 0:GT], ACT.Identity, bias=cbh[:, b:b + 1], scale=cwh[:, b, 0:1]).then_inc(tap0.sem, 1)
                if m in BY_ACT:
                    act.wait_ge(tap1.sem, added(g, m - 2))
                    act.activation(tap[:, g.tbuf(m), :], raw[:, b, 1:1 + GT], ACT.Copy, scale=cwh[:, b, 1:2]).then_inc(tap_act.sem, 1)

            def tanh(g, m):
                B = g.block(m)
                act.wait_ge(taps.sem, taps.done(B))
                act.wait_ge(xc_done.sem, xc_done.done(B - 2))
                act.activation(tb[:, g.tbuf(m), :], acc[:, g.q, ORDER[m], :], ACT.Tanh).then_inc(tb_done.sem, 1)

            def copy_b(g, k):
                i = g.chunk(k)
                act.wait_ge(sm_ready.sem, sm_ready.done(i))
                act.activation(Bt[:, :], pBt, ACT.Copy).then_inc(bt_done.sem, 1)

            def copy_x(g, k):
                i = g.chunk(k)
                act.wait_ge(turned.sem, turned.done(i))
                act.activation(xt[:, :], pX[:, :], ACT.Copy).then_inc(xt_done.sem, 1)

            def decay(g, k, half):
                i = g.chunk(k)
                ready, done = ((e0_ready, ex0_done), (e1_ready, ex_done))[half]
                act.wait_ge(ready.sem, ready.done(i))
                for n in range(GC):
                    h = half * GC + n
                    at = k * H + h
                    last = act.activation(ex[:, h, :], pE[:, n * P:(n + 1) * P], ACT.Exp, bias=dts[:, g.q, NCUM, at:at + 1])
                last.then_inc(done.sem, 1)

            def convolve(g, before):
                G = g.group
                act.wait_ge(soft.sem, soft.done(G))
                act.activation(row(g, DU), row(g, DABS), ACT.Exp, scale=-1.0).then_inc(exp_u.sem, 1)
                tanh_z(g, GC - 1)
                act.wait_ge(halo.sem, halo.done(G - 1))
                first_tap(g, 0)
                act.wait_ge(cum_ready.sem, cum_ready.done(G))
                act.activation(row(g, ECUM), pCum, ACT.Exp)
                act.activation(row(g, ETOT), pTot, ACT.Exp).then_inc(exps.sem, 1)
                first_tap(g, 1)
                first_tap(g, 2)
                tanh(g, 0)
                act.wait_ge(dec_in.sem, dec_in.done(G))
                act.activation(row(g, DEC), row(g, DEC), ACT.Exp).then_inc(dec_out.sem, 1)
                first_tap(g, 3)
                tanh(g, 1)
                decay(g, 0, 0)
                first_tap(g, 4)
                tanh(g, 2)
                decay(g, 0, 1)
                tanh(g, 3)
                copy_b(g, 0)
                tanh(g, 4)
                copy_x(g, 0)

            def slot(g, k, following):
                i = g.chunk(k)
                if k + 1 < GC:
                    copy_b(g, k + 1)
                    copy_x(g, k + 1)
                    decay(g, k + 1, 0)
                if following is not None:
                    turn_x(following, k)
                act.wait_ge(yv_done.sem, yv_done.done(i))
                act.activation(td[:, :], yv[:, :], ACT.Square, accum_out=ss[:, :]).then_inc(sq_done.sem, 1)
                act.wait_ge(yT_ready.sem, yT_ready.done(i))
                act.activation(yTh[:, :, :], by_head(pYT[:, :], KI), ACT.Copy).then_inc(yT_hi.sem, 1)
                if k + 1 < GC:
                    decay(g, k + 1, 1)
                if following is not None and k + 1 < GC:
                    tanh_z(following, k)

            run(act, front, convolve, slot, lambda g: None)

        @block.tensor
        def _(pe):
            for s in (xT_ready, z_ready, dt_ready, cum_ready, p_ready, turned, sm_ready, e0_ready, e1_ready, i_ready, y_ready, s_ready, yT_ready, o_ready):
                s.open(pe)
            pe.wait_ge(consts, 3)
            pe.wait_ge(d_prep, 3)

            def product(out, parts):
                for m, (a, b) in enumerate(parts):
                    last = pe.matmul(out, a, b, start=(m == 0), stop=(m == len(parts) - 1))
                return last

            def turn_x(g, k):
                pe.wait_ge(norm_done.sem, norm_done.done(g.chunk(k)))
                for n in range(KD):
                    last = pe.transpose(pXN[:, n * P:(n + 1) * P], xn[:, n * P:(n + 1) * P], ident[:, :])
                last.then_inc(xT_ready.sem, 1)

            def project(g, k):
                i = g.chunk(k)
                pe.wait_ge(xT_lo.sem, xT_lo.done(i))
                tok = slice(k * P, (k + 1) * P)
                turns = ((xTh, wih), (xTh, wil), (xTl, wih))
                product(pDt, [(a[:, n, tok], w[:, n, NIN - H:NIN]) for a, w in turns for n in range(KD)]).then_inc(dt_ready.sem, 1)
                pe.wait_ge(sz_done.sem, sz_done.done(i - 1))
                product(pZ[:, :], [(a[:, n, tok], w[:, n, 0:DIN]) for a, w in turns for n in range(KD)]).then_inc(z_ready.sem, 1)

            def front(g, k):
                turn_x(g, k)
                project(g, k)

            def out_product(g, k):
                pe.wait_ge(yT_lo.sem, yT_lo.done(g.chunk(k)))
                product(pO[:, 0:D], [(a[:, n, :], w[:, n, :]) for a, w in ((yTh, woh), (yTh, wol), (yTl, woh)) for n in range(KI)]).then_inc(o_ready.sem, 1)

            def turn_b(g, k):
                tok = slice(k * P, (k + 1) * P)
                pe.matmul(pG, acc[0:NS, g.q, KI, tok], CT[:, g.q, tok], start=True, stop=True)
                pe.transpose(pBt, acc[0:NS, g.q, KI, tok], ident[0:NS, 0:NS]).then_inc(sm_ready.sem, 1)

            def turn_xc(g, k):
                for n in range(KI):
                    if k == 0:
                        pe.wait_ge(xc_done.sem, xc_done.done(g.block(n + 1)))
                    last = pe.transpose(pX[:, n * P:(n + 1) * P], acc[:, g.q, n, k * P:(k + 1) * P], ident[:, :])
                last.then_inc(turned.sem, 1)

            def sums(g, k, half):
                i = g.chunk(k)
                if half == 1:
                    pe.wait_ge(ex0_done.sem, ex0_done.done(i))
                for n in range(GC):
                    at = k * H + half * GC + n
                    for part in range(3):
                        pe.matmul(pE[:, n * P:(n + 1) * P], al[:, g.q, part, at:at + 1].to_broadcast([P, P]), tri_bf[:, :],
                                  start=(n == 0 and part == 0), stop=False, skip_group_check=True)
                pe.matmul(pE[:, :], ident_bf[:, :], future[:, :, :].rearrange("p h t -> p (h t)"),
                          start=False, stop=True, skip_group_check=True).then_inc((e0_ready, e1_ready)[half].sem, 1)

            def convolve(g, before):
                G, B0 = g.group, g.block(0)
                pe.wait_ge(dt_added.sem, dt_added.done(g.chunk(GC - 1)))
                if before is not None:
                    out_product(before, GC - 1)
                for m, b in enumerate(ORDER):
                    B = B0 + m
                    if m == 0:
                        pe.wait_ge(sz_done.sem, sz_done.done(g.chunk(GC - 1)))
                    elif m == 1:
                        if before is not None:
                            pe.wait_ge(xo_done.sem, xo_done.done(before.chunk(GC - 1)))
                    else:
                        pe.wait_ge(raw_done.sem, raw_done.done(B - 2))
                    ch = slice(DIN + b * P, DIN + (b + 1) * P)
                    parts = [(w[:, n, ch], a[:, n, :]) for w, a in ((wih, xTh), (wih, xTl), (wil, xTh)) for n in range(KD)]
                    product(pP[m % 2][:, :], parts).then_inc(p_ready.sem, 1)
                    if m == 0:
                        pe.wait_ge(a_done.sem, a_done.done(G))
                        pe.matmul(pCum, tri[:, :], row(g, DA), start=True, stop=True)
                        pe.matmul(pTot, c["ones_f"][:, :], row(g, DA), start=True, stop=True).then_inc(cum_ready.sem, 1)
                    if m == 1:
                        pe.wait_ge(al_done.sem, al_done.done(G))
                        sums(g, 0, 0)
                    if m == 4:
                        sums(g, 0, 1)
                pe.wait_ge(dec_in.sem, dec_in.done(G))
                pe.wait_ge(xc_done.sem, xc_done.done(B0))
                turn_b(g, 0)
                turn_xc(g, 0)

            def slot(g, k, following):
                i = g.chunk(k)
                tok = slice(k * P, (k + 1) * P)
                pe.wait_ge(S_done.sem, S_done.done(i - 1))
                pe.matmul(pS[:, :], CT[:, g.q, tok], S[:, :], start=True, stop=True).then_inc(i_ready.sem, 1)
                if k > 0:
                    if following is not None:
                        pe.wait_ge(dt_added.sem, dt_added.done(following.chunk(k - 1)))
                    out_product(g, k - 1)
                pe.wait_ge(xdt_done.sem, xdt_done.done(i))
                pe.wait_ge(M_done.sem, M_done.done(i))
                for h in range(H):
                    last = pe.matmul(pY[:, h * HD:(h + 1) * HD], M[:, h, :], xdt[:, h * HD:(h + 1) * HD], start=True, stop=True)
                last.then_inc(y_ready.sem, 1)
                pe.wait_ge(xw_done.sem, xw_done.done(i))
                pe.wait_ge(t1_done.sem, t1_done.done(i))
                pe.matmul(pS[0:NS, :], Bt[:, :], xw[:, :], start=True, stop=True).then_inc(s_ready.sem, 1)
                if k + 1 < GC:
                    turn_b(g, k + 1)
                    turn_xc(g, k + 1)
                    sums(g, k + 1, 0)
                if following is not None:
                    turn_x(following, k)
                pe.wait_ge(yv_done.sem, yv_done.done(i))
                for n in range(KI):
                    last = pe.transpose(pYT[:, n * P:(n + 1) * P], yv[:, n * P:(n + 1) * P], ident[:, :])
                last.then_inc(yT_ready.sem, 1)
                if k + 1 < GC:
                    sums(g, k + 1, 1)
                if following is not None:
                    project(following, k)

            run(pe, front, convolve, slot, lambda g: out_product(g, GC - 1))

        @block.vector
        def _(dve):
            for s in (add1, add2, stats, aggr, var_done, norm_done, xT_lo, sz_done, dt_added, soft, a_done, al_done, tap_own, cum_copied, decdt, dec_in, halo, tap_chain, s_sum,
                      taps, xc_done, M_done, S_done, t1_done, t2_done, rs_in, yT_lo, xo_done):
                s.open(dve)
            link = Chain(dve, prep).link
            dve.wait_ge(in_loaded, 16)
            link(dve.tensor_scalar(wst[:, :, 0:DIN], wst[:, :, 0:DIN], 0.5, None, ALU.mult))
            dve.sem_inc(d_prep, 1)
            dve.wait_ge(loads, 7 * 16)
            dve.wait_ge(consts, 3)
            for n in range(KI):
                link(dve.tensor_scalar(wost[:, n, :], wost[:, n, :], nw[:, n:n + 1], None, ALU.mult))
            dve.sem_inc(d_prep, 1)
            for n in range(KD):
                dve.wait_ge(a_prep, n + 1)
                link(dve.tensor_tensor(wil[:, n, :], wst[:, n, :], wih[:, n, :].bitcast(F32), ALU.subtract))
            dve.sem_inc(d_prep, 1)

            def prepare():
                link(dve.tensor_scalar(cwh[:, :, :], cw[:, :, :], 0.5, None, ALU.mult))
                link(dve.tensor_scalar(cbh[:, :], cb[:, :], 0.5, None, ALU.mult))
                link(dve.tensor_copy(tri_bf[:, :], tri[:, :]))
                dve.wait_ge(a_prep, KD + 1)
                for k in range(GC):
                    link(dve.tensor_scalar(negA[:, k, :], heads[:, 1, :], -1.0, None, ALU.mult))
                link(dve.tensor_tensor(wol[:, :, :], wost[:, :, :], woh[:, :, :].bitcast(F32), ALU.subtract))

            def moments(g, k):
                i, n, u = g.chunk(k), g.q * GC + k, k % 2
                dve.wait_ge(x_loaded[n].sem, x_loaded[n].done(g.j))
                dve.wait_ge(y_loaded[u].sem, y_loaded[u].done(g.nth(k)))
                dve.scalar_tensor_tensor(xr[:, n, :], yg[:, u, 0, :], gates[:, bass.ds(i, 1)], xr[:, n, :], ALU.mult, ALU.add).then_inc(add1.sem, 1)
                dve.wait_ge(add1.sem, add1.done(i))
                dve.scalar_tensor_tensor(xr[:, n, :], yg[:, u, 1, :], gates[:, bass.ds(i + T, 1)], xr[:, n, :], ALU.mult, ALU.add).then_inc(add2.sem, 1)
                dve.wait_ge(add2.sem, add2.done(i))
                dve.bn_stats(st[:, :], xr[:, n, :]).then_inc(stats.sem, 1)
                dve.wait_ge(stats.sem, stats.done(i))
                dve.sem_inc(go, 1)
                dve.bn_aggr(mv[:, :], st[:, :]).then_inc(aggr.sem, 1)
                dve.wait_ge(aggr.sem, aggr.done(i))
                dve.tensor_scalar(ve[:, :], mv[:, 1:2], EPS, None, ALU.add).then_inc(var_done.sem, 1)

            def normalise(g, k):
                i, n = g.chunk(k), g.q * GC + k
                dve.wait_ge(pow_done.sem, pow_done.done(i))
                dve.tensor_scalar(xn[:, :], xr[:, n, :], mv[:, 0:1], rstd[:, 0:1], ALU.subtract, ALU.mult).then_inc(norm_done.sem, 1)

            def gate(g, k):
                i = g.chunk(k)
                dve.wait_ge(tz_done.sem, tz_done.done(i))
                dve.scalar_tensor_tensor(sz[:, k, :], tz[:, :], 1.0, pZ[:, :], ALU.add, ALU.mult).then_inc(sz_done.sem, 1)

            def split_x(g, k):
                i = g.chunk(k)
                dve.wait_ge(xT_hi.sem, xT_hi.done(i))
                dve.tensor_tensor(xTl[:, :, k * P:(k + 1) * P], by_head(pXN, KD), xTh[:, :, k * P:(k + 1) * P].bitcast(F32), ALU.subtract).then_inc(xT_lo.sem, 1)

            def add_bias(g, k):
                i = g.chunk(k)
                dve.wait_ge(dt_ready.sem, dt_ready.done(i))
                dve.tensor_tensor(row(g, DTR, k, 1), pDt, heads[:, 0, :], ALU.add).then_inc(dt_added.sem, 1)

            def front(g, k):
                if k == 0:
                    moments(g, 0)
                normalise(g, k)
                if k > 0:
                    gate(g, k - 1)
                split_x(g, k)
                if k == 0:
                    prepare()
                if k + 1 < GC:
                    moments(g, k + 1)
                add_bias(g, k)

            NCH = 1 + 5 + (len(ATANH) - 1) + 2 + 4

            def softplus(g):
                G, m = g.group, [0]

                def linked(ins):
                    m[0] += 1
                    ins.then_inc(soft_chain, 1)
                    dve.wait_ge(soft_chain, G * NCH + m[0])

                dve.wait_ge(dt_added.sem, dt_added.done(g.chunk(GC - 1)))
                linked(dve.tensor_scalar(row(g, DPOS), row(g, DTR), 0.0, None, ALU.max))
                dve.scalar_tensor_tensor(row(g, DABS), row(g, DPOS), 2.0, row(g, DTR), ALU.mult, ALU.subtract).then_inc(soft.sem, 1)
                dve.wait_ge(exp_u.sem, exp_u.done(G))
                linked(dve.tensor_scalar(row(g, DS2), row(g, DU), 2.0, None, ALU.add))
                linked(dve.reciprocal(row(g, DQ), row(g, DS2)))
                linked(dve.tensor_tensor(row(g, DS), row(g, DU), row(g, DQ), ALU.mult))
                linked(dve.tensor_tensor(row(g, DS2), row(g, DS), row(g, DS), ALU.mult))
                linked(dve.tensor_scalar(row(g, DQ), row(g, DS2), ATANH[0], None, ALU.mult))
                for a in ATANH[1:]:
                    linked(dve.scalar_tensor_tensor(row(g, DQ), row(g, DQ), a, row(g, DS2), ALU.add, ALU.mult))
                gate(g, GC - 1)
                linked(dve.scalar_tensor_tensor(row(g, DQ), row(g, DQ), 1.0, row(g, DS), ALU.add, ALU.mult))
                linked(dve.scalar_tensor_tensor(row(g, DT), row(g, DQ), 2.0, row(g, DPOS), ALU.mult, ALU.add))
                dve.tensor_tensor(row(g, DA), row(g, DT), negA[:, :, :].rearrange("p k h -> p (k h)"), ALU.mult).then_inc(a_done.sem, 1)
                dve.wait_ge(a_done.sem, a_done.done(G))
                linked(dve.tensor_copy(al[:, g.q, 0, :], row(g, DA)))
                linked(dve.tensor_tensor(row(g, DS), row(g, DA), al[:, g.q, 0, :], ALU.subtract))
                linked(dve.tensor_copy(al[:, g.q, 1, :], row(g, DS)))
                linked(dve.tensor_tensor(row(g, DS2), row(g, DS), al[:, g.q, 1, :], ALU.subtract))
                dve.tensor_copy(al[:, g.q, 2, :], row(g, DS2)).then_inc(al_done.sem, 1)
                assert m[0] == NCH

            def silu(g, m):
                a, t = acc[:, g.q, ORDER[m], :], tb[:, g.tbuf(m), :]
                dve.wait_ge(tb_done.sem, tb_done.done(g.block(m)))
                if ORDER[m] < KI:
                    dve.scalar_tensor_tensor(a, t, 1.0, a, ALU.add, ALU.mult).then_inc(xc_done.sem, 1)
                else:
                    dve.scalar_tensor_tensor(CT[:, g.q, :], t[NS:P, :], 1.0, a[NS:P, :], ALU.add, ALU.mult)
                    dve.scalar_tensor_tensor(a[0:NS, :], t[0:NS, :], 1.0, a[0:NS, :], ALU.add, ALU.mult).then_inc(xc_done.sem, 1)

            def convolve(g, before):
                G, B0 = g.group, g.block(0)
                softplus(g)
                if before is not None:
                    add_residual(before, GC - 1)
                dve.wait_ge(exps.sem, exps.done(G))
                dve.tensor_scalar(row(g, NCUM), pCum, -1.0, None, ALU.mult).then_inc(cum_copied.sem, 1)
                dve.wait_ge(cum_copied.sem, cum_copied.done(G))
                dve.tensor_tensor(row(g, DEC), pTot, row(g, NCUM), ALU.add).then_inc(dec_in.sem, 1)
                for m, b in enumerate(ORDER):
                    B, a = B0 + m, acc[:, g.q, b, :]
                    if m == 0:
                        dve.wait_ge(tap0.sem, tap0.done(B))
                        dve.scalar_tensor_tensor(a, raw[:, b, 1:1 + GT], cwh[:, b, 1:2], a, ALU.mult, ALU.add).then_inc(tap_own.sem, 1)
                        dve.wait_ge(tap_own.sem, tap_own.done(G))
                    else:
                        dve.wait_ge(tap1.sem, added(g, m))
                    dve.scalar_tensor_tensor(a, raw[:, b, 2:2 + GT], cwh[:, b, 2:3], a, ALU.mult, ALU.add).then_inc(tap_chain.sem, 1)
                    if m > 0:
                        silu(g, m - 1)
                    dve.wait_ge(tap_chain.sem, tap_chain.done(B))
                    dve.scalar_tensor_tensor(a, raw[:, b, 3:3 + GT], cwh[:, b, 3:4], a, ALU.mult, ALU.add).then_inc(taps.sem, 1)
                    if m == 2:
                        dve.wait_ge(dec_out.sem, dec_out.done(G))
                        dve.tensor_tensor(row(g, DECDT), row(g, DEC), row(g, DT), ALU.mult).then_inc(decdt.sem, 1)
                dve.wait_ge(taps.sem, taps.done(B0 + (NB - 1)))
                dve.tensor_scalar(raw[:, :, 0:CONV - 1], raw[:, :, GT:GT + CONV - 1], flags[:, bass.ds(G + 1, 1)], None, ALU.mult).then_inc(halo.sem, 1)
                silu(g, NB - 1)

            def add_residual(g, k):
                i, n = g.chunk(k), g.q * GC + k
                dve.wait_ge(o_ready.sem, o_ready.done(i))
                dve.wait_ge(rs_done.sem, rs_done.done(i))
                dve.wait_ge(o_stored[k % 2].sem, o_stored[k % 2].done(g.nth(k) - 1))
                dve.scalar_tensor_tensor(xo[:, k % 2, :], pO[:, 0:D], rs[:, 0:1], xr[:, n, :], ALU.mult, ALU.add).then_inc(xo_done.sem, 1)

            def slot(g, k, following):
                i, G = g.chunk(k), g.group
                if k == 0:
                    dve.wait_ge(bt_done.sem, bt_done.done(i))
                dve.wait_ge(ex_done.sem, ex_done.done(i))
                dve.tensor_tensor(M[:, :, :], ex[:, :, :], pG.rearrange("p (a t) -> p a t", a=1).to_broadcast([P, H, P]), ALU.mult).then_inc(M_done.sem, 1)
                dve.wait_ge(i_ready.sem, i_ready.done(i))
                dve.tensor_tensor(by_head(t1[:, :]), by_head(pS[:, :]), per_head(row(g, ECUM, k, 1), HD), ALU.mult).then_inc(t1_done.sem, 1)
                if k > 0:
                    add_residual(g, k - 1)
                if following is not None:
                    moments(following, k)
                dve.wait_ge(td_done.sem, td_done.done(i))
                dve.wait_ge(y_ready.sem, y_ready.done(i))
                dve.tensor_tensor(t2[:, :], td[:, :], pY[:, :], ALU.add).then_inc(t2_done.sem, 1)
                dve.wait_ge(s1_done.sem, s1_done.done(i))
                dve.wait_ge(s_ready.sem, s_ready.done(i))
                if k == GC - 1:
                    dve.tensor_tensor(S[:, :], S1[:, :], pS[0:NS, :], ALU.add).then_inc(s_sum.sem, 1)
                    dve.wait_ge(s_sum.sem, s_sum.done(G))
                    dve.tensor_scalar(S[:, :], S[:, :], flags[0:NS, bass.ds(G + 1, 1)], None, ALU.mult).then_inc(S_done.sem, 1)
                else:
                    dve.tensor_tensor(S[:, :], S1[:, :], pS[0:NS, :], ALU.add).then_inc(S_done.sem, 1)
                if following is not None:
                    normalise(following, k)
                    if k > 0:
                        gate(following, k - 1)
                    split_x(following, k)
                dve.wait_ge(yT_hi.sem, yT_hi.done(i))
                dve.tensor_tensor(yTl[:, :, :], by_head(pYT[:, :], KI), yTh[:, :, :].bitcast(F32), ALU.subtract).then_inc(yT_lo.sem, 1)
                dve.wait_ge(sq_done.sem, sq_done.done(i))
                dve.tensor_scalar(vr[:, :], ss[:, :], 1.0 / DIN, EPS, ALU.mult, ALU.add).then_inc(rs_in.sem, 1)
                if following is not None:
                    add_bias(following, k)

            run(dve, front, convolve, slot, lambda g: add_residual(g, GC - 1))


def program(nc, x, w_in, conv_w, conv_b, dt_bias, a_log, d_skip, norm_w, w_out, router_w, w1, w2, out):
    with ExitStack() as ctx:
        batches, tokens = x.shape[0], x.shape[0] * x.shape[1]
        xf, of = x.rearrange("b t d -> (b t) d"), out.rearrange("b t d -> (b t) d")

        xn_d = nc.dram_tensor("xn_d", (tokens, D), F32, kind="Internal").ap()
        ys_d = nc.dram_tensor("ys_d", ((TOP * (tokens // P) + 2) * P, D), F32, kind="Internal").ap()
        x2_d = nc.dram_tensor("x2_d", (tokens, D), F32, kind="Internal").ap()
        lo_d = nc.dram_tensor("lo_d", (2, P, E * WCOLS), F32, kind="Internal").ap()
        c = make_constants(nc, ctx)
        keep = make_keep(nc, ctx, tokens)
        build_constants(nc, c)
        ffn_block(nc, c, keep, xf, router_w, w1, w2, xn_d, ys_d, lo_d, None, True)
        mamba_block(nc, c, keep, xf, ys_d, w_in, conv_w, conv_b, dt_bias, a_log, d_skip, norm_w, w_out, x2_d, batches)
        ffn_block(nc, c, keep, x2_d, router_w, w1, w2, xn_d, ys_d, lo_d, of, False)


_INS = ["L0_attn_x", "L0_attn_W_in", "L0_attn_conv_w", "L0_attn_conv_b", "L0_attn_dt_bias", "L0_attn_A_log", "L0_attn_D",
        "L0_attn_norm_weight", "L0_attn_W_out", "L0_ffn_router_w", "L0_ffn_w1", "L0_ffn_w2"]


def kernel(**inputs):
    import numpy as _np
    import concourse.bacc as _bacc
    from concourse import mybir as _mybir
    from concourse.bass_utils import run_bass_kernel_spmd as _run

    nc = _bacc.Bacc("TRN2", target_bir_lowering=False, num_devices=1)
    arrays, args = {}, []
    for name in _INS:
        a = _np.ascontiguousarray(inputs[name])
        arrays[f"in_{name}_dram"] = a
        args.append(nc.dram_tensor(f"in_{name}_dram", a.shape, _mybir.dt.from_np(a.dtype), kind="ExternalInput").ap())
    shape = inputs["L0_attn_x"].shape
    args.append(nc.dram_tensor("out_0_dram", shape, _mybir.dt.float32, kind="ExternalOutput").ap())
    program(nc, *args)
    r = _run(nc, [arrays], core_ids=[0])
    return r.results[0]["out_0_dram"]
```
